# Optimizing a Trainium2 kernel written in Bass

```python
import numpy as np
import jax
import jax.numpy as jnp

def _softmax(x, axis=-1):
    return jax.nn.softmax(x, axis=axis)

def _gelu(x):
    return jax.nn.gelu(x, approximate=True)

def _silu(x):
    return jax.nn.silu(x)

def _sigmoid(x):
    return jax.nn.sigmoid(x)

def _layernorm(x, axis=-1, eps=1e-05):
    m = jnp.mean(x, axis=axis, keepdims=True)
    v = jnp.var(x, axis=axis, keepdims=True)
    return (x - m) / jnp.sqrt(v + eps)

def _scatter_add(tgt, idx, src, axis=0):
    return tgt.at[idx].add(src)

def _segment_sum(src, seg, n):
    return jax.ops.segment_sum(src, seg, n)
kernel_name = 'mk_lm_tower_d1_tok_ids2048_r4_ed7b90'

def setup_inputs(seed: int=0):
    np.random.seed(seed)
    _w = jnp.asarray

    def _rec_inputs():
        import jax
        import jax.numpy as jnp
        _rk = jax.random.key(seed)
        x = jax.random.randint(jax.random.fold_in(_rk, 1), (2, 1024), 0, 12500, jnp.int32)
        return x
    x = _rec_inputs()

    def _L0_tok_setup():
        import jax, jax.numpy as jnp
        import numpy as np
        import math
        VOCAB = 12500
        EMB_DIM = 75
        D_MODEL = 512
        BATCH = 4
        SEQ = 2048
        key = jax.random.key(seed)
        k1, k2, k3, k4 = jax.random.split(key, 4)
        x = jax.random.randint(k1, (BATCH, SEQ), 0, VOCAB, dtype=jnp.int64 if jax.config.jax_enable_x64 else jnp.int32)
        emb = jax.random.normal(k2, (VOCAB, EMB_DIM), dtype=jnp.float32)
        W = jax.random.normal(k3, (EMB_DIM, D_MODEL), dtype=jnp.float32) * (1.0 / math.sqrt(EMB_DIM))
        b = jax.random.normal(k4, (D_MODEL,), dtype=jnp.float32) * 0.01
        return {'x': x, 'emb': emb, 'W': W, 'b': b}
    _L0_tok_all = _L0_tok_setup()
    _L0_tok_in = {k: v for k, v in _L0_tok_all.items() if k in ('emb', 'W', 'b')}
    del _L0_tok_all

    def _L0_attn_setup():
        import jax, jax.numpy as jnp
        import numpy as np
        N_HEADS = 16
        D_ROPE = 32
        ROPE_BASE = 10000.0
        MASK_FILL = -10000.0

        def _rope(x):
            S = x.shape[1]
            theta = 1.0 / ROPE_BASE ** (jnp.arange(0, D_ROPE, 2, dtype=jnp.float32) / D_ROPE)
            idx_theta = jnp.arange(S, dtype=jnp.float32)[:, None] * theta[None, :]
            idx_theta2 = jnp.concatenate([idx_theta, idx_theta], axis=-1)
            cos = jnp.cos(idx_theta2)[:, None, :].astype(x.dtype)
            sin = jnp.sin(idx_theta2)[:, None, :].astype(x.dtype)
            x_rope, x_pass = (x[..., :D_ROPE], x[..., D_ROPE:])
            half = D_ROPE // 2
            rot = jnp.concatenate([-x_rope[..., half:], x_rope[..., :half]], axis=-1)
            x_rope = x_rope * cos + rot * sin
            return jnp.concatenate([x_rope, x_pass], axis=-1)
        key = jax.random.key(seed)
        k1, k2, k3, k4, k5 = jax.random.split(key, 5)
        B, S, D = (2, 512, 512)
        sc = 0.02
        return {'x': jax.random.normal(k1, (B, S, D), jnp.float32), 'W_qkv': jax.random.normal(k2, (3 * D, D), jnp.float32) * sc, 'b_qkv': jax.random.normal(k3, (3 * D,), jnp.float32) * sc, 'W_out': jax.random.normal(k4, (D, D), jnp.float32) * sc, 'b_out': jax.random.normal(k5, (D,), jnp.float32) * sc}
    _L0_attn_all = _L0_attn_setup()
    _L0_attn_in = {k: v for k, v in _L0_attn_all.items() if k in ('W_qkv', 'b_qkv', 'W_out', 'b_out')}
    del _L0_attn_all

    def _L0_ffn_setup():
        import jax, jax.numpy as jnp
        import numpy as np
        NUM_ROUTED = 7
        TOP_K = 3
        D = 512
        H = 512
        B, S = (4, 512)

        def _expert_ffn(x, w1, wg, w2):
            return jax.nn.silu(x @ w1) * (x @ wg) @ w2
        key = jax.random.key(seed)
        ks = jax.random.split(key, 8)
        s = 0.02
        return {'x': jax.random.normal(ks[0], (B, S, D), jnp.float32), 'W1': jax.random.normal(ks[1], (NUM_ROUTED, D, H), jnp.float32) * s, 'Wg': jax.random.normal(ks[2], (NUM_ROUTED, D, H), jnp.float32) * s, 'W2': jax.random.normal(ks[3], (NUM_ROUTED, H, D), jnp.float32) * s, 'Ws1': jax.random.normal(ks[4], (D, H), jnp.float32) * s, 'Wsg': jax.random.normal(ks[5], (D, H), jnp.float32) * s, 'Ws2': jax.random.normal(ks[6], (H, D), jnp.float32) * s, 'gate_w': jax.random.normal(ks[7], (D, NUM_ROUTED), jnp.float32) * s, 'gate_b': jnp.zeros((NUM_ROUTED,), jnp.float32), 'biases': jnp.zeros((NUM_ROUTED,), jnp.float32)}
    _L0_ffn_all = _L0_ffn_setup()
    _L0_ffn_in = {k: v for k, v in _L0_ffn_all.items() if k in ('W1', 'Wg', 'W2', 'Ws1', 'Wsg', 'Ws2', 'gate_w', 'gate_b', 'biases')}
    del _L0_ffn_all
    return {'x': x, 'L0_tok_emb': _L0_tok_in['emb'], 'L0_tok_W': _L0_tok_in['W'], 'L0_tok_b': _L0_tok_in['b'], 'L0_attn_W_qkv': _L0_attn_in['W_qkv'], 'L0_attn_b_qkv': _L0_attn_in['b_qkv'], 'L0_attn_W_out': _L0_attn_in['W_out'], 'L0_attn_b_out': _L0_attn_in['b_out'], 'L0_ffn_W1': _L0_ffn_in['W1'], 'L0_ffn_Wg': _L0_ffn_in['Wg'], 'L0_ffn_W2': _L0_ffn_in['W2'], 'L0_ffn_Ws1': _L0_ffn_in['Ws1'], 'L0_ffn_Wsg': _L0_ffn_in['Wsg'], 'L0_ffn_Ws2': _L0_ffn_in['Ws2'], 'L0_ffn_gate_w': _L0_ffn_in['gate_w'], 'L0_ffn_gate_b': _L0_ffn_in['gate_b'], 'L0_ffn_biases': _L0_ffn_in['biases']}

def reference(x, L0_tok_emb, L0_tok_W, L0_tok_b, L0_attn_W_qkv, L0_attn_b_qkv, L0_attn_W_out, L0_attn_b_out, L0_ffn_W1, L0_ffn_Wg, L0_ffn_W2, L0_ffn_Ws1, L0_ffn_Wsg, L0_ffn_Ws2, L0_ffn_gate_w, L0_ffn_gate_b, L0_ffn_biases):
    import jax
    import jax.numpy as jnp

    def _L0_tok_ref(x, emb, W, b):
        import jax, jax.numpy as jnp
        import numpy as np
        import math
        VOCAB = 12500
        EMB_DIM = 75
        D_MODEL = 512
        BATCH = 4
        SEQ = 2048
        vecs = emb[x]
        out = jnp.einsum('bse,ed->bsd', vecs, W) + b
        return out * jnp.sqrt(jnp.asarray(W.shape[1], dtype=out.dtype))

    def _L0_attn_ref(x, W_qkv, b_qkv, W_out, b_out):
        import jax, jax.numpy as jnp
        import numpy as np
        N_HEADS = 16
        D_ROPE = 32
        ROPE_BASE = 10000.0
        MASK_FILL = -10000.0

        def _rope(x):
            S = x.shape[1]
            theta = 1.0 / ROPE_BASE ** (jnp.arange(0, D_ROPE, 2, dtype=jnp.float32) / D_ROPE)
            idx_theta = jnp.arange(S, dtype=jnp.float32)[:, None] * theta[None, :]
            idx_theta2 = jnp.concatenate([idx_theta, idx_theta], axis=-1)
            cos = jnp.cos(idx_theta2)[:, None, :].astype(x.dtype)
            sin = jnp.sin(idx_theta2)[:, None, :].astype(x.dtype)
            x_rope, x_pass = (x[..., :D_ROPE], x[..., D_ROPE:])
            half = D_ROPE // 2
            rot = jnp.concatenate([-x_rope[..., half:], x_rope[..., :half]], axis=-1)
            x_rope = x_rope * cos + rot * sin
            return jnp.concatenate([x_rope, x_pass], axis=-1)
        B, S, D = x.shape
        d_k = D // N_HEADS
        scale = 1.0 / jnp.sqrt(jnp.asarray(d_k, x.dtype))
        qkv = x @ W_qkv.T + b_qkv
        qkv = qkv.reshape(B, S, N_HEADS, 3 * d_k)
        q, k, v = jnp.split(qkv, 3, axis=-1)
        q = _rope(q)
        k = _rope(k)
        attn = jnp.einsum('bihk,bjhk->bijh', q, k) * scale
        causal = jnp.triu(jnp.ones((S, S), dtype=bool), 1)
        attn = jnp.where(causal[None, :, :, None], MASK_FILL, attn)
        attn = jax.nn.softmax(attn, axis=2)
        out = jnp.einsum('bijh,bjhk->bihk', attn, v)
        out = out.reshape(B, S, D)
        return out @ W_out.T + b_out

    def _L0_ffn_ref(x, W1, Wg, W2, Ws1, Wsg, Ws2, gate_w, gate_b, biases):
        import jax, jax.numpy as jnp
        import numpy as np
        NUM_ROUTED = 7
        TOP_K = 3
        D = 512
        H = 512
        B, S = (4, 512)

        def _expert_ffn(x, w1, wg, w2):
            return jax.nn.silu(x @ w1) * (x @ wg) @ w2
        output = _expert_ffn(x, Ws1, Wsg, Ws2)
        gate_logits = x @ gate_w + gate_b
        gate_probas = jax.nn.softmax(gate_logits, axis=-1)
        biased_probas = gate_probas + biases
        _, topk_idxs = jax.lax.top_k(biased_probas, TOP_K)
        topk_probas = jnp.take_along_axis(gate_probas, topk_idxs, axis=-1)
        topk_probas = topk_probas / jnp.sum(topk_probas, axis=-1, keepdims=True)
        for e in range(NUM_ROUTED):
            w_e = jnp.sum(topk_probas * (topk_idxs == e), axis=-1)
            output = output + _expert_ffn(x, W1[e], Wg[e], W2[e]) * w_e[..., None]
        return output
    h = _L0_tok_ref(x, L0_tok_emb, L0_tok_W, L0_tok_b)
    h = h + _L0_attn_ref(_layernorm(h, axis=-1), L0_attn_W_qkv, L0_attn_b_qkv, L0_attn_W_out, L0_attn_b_out)
    h = h + _L0_ffn_ref(_layernorm(h, axis=-1), L0_ffn_W1, L0_ffn_Wg, L0_ffn_W2, L0_ffn_Ws1, L0_ffn_Wsg, L0_ffn_Ws2, L0_ffn_gate_w, L0_ffn_gate_b, L0_ffn_biases)
    return h

_drawn_inputs = setup_inputs


def setup_inputs(seed=0):
    import zlib

    import numpy as np

    out = dict(_drawn_inputs(seed))
    spreads = {'L0_ffn_gate_b': (0.0, 0.8), 'L0_ffn_biases': (0.0, 0.8)}
    factors = {'L0_tok_b': 6.011,
     'L0_attn_W_qkv': 8.0,
     'L0_attn_b_qkv': 8.0,
     'L0_attn_W_out': 8.0,
     'L0_attn_b_out': 45.344,
     'L0_ffn_W1': 8.0,
     'L0_ffn_Wg': 8.0,
     'L0_ffn_W2': 8.0,
     'L0_ffn_Ws1': 8.0,
     'L0_ffn_Wsg': 8.0,
     'L0_ffn_Ws2': 8.0,
     'L0_ffn_gate_w': 8.0}
    for name, (base, spread) in spreads.items():
        noise = np.random.default_rng([zlib.crc32(name.encode()), seed]).standard_normal(out[name].shape)
        drawn = base * np.exp(spread * noise) if base else spread * noise
        out[name] = jnp.asarray(drawn.astype(out[name].dtype))
    for name, factor in factors.items():
        out[name] = (out[name] * factor).astype(out[name].dtype)
    return out
```

```python
from contextlib import ExitStack

import concourse.bass as bass
from concourse import mybir

ALU = mybir.AluOpType
ACT = mybir.ActivationFunctionType
AXX = mybir.AxisListType.X
F32 = mybir.dt.float32
F32R = mybir.dt.float32r
BF16 = mybir.dt.bfloat16
I32 = mybir.dt.int32

P = 128
BATCH, SEQ = 2, 1024
TOKENS = BATCH * SEQ
TILES = TOKENS // P
TPB = SEQ // P
D = 512
DC = D // P
EMB = 75
HEADS, DK = 16, 32
HPG = P // DK
GROUPS = HEADS // HPG
UNITS = BATCH * GROUPS
KS = 3 * DK
EXPERTS, TOPK = 7, 3
HID = 512
SLOTS = TOKENS * TOPK // P + EXPERTS - 1
LN_EPS = 1e-5
SCALE = float(DK) ** -0.5
NEG = -1.0e30
HF = DK // 2
QB = 512


class Chain:

    def __init__(self, eng, sem, per_iter, base):
        self.eng, self.sem, self.per_iter, self.base, self.n = eng, sem, per_iter, base, 0

    def inc(self, ins):
        self.n += 1
        return ins.then_inc(self.sem, 1)

    def wait(self):
        self.eng.wait_ge(self.sem, self.base * self.per_iter + self.n)

    def done(self):
        assert self.n == self.per_iter, (self.n, self.per_iter)


def split_load(nc, ctx, sb, sem, name, jobs):
    stage = sb(name + "_stage", [P, 2, 1536], F32)
    landed = sem(name + "_landed")
    high = sem(name + "_high")
    low = sem(name + "_low")
    n = len(jobs)

    def st(i):
        rows, cols = jobs[i][1].shape
        return stage[0:rows, i % 2, 0:cols]

    with nc.Block() as block:
        @block.sync
        def _(sp):
            for i, (src, hi, lo) in enumerate(jobs):
                if i >= 2:
                    sp.wait_ge(low, i - 1)
                sp.dma_start(st(i), src).then_inc(landed, 16)
                sp.wait_ge(landed, 16 * (i + 1))

        @block.scalar
        def _(act):
            for i, (src, hi, lo) in enumerate(jobs):
                act.wait_ge(landed, 16 * (i + 1))
                act.activation(hi, st(i), ACT.Copy).then_inc(high, 1)

        @block.vector
        def _(dve):
            for i, (src, hi, lo) in enumerate(jobs):
                dve.wait_ge(high, i + 1)
                dve.tensor_tensor(lo, st(i), hi.bitcast(F32), ALU.subtract).then_inc(low, 1)


def products(pe, out, terms):
    last = None
    for i, (l, r) in enumerate(terms):
        last = pe.matmul(out, l, r, start=(i == 0), stop=(i == len(terms) - 1))
    return last


def phase_a(nc, t, keep):
    qk, v_all, ident, cs = keep["qk"], keep["v"], keep["ident"], keep["cs"]
    with ExitStack() as ctx:
        sb = lambda n, s, d: ctx.enter_context(nc.sbuf_tensor("a_" + n, s, d))
        sem = lambda n: ctx.enter_context(nc.semaphore("a_" + n))
        ps = [ctx.enter_context(nc.psum_tensor(f"a_ps{i}", [P, 512], F32)) for i in range(8)]
        wh = sb("wh", [P, DC, 3 * D], F32R)
        wl = sb("wl", [P, DC, 3 * D], F32R)
        th = sb("th", [EMB + 1, D], F32R)
        tl = sb("tl", [EMB + 1, D], F32R)
        with ExitStack() as c2:
            sb2 = lambda n, s, d: c2.enter_context(nc.sbuf_tensor("a_" + n, s, d))
            jobs = [(t["tok_w"], th[0:EMB + 1, :], tl[0:EMB + 1, :])]
            jobs += [(t["qkv_w"][c * P:(c + 1) * P, :], wh[:, c, :], wl[:, c, :]) for c in range(DC)]
            split_load(nc, c2, sb2, lambda n: c2.enter_context(nc.semaphore("a_" + n)), "w", jobs)
        ids = sb("ids", [P, TILES], I32)
        row_ids = sb("row_ids", [P, 2, 1], I32)
        bias = sb("bias", [P, 3 * D], F32)
        rows = sb("rows", [P, 2, EMB + 1], F32)
        rth = sb("rth", [EMB + 1, P], F32R)
        rtl = sb("rtl", [EMB + 1, P], F32R)
        h = sb("h", [P, 2, D], F32)
        stats = sb("stats", [P, 6], F32)
        mv = sb("mv", [P, 2], F32)
        eps = sb("eps", [P, 1], F32)
        rstd = sb("rstd", [P, 1], F32)
        nhalf = sb("nhalf", [P, 1], F32)
        xn = sb("xn", [P, D], F32)
        xh = sb("xh", [P, 2, D], F32R)
        xl = sb("xl", [P, 2, D], F32R)
        qb = sb("qb", [P, 2, D], F32)
        ra = sb("ra", [P, 2, D], F32)
        rb = sb("rb", [P, 2, D], F32)

        held = sem("held")
        const_in = sem("const_in")
        const_set = sem("const_set")
        ids_ok = sem("ids_ok")
        gathered = [sem(f"gathered{u}") for u in range(2)]
        rows_t = sem("rows_t")
        rth_ok = sem("rth_ok")
        rtl_ok = sem("rtl_ok")
        h_ps = sem("h_ps")
        h_ok = sem("h_ok")
        h_out = [sem(f"h_out{u}") for u in range(2)]
        var_ok = sem("var_ok")
        rstd_ok = sem("rstd_ok")
        xn_ok = sem("xn_ok")
        xt_ps = sem("xt_ps")
        xh_ok = sem("xh_ok")
        xl_ok = sem("xl_ok")
        proj = sem("proj")
        biased = sem("biased")
        v_ok = sem("v_ok")
        turned = sem("turned")
        roped = sem("roped")
        dch = sem("dch")
        PEEL = 4

        def steps(eng, body):
            with eng.Fori(0, (TILES - PEEL) // 2) as i:
                for u in range(2):
                    body(i * 2 + u, u, TILES)
            for n in range(TILES - PEEL, TILES):
                body(n, n % 2, TILES - n)

        def uses(n, u):
            return (n - u) // 2 + 1

        with nc.Block() as block:
            @block.sync
            def _(sp):
                sp.dma_start(ids[:, :], t["ids"]).then_inc(const_in, 16)
                sp.dma_start(bias[:, :], t["qkv_b"].partition_broadcast(P)).then_inc(const_in, 16)
                for u in range(2):
                    sp.nop().then_inc(h_out[u], 16)

                def store(n, u, left):
                    sp.wait_ge(h_ok, n + 1)
                    sp.dma_start(t["h0"][bass.ds(n * P, P), :], h[:, u, :]).then_inc(h_out[u], 16)
                steps(sp, store)
                for u in range(2):
                    sp.wait_ge(h_out[u], 8 * TILES + 16)

            @block.gpsimd
            def _(pool):
                def gather(n, u):
                    pool.tensor_copy(row_ids[:, u, :], ids[:, bass.ds(n, 1)]).then_inc(ids_ok, 1)
                    pool.wait_ge(ids_ok, n + 1)
                    pool.nop().then_inc(held, 1)
                    pool.indirect_dma_start(out=rows[:, u, 0:EMB], out_offset=None, in_=t["emb"],
                                            in_offset=bass.IndirectOffsetOnAxis(ap=row_ids[:, u, :], axis=0)
                                            ).then_inc(gathered[u], 16)

                def root(n):
                    pool.wait_ge(var_ok, n + 1)
                    pool.tensor_tensor(rstd[:, :], mv[:, 1:2], nhalf[:, :], ALU.pow).then_inc(rstd_ok, 1)

                pool.nop().then_inc(roped, 2)
                pool.memset(rows[:, :, :], 1.0).then_inc(const_set, 1)
                pool.memset(eps[:, :], LN_EPS).then_inc(const_set, 1)
                pool.memset(nhalf[:, :], -0.5).then_inc(const_set, 1)
                pool.wait_ge(const_set, 3)
                pool.wait_ge(const_in, 32)
                gather(0, 0)
                gather(1, 1)
                pool.wait_ge(rows_t, 1)
                gather(2, 0)
                root(0)

                def body(n, u, left):
                    if left > 3:
                        pool.wait_ge(rows_t, n + 2)
                        gather(n + 3, 1 - u)
                    if left > 1:
                        root(n + 1)
                    for j in range(2):
                        pool.wait_ge(turned, n * 4 + 2 * j + 2)
                        pool.tensor_tensor(qk[:, j, bass.ds(n, 1), :].rearrange("p a d -> p (a d)"),
                                           ra[:, j, :], rb[:, j, :], ALU.add).then_inc(roped, 1)
                steps(pool, body)
                pool.wait_ge(roped, 2 * TILES + 2)

            @block.tensor
            def _(pe):
                def turn_rows(n, u):
                    pe.wait_ge(gathered[u], uses(n, u) * 16)
                    pe.transpose(ps[0][0:EMB + 1, 0:P], rows[:, u, :], ident[:, :]).then_inc(rows_t, 1)

                def embed(n, u):
                    pe.wait_ge(rtl_ok, n + 1)
                    products(pe, ps[1][:, :], [(rth[:, :], th[:, :]), (rth[:, :], tl[:, :]), (rtl[:, :], th[:, :])]
                             ).then_inc(h_ps, 1)

                def turn_x(n):
                    pe.wait_ge(xn_ok, n + 1)
                    for c in range(DC):
                        mm = pe.transpose(ps[2][:, c * P:(c + 1) * P], xn[:, c * P:(c + 1) * P], ident[:, :])
                    mm.then_inc(xt_ps, 1)

                def project(n, u, j):
                    products(pe, ps[3 + j][:, :],
                             [(a[:, u, c * P:(c + 1) * P], w[:, c, j * D:(j + 1) * D])
                              for c in range(DC) for a, w in ((xh, wh), (xh, wl), (xl, wh))]).then_inc(proj, 1)

                turn_rows(0, 0)
                embed(0, 0)
                turn_rows(1, 1)
                turn_x(0)

                def body(n, u, left):
                    if left > 1:
                        pe.wait_ge(h_ok, n + 1)
                        embed(n + 1, 1 - u)
                    if left > 2:
                        turn_rows(n + 2, u)
                    pe.wait_ge(xl_ok, n + 1)
                    pe.wait_ge(biased, n * 2 + 1)
                    project(n, u, 0)
                    if left > 1:
                        turn_x(n + 1)
                    pe.wait_ge(biased, n * 2 + 2)
                    project(n, u, 1)
                    pe.wait_ge(v_ok, n + 1)
                    project(n, u, 2)
                steps(pe, body)

            @block.scalar
            def _(act):
                def rows_high(n):
                    act.wait_ge(rows_t, n + 1)
                    act.activation(rth[:, :], ps[0][0:EMB + 1, 0:P], ACT.Copy).then_inc(rth_ok, 1)

                def scale_h(n, u):
                    act.wait_ge(h_ps, n + 1)
                    act.wait_ge(h_out[u], uses(n, u) * 16)
                    act.activation(h[:, u, :], ps[1][:, :], ACT.Copy, scale=float(D) ** 0.5).then_inc(h_ok, 1)

                def x_high(n, u):
                    act.wait_ge(xt_ps, n + 1)
                    act.activation(xh[:, u, :], ps[2][:, :], ACT.Copy).then_inc(xh_ok, 1)

                rows_high(0)
                scale_h(0, 0)
                rows_high(1)
                x_high(0, 0)

                def body(n, u, left):
                    if left > 1:
                        scale_h(n + 1, 1 - u)
                    if left > 2:
                        rows_high(n + 2)
                    if left > 1:
                        x_high(n + 1, 1 - u)
                steps(act, body)

            @block.vector
            def _(dve):
                def rows_low(n):
                    dve.wait_ge(rth_ok, n + 1)
                    dve.tensor_tensor(rtl[:, :], ps[0][0:EMB + 1, 0:P], rth[:, :].bitcast(F32), ALU.subtract
                                      ).then_inc(rtl_ok, 1)

                def normalise(n, u):
                    ch = Chain(dve, dch, 2, n)
                    dve.wait_ge(h_ok, n + 1)
                    ch.inc(dve.bn_stats(stats[:, :], h[:, u, :]))
                    ch.wait()
                    dve.nop().then_inc(held, 1)
                    ch.inc(dve.bn_aggr(mv[:, :], stats[:, :]))
                    ch.wait()
                    ch.done()
                    dve.tensor_scalar(mv[:, 1:2], mv[:, 1:2], eps[:, 0:1], None, ALU.add).then_inc(var_ok, 1)
                    dve.wait_ge(rstd_ok, n + 1)
                    dve.tensor_scalar(xn[:, :], h[:, u, :], mv[:, 0:1], rstd[:, 0:1], ALU.subtract, ALU.mult
                                      ).then_inc(xn_ok, 1)

                def x_low(n, u):
                    dve.wait_ge(xh_ok, n + 1)
                    dve.tensor_tensor(xl[:, u, :], ps[2][:, :], xh[:, u, :].bitcast(F32), ALU.subtract
                                      ).then_inc(xl_ok, 1)

                def rotate(n, j):
                    dve.wait_ge(proj, n * 3 + j + 1)
                    dve.tensor_tensor(qb[:, j, :], ps[3 + j][:, :], bias[:, j * D:(j + 1) * D], ALU.add
                                      ).then_inc(biased, 1)
                    dve.wait_ge(biased, n * 2 + j + 3)
                    dve.wait_ge(roped, n * 2 + j + 1)
                    src = qb[:, j, :].rearrange("p (a d) -> p a d", a=HEADS)
                    cos = cs[:, 0, bass.ds(n * DK, DK)]
                    dve.tensor_tensor(ra[:, j, :].rearrange("p (a d) -> p a d", a=HEADS), src,
                                      cos.unsqueeze(1).broadcast_to([P, HEADS, DK]), ALU.mult).then_inc(turned, 1)
                    dst = rb[:, j, :].rearrange("p (a d) -> p a d", a=HEADS)
                    for k in range(2):
                        sin = cs[:, 1, bass.ds(n * DK + k * HF, HF)]
                        ins = dve.tensor_tensor(dst[:, :, k * HF:(k + 1) * HF], src[:, :, (1 - k) * HF:(2 - k) * HF],
                                                sin.unsqueeze(1).broadcast_to([P, HEADS, HF]), ALU.mult)
                    ins.then_inc(turned, 1)

                dve.nop().then_inc(biased, 2)
                dve.nop().then_inc(v_ok, 1)
                dve.wait_ge(const_in, 32)
                dve.wait_ge(const_set, 3)
                rows_low(0)
                normalise(0, 0)
                rows_low(1)
                x_low(0, 0)

                def body(n, u, left):
                    if left > 1:
                        normalise(n + 1, 1 - u)
                    if left > 2:
                        rows_low(n + 2)
                    rotate(n, 0)
                    if left > 1:
                        x_low(n + 1, 1 - u)
                    rotate(n, 1)
                    dve.wait_ge(proj, n * 3 + 3)
                    dve.tensor_tensor(v_all[:, bass.ds(n, 1), :].rearrange("p a d -> p (a d)"),
                                      ps[5][:, :], bias[:, 2 * D:3 * D], ALU.add).then_inc(v_ok, 1)
                steps(dve, body)
                dve.wait_ge(v_ok, TILES + 1)


def phase_b(nc, t, keep):
    qk, v_all, ident, identb = keep["qk"], keep["v"], keep["ident"], keep["identb"]
    with ExitStack() as ctx:
        sb = lambda n, s, d: ctx.enter_context(nc.sbuf_tensor("b_" + n, s, d))
        sem = lambda n: ctx.enter_context(nc.semaphore("b_" + n))
        sc = [ctx.enter_context(nc.psum_tensor(f"b_sc{i}", [P, 2, QB], F32)) for i in range(2)]
        acc = [[ctx.enter_context(nc.psum_tensor(f"b_acc{i}{j}", [P, QB], F32)) for j in range(2)] for i in range(2)]
        tp = acc[1]
        q3 = sb("q3", [P, 2, HPG, KS], F32R)
        k3 = sb("k3", [P, 2, HPG, KS], F32R)
        q3t = sb("q3t", [KS + 1, HPG, SEQ], F32R)
        k3t = sb("k3t", [KS + 1, HPG, SEQ], F32R)
        vu = sb("vu", [P, TPB, P], F32)
        ones = sb("ones", [P, DK], F32)
        mx = sb("mx", [P, HPG * TPB], F32)
        mxt = sb("mxt", [HPG * TPB, P], F32R)
        e = sb("e", [P, 4, 2, QB], F32)
        rec = sb("rec", [P, 2, QB], F32)

        set_ = sem("set")
        high = sem("high")
        low = sem("low")
        turned = sem("turned")
        q_in = sem("q_in")
        k_in = sem("k_in")
        v_in = sem("v_in")
        smax = sem("smax")
        mx_ok = sem("mx_ok")
        mxt_ps = sem("mxt_ps")
        mxt_ok = sem("mxt_ok")
        row_in = sem("row_in")
        st = sem("st")
        ex = sem("ex")
        pv = sem("pv")
        rec_ok = sem("rec_ok")
        norm = sem("norm")
        blocks = [(Q, kt) for Q in range(SEQ // QB) for kt in range((Q + 1) * QB // P)]
        NB = len(blocks)
        NR = HPG * TPB

        def units(eng, body):
            with eng.Fori(0, BATCH) as b:
                with eng.Fori(0, GROUPS) as g:
                    body(b * GROUPS + g, b, g)

        def chunk(ten, j, b, g, k):
            a = ten[:, j, bass.ds(b * TPB + k, 1), bass.ds(g * P, P)]
            return a.rearrange("p a (h d) -> p (a h) d", h=HPG)

        with nc.Block() as block:
            @block.sync
            def _(sp):
                def body(n, b, g):
                    sp.wait_ge(mxt_ok, n + 1)
                    sp.dma_start(q3t[KS:KS + 1, :, :].rearrange("o h (k q) -> o (h k) q", q=P).bitcast(F32),
                                 mxt[:, :].bitcast(F32)
                                 ).then_inc(row_in, 16)
                units(sp, body)
                sp.wait_ge(row_in, 16 * UNITS)

            @block.gpsimd
            def _(pool):
                pool.memset(ones[:, :], 1.0).then_inc(set_, 1)
                pool.wait_ge(set_, 1)
                pool.memset(k3t[KS:KS + 1, :, :].bitcast(F32), 1.0).then_inc(set_, 1)
                pool.wait_ge(set_, 2)

                def body(n, b, g):
                    pool.wait_ge(pv, n * NB + NB)
                    pool.tensor_copy(vu[:, :, :], v_all[:, bass.ds(b * TPB, TPB), bass.ds(g * P, P)]).then_inc(v_in, 1)
                units(pool, body)

            @block.tensor
            def _(pe):
                pe.wait_ge(set_, 2)
                pe.nop().then_inc(turned, 4)
                pe.nop().then_inc(pv, NB)

                def turn(n, k):
                    for j, (src, done_) in enumerate(((q3, q_in), (k3, k_in))):
                        pe.wait_ge(low, n * 2 * TPB + 2 * k + j + 1)
                        pe.wait_ge(done_, n * TPB + k + 1)
                        for h in range(HPG):
                            mm = pe.transpose(tp[j][0:KS, h * P:(h + 1) * P], src[:, k % 2, h, :].bitcast(F32), ident[:, :])
                        mm.then_inc(turned, 1)

                def score(n, i):
                    qt, h = divmod(i, HPG)
                    if i < 2:
                        pe.wait_ge(ex, n * 2 * NB + 2 * NB)
                    else:
                        pe.wait_ge(mx_ok, n * NR + i - 1)
                    keys = (qt + 1) * P
                    for s in range(0, keys, QB):
                        w = min(QB, keys - s)
                        pe.matmul(sc[i % 2][:, s // QB, 0:w], q3t[0:KS, h, qt * P:(qt + 1) * P], k3t[0:KS, h, s:s + w],
                                  start=True, stop=s + w < keys)
                    s, o = divmod(qt * P, QB)
                    pe.matmul(sc[i % 2][:, s, o:o + P], identb[:, :], keep["mask_q"][:, :], start=False, stop=True
                              ).then_inc(smax, 1)

                def score_t(n, j):
                    (Q, kt), pair = blocks[j // 2], j % 2
                    off = max(0, kt * P - Q * QB)
                    if j >= 2:
                        pe.wait_ge(ex, n * 2 * NB + 2 * NB + j - 1)
                    for hh in range(2):
                        h = 2 * pair + hh
                        diag = kt * P >= Q * QB
                        mm = pe.matmul(sc[j % 2][:, hh, 0:QB - off], k3t[:, h, kt * P:(kt + 1) * P],
                                       q3t[:, h, Q * QB + off:(Q + 1) * QB], start=True, stop=not diag)
                        if diag:
                            mm = pe.matmul(sc[j % 2][:, hh, 0:P], identb[:, :], keep["mask_k"][:, :], start=False, stop=True)
                    mm.then_inc(st, 1)

                def weigh(n, i):
                    Q, kt = blocks[i]
                    off = max(0, kt * P - Q * QB)
                    if kt == 0:
                        pe.wait_ge(norm, n * 2 + Q + 1)
                    pe.wait_ge(ex, n * 2 * NB + 2 * NB + 2 * i + 2)
                    ends = kt == (Q + 1) * QB // P - 1
                    for which in range(2):
                        for h in range(HPG):
                            lhs = vu[:, kt, h * DK:(h + 1) * DK] if which == 0 else ones[:, :]
                            mm = pe.matmul(acc[Q][which][h * DK:(h + 1) * DK, off:QB], lhs,
                                           e[:, (2 * i + h // 2) % 4, h % 2, 0:QB - off], start=(kt == 0), stop=ends)
                    mm.then_inc(pv, 1)

                def body(n, b, g):
                    pe.wait_ge(norm, n * 2 + 2)
                    for k in range(TPB):
                        turn(n, k)
                    pe.wait_ge(q_in, n * TPB + TPB + 1)
                    pe.wait_ge(k_in, n * TPB + TPB + 1)
                    for i in range(NR):
                        score(n, i)
                    pe.wait_ge(mx_ok, n * NR + NR)
                    pe.transpose(tp[0][0:NR, 0:P], mx[:, :], ident[:, :]).then_inc(mxt_ps, 1)
                    pe.wait_ge(row_in, n * 16 + 16)
                    pe.wait_ge(v_in, n + 1)
                    for i in range(NB):
                        score_t(n, 2 * i)
                        score_t(n, 2 * i + 1)
                        if i > 0:
                            weigh(n, i - 1)
                    weigh(n, NB - 1)
                units(pe, body)

            @block.scalar
            def _(act):
                act.nop().then_inc(q_in, 1)
                act.nop().then_inc(ex, 2 * NB)

                def q_out(n, k):
                    act.wait_ge(turned, n * 2 * TPB + 2 * k + 1 + 4)
                    act.activation(q3t[0:KS, :, k * P:(k + 1) * P], tp[0][0:KS, :].rearrange("p (h q) -> p h q", h=HPG),
                                   ACT.Copy).then_inc(q_in, 1)

                def body(n, b, g):
                    for k in range(TPB):
                        act.wait_ge(turned, n * 2 * TPB + 2 * k + 2)
                        q = chunk(qk, 0, b, g, k)
                        for r in range(2):
                            ins = act.activation(q3[:, k % 2, :, r * DK:(r + 1) * DK], q, ACT.Copy)
                        ins.then_inc(high, 1)
                        kk = chunk(qk, 1, b, g, k)
                        for r in range(2):
                            ins = act.activation(k3[:, k % 2, :, 2 * r * DK:(2 * r + 1) * DK], kk, ACT.Copy)
                        ins.then_inc(high, 1)
                        if k > 0:
                            q_out(n, k - 1)
                    q_out(n, TPB - 1)
                    act.wait_ge(mxt_ps, n + 1)
                    act.activation(mxt[:, :], tp[0][0:NR, 0:P], ACT.Copy, scale=-1.0).then_inc(mxt_ok, 1)
                    for j in range(2 * NB):
                        Q, kt = blocks[j // 2]
                        w = QB - max(0, kt * P - Q * QB)
                        act.wait_ge(st, n * 2 * NB + j + 1)
                        act.wait_ge(pv, n * NB + j // 2 + NB - 1)
                        act.activation(e[:, j % 4, :, 0:w], sc[j % 2][:, :, 0:w], ACT.Exp, scale=SCALE).then_inc(ex, 1)
                units(act, body)

            @block.vector
            def _(dve):
                dve.nop().then_inc(k_in, 1)
                dve.nop().then_inc(norm, 2)

                def k_out(n, k):
                    dve.wait_ge(turned, n * 2 * TPB + 2 * k + 2 + 4)
                    dve.tensor_copy(k3t[0:KS, :, k * P:(k + 1) * P], tp[1][0:KS, :].rearrange("p (h q) -> p h q", h=HPG)
                                    ).then_inc(k_in, 1)

                def body(n, b, g):
                    for k in range(TPB):
                        dve.wait_ge(high, n * 2 * TPB + 2 * k + 1)
                        dve.tensor_tensor(q3[:, k % 2, :, 2 * DK:3 * DK], chunk(qk, 0, b, g, k),
                                          q3[:, k % 2, :, 0:DK].bitcast(F32), ALU.subtract).then_inc(low, 1)
                        dve.wait_ge(high, n * 2 * TPB + 2 * k + 2)
                        dve.tensor_tensor(k3[:, k % 2, :, DK:2 * DK], chunk(qk, 1, b, g, k),
                                          k3[:, k % 2, :, 0:DK].bitcast(F32), ALU.subtract).then_inc(low, 1)
                        if k > 0:
                            k_out(n, k - 1)
                    k_out(n, TPB - 1)
                    for i in range(NR):
                        qt, h = divmod(i, HPG)
                        dve.wait_ge(smax, n * NR + i + 1)
                        keys = (qt + 1) * P
                        src = sc[i % 2][:, :, :].rearrange("p a b -> p (a b)")[:, 0:keys]
                        dve.tensor_reduce(mx[:, h * TPB + qt:h * TPB + qt + 1], src, AXX, ALU.max).then_inc(mx_ok, 1)
                    for Q in range(SEQ // QB):
                        dve.wait_ge(pv, n * NB + NB + sum(1 for a, _ in blocks if a <= Q))
                        dve.reciprocal(rec[:, Q, :], acc[Q][1][:, :]).then_inc(rec_ok, 1)
                        dve.wait_ge(rec_ok, n * 2 + Q + 1)
                        dve.tensor_tensor(qk[:, 0, bass.ds(b * TPB + Q * QB // P, QB // P), bass.ds(g * P, P)],
                                          acc[Q][0][:, :].rearrange("p (a q) -> p a q", q=P),
                                          rec[:, Q, :].rearrange("p (a q) -> p a q", q=P), ALU.mult).then_inc(norm, 1)
                units(dve, body)
                dve.wait_ge(norm, 2 * UNITS + 2)


def phase_c(nc, t, keep, logits):
    qk, ident = keep["qk"], keep["ident"]
    with ExitStack() as ctx:
        sb = lambda n, s, d: ctx.enter_context(nc.sbuf_tensor("c_" + n, s, d))
        sem = lambda n: ctx.enter_context(nc.semaphore("c_" + n))
        ps_o = ctx.enter_context(nc.psum_tensor("c_ps_o", [P, D], F32))
        ps_x = ctx.enter_context(nc.psum_tensor("c_ps_x", [P, D], F32))
        ps_g = ctx.enter_context(nc.psum_tensor("c_ps_g", [P, D], F32))
        wh = sb("wh", [P, DC, D], F32R)
        wl = sb("wl", [P, DC, D], F32R)
        with ExitStack() as c2:
            split_load(nc, c2, lambda n, s, d: c2.enter_context(nc.sbuf_tensor("c_" + n, s, d)),
                       lambda n: c2.enter_context(nc.semaphore("c_" + n)), "w",
                       [(t["out_w"][c * P:(c + 1) * P, :], wh[:, c, :], wl[:, c, :]) for c in range(DC)])
        gw = sb("gw", [P, DC, EXPERTS], F32)
        gb = sb("gb", [P, EXPERTS], F32)
        ob = sb("ob", [P, D], F32)
        hin = sb("hin", [P, 2, D], F32)
        hb = sb("hb", [P, D], F32)
        ah = sb("ah", [P, 2, D], F32R)
        al = sb("al", [P, 2, D], F32R)
        h = sb("h", [P, 2, D], F32)
        xn = sb("xn", [P, 2, D], F32)
        xt = sb("xt", [P, D], F32)
        stats = sb("stats", [P, 6], F32)
        mv = sb("mv", [P, 2], F32)
        rstd = sb("rstd", [P, 1], F32)
        nhalf = sb("nhalf", [P, 1], F32)

        held = sem("held")
        const_in = sem("const_in")
        const_set = sem("const_set")
        h_in = [sem(f"h_in{u}") for u in range(2)]
        hb_ok = sem("hb_ok")
        ah_ok = sem("ah_ok")
        al_ok = sem("al_ok")
        proj = sem("proj")
        h_ok = sem("h_ok")
        h_out = [sem(f"h_out{u}") for u in range(2)]
        x_out = [sem(f"x_out{u}") for u in range(2)]
        var_ok = sem("var_ok")
        rstd_ok = sem("rstd_ok")
        xn_ok = sem("xn_ok")
        xt_ps = sem("xt_ps")
        xt_ok = sem("xt_ok")
        gate = sem("gate")
        gate_ok = sem("gate_ok")
        dch = sem("dch")
        PEEL = 2

        def steps(eng, body):
            with eng.Fori(0, (TILES - PEEL) // 2) as i:
                for u in range(2):
                    body(i * 2 + u, u, TILES)
            for n in range(TILES - PEEL, TILES):
                body(n, n % 2, TILES - n)

        def uses(n, u):
            return (n - u) // 2 + 1

        with nc.Block() as block:
            @block.sync
            def _(sp):
                def load(n, u):
                    sp.dma_start(hin[:, u, :], t["h0"][bass.ds(n * P, P), :]).then_inc(h_in[u], 16)

                sp.dma_start(gw[:, :, :], t["gate_w"].rearrange("(c p) e -> p c e", p=P)).then_inc(const_in, 16)
                sp.dma_start(gb[:, :], t["gate_b"].partition_broadcast(P)).then_inc(const_in, 16)
                sp.dma_start(ob[:, :], t["out_b"].partition_broadcast(P)).then_inc(const_in, 16)
                for u in range(2):
                    sp.nop().then_inc(h_out[u], 16)
                    sp.nop().then_inc(x_out[u], 16)
                    load(u, u)

                def body(n, u, left):
                    sp.wait_ge(hb_ok, n + 1)
                    if left > 2:
                        load(n + 2, u)
                    sp.wait_ge(h_ok, n + 1)
                    sp.dma_start(t["out"][bass.ds(n * P, P), :], h[:, u, :]).then_inc(h_out[u], 16)
                    sp.wait_ge(xn_ok, n + 1)
                    sp.dma_start(t["xn"][bass.ds(n * P, P), :], xn[:, u, :]).then_inc(x_out[u], 16)
                steps(sp, body)
                for u in range(2):
                    sp.wait_ge(h_out[u], 8 * TILES + 16)
                    sp.wait_ge(x_out[u], 8 * TILES + 16)

            @block.gpsimd
            def _(pool):
                pool.memset(nhalf[:, :], -0.5).then_inc(const_set, 1)
                pool.wait_ge(const_set, 1)
                pool.wait_ge(const_in, 48)

                def bias(n, u):
                    pool.wait_ge(h_in[u], uses(n, u) * 16)
                    pool.tensor_tensor(hb[:, :], hin[:, u, :], ob[:, :], ALU.add).then_inc(hb_ok, 1)

                bias(0, 0)

                def body(n, u, left):
                    pool.wait_ge(var_ok, n + 1)
                    pool.tensor_tensor(rstd[:, :], mv[:, 1:2], nhalf[:, :], ALU.pow).then_inc(rstd_ok, 1)
                    if left > 1:
                        bias(n + 1, 1 - u)
                steps(pool, body)

            @block.tensor
            def _(pe):
                pe.wait_ge(const_in, 48)

                def project(n, u):
                    pe.wait_ge(al_ok, n + 1)
                    products(pe, ps_o[:, :], [(a[:, u, c * P:(c + 1) * P], w[:, c, :])
                                              for c in range(DC) for a, w in ((ah, wh), (ah, wl), (al, wh))]
                             ).then_inc(proj, 1)

                project(0, 0)

                def body(n, u, left):
                    if left > 1:
                        pe.wait_ge(h_ok, n + 1)
                        project(n + 1, 1 - u)
                    pe.wait_ge(xn_ok, n + 1)
                    for c in range(DC):
                        mm = pe.transpose(ps_x[:, c * P:(c + 1) * P], xn[:, u, c * P:(c + 1) * P], ident[:, :])
                    mm.then_inc(xt_ps, 1)
                    pe.wait_ge(xt_ok, n + 1)
                    pe.wait_ge(gate_ok, n + 1)
                    products(pe, ps_g[:, 0:EXPERTS], [(xt[:, c * P:(c + 1) * P], gw[:, c, :]) for c in range(DC)]
                             ).then_inc(gate, 1)
                steps(pe, body)

            @block.scalar
            def _(act):
                def high(n, u):
                    act.activation(ah[:, u, :], qk[:, 0, bass.ds(n, 1), :].rearrange("p a d -> p (a d)"), ACT.Copy
                                   ).then_inc(ah_ok, 1)

                high(0, 0)

                def body(n, u, left):
                    if left > 1:
                        if left < TILES:
                            act.wait_ge(proj, n)
                        high(n + 1, 1 - u)
                    act.wait_ge(xt_ps, n + 1)
                    act.activation(xt[:, :], ps_x[:, :], ACT.Copy).then_inc(xt_ok, 1)
                steps(act, body)

            @block.vector
            def _(dve):
                dve.nop().then_inc(gate_ok, 1)
                dve.wait_ge(const_in, 48)

                def low(n, u):
                    dve.wait_ge(ah_ok, n + 1)
                    dve.tensor_tensor(al[:, u, :], qk[:, 0, bass.ds(n, 1), :].rearrange("p a d -> p (a d)"),
                                      ah[:, u, :].bitcast(F32), ALU.subtract).then_inc(al_ok, 1)

                low(0, 0)

                def body(n, u, left):
                    ch = Chain(dve, dch, 2, n)
                    if left > 1:
                        low(n + 1, 1 - u)
                    dve.wait_ge(proj, n + 1)
                    dve.wait_ge(hb_ok, n + 1)
                    dve.wait_ge(h_out[u], uses(n, u) * 16)
                    dve.tensor_tensor(h[:, u, :], ps_o[:, :], hb[:, :], ALU.add).then_inc(h_ok, 1)
                    dve.wait_ge(h_ok, n + 1)
                    ch.inc(dve.bn_stats(stats[:, :], h[:, u, :]))
                    ch.wait()
                    dve.nop().then_inc(held, 1)
                    ch.inc(dve.bn_aggr(mv[:, :], stats[:, :]))
                    ch.wait()
                    dve.tensor_scalar(mv[:, 1:2], mv[:, 1:2], LN_EPS, None, ALU.add).then_inc(var_ok, 1)
                    dve.wait_ge(rstd_ok, n + 1)
                    dve.wait_ge(x_out[u], uses(n, u) * 16)
                    dve.tensor_scalar(xn[:, u, :], h[:, u, :], mv[:, 0:1], rstd[:, 0:1], ALU.subtract, ALU.mult
                                      ).then_inc(xn_ok, 1)
                    dve.wait_ge(gate, n + 1)
                    dve.tensor_tensor(logits[:, bass.ds(n, 1), :].rearrange("p a e -> p (a e)"), ps_g[:, 0:EXPERTS],
                                      gb[:, :], ALU.add).then_inc(gate_ok, 1)
                    ch.done()
                steps(dve, body)
                dve.wait_ge(gate_ok, TILES + 1)


def routing(nc, t, keep, logits, plan):
    E, T = EXPERTS, TILES
    PAD = 8
    with ExitStack() as ctx:
        sb = lambda n, s, d=F32: ctx.enter_context(nc.sbuf_tensor("r_" + n, s, d))
        sem = lambda n: ctx.enter_context(nc.semaphore("r_" + n))
        ps = ctx.enter_context(nc.psum_tensor("r_ps", [P, 2, 512], F32))
        bb = sb("bb", [P, E])
        tri = sb("tri", [P, E, E])
        ones_f = sb("ones_f", [P, P])
        before = sb("before", [P, P], BF16)
        ones_b = sb("ones_b", [P, P], BF16)
        marks = sb("marks", [P, T])
        slot_no = sb("slot_no", [P, SLOTS])
        number = sb("number", [P, E])
        m1 = sb("m1", [P, T])
        lc = sb("lc", [P, T, E])
        ex = sb("ex", [P, T, E])
        s1 = sb("s1", [P, T])
        r1 = sb("r1", [P, T])
        pr = sb("pr", [P, T, E])
        bp = sb("bp", [P, T, E])
        gt = sb("gt", [P, T, E * E])
        eq = sb("eq", [P, T, E * E])
        eqt = sb("eqt", [P, T, E * E])
        gts = sb("gts", [P, T, E * E])
        rank = sb("rank", [P, T, E])
        sel = sb("sel", [P, T, E])
        selb = sb("selb", [P, T, E], BF16)
        sp_ = sb("sp", [P, T, E])
        s2 = sb("s2", [P, T])
        r2 = sb("r2", [P, T])
        w = sb("w", [P, T, E])
        cum = sb("cum", [P, 5, PAD + T, E])
        cnt = sb("cnt", [P, E, T])
        nt = sb("nt", [P, E])
        ntt = sb("ntt", [P, E, E])
        base = sb("base", [P, E])
        end = sb("end", [P, E])
        base128 = sb("base128", [P, E])
        off = sb("off", [P, T, E])
        off2 = sb("off2", [P, T, E])
        pos = sb("pos", [P, T, E])
        is_k = sb("is_k", [P, TOPK, T, E])
        pos_k = sb("pos_k", [P, TOPK, T, E])
        w_k = sb("w_k", [P, TOPK, T, E])
        some = sb("some", [P, E])
        sot = sb("sot", [P, E, E])
        run_of = sb("run_of", [P, E])
        at = sb("at", [P, 3, SLOTS, E])
        at2 = sb("at2", [P, 3, SLOTS, E])
        run1 = sb("run1", [P, SLOTS])
        runp = sb("runp", [P, SLOTS])
        isf = sb("isf", [P, SLOTS])
        late = sb("late", [P, SLOTS])
        num_some = sb("num_some", [P, E])

        const_in = sem("const_in")
        pset = sem("pset")
        c = sem("c")
        exp_ok = sem("exp_ok")
        pre = sem("pre")

        with nc.allow_low_precision(reason="whole numbers, written as int32"), nc.Block() as block:
            @block.sync
            def _(sp):
                sp.dma_start(bb[:, :], t["biases"].partition_broadcast(P)).then_inc(const_in, 16)
                sp.wait_ge(const_in, 16)

            @block.gpsimd
            def _(pool):
                n = 0
                for a, val in ((tri, 1.0), (ones_f, 1.0), (cum, 0.0)):
                    pool.memset(a[:], val).then_inc(pset, 1)
                    n += 1
                pool.wait_ge(pset, n)
                pool.affine_select(out=tri[:, :, :], in_=tri[:, :, :], compare_op=ALU.is_gt, fill=0.0, base=0,
                                   pattern=[[1, E], [-1, E]], channel_multiplier=0).then_inc(pset, 1)
                pool.affine_select(out=before[:, :], in_=ones_f[:, :], compare_op=ALU.is_gt, fill=0.0, base=0,
                                   pattern=[[1, P]], channel_multiplier=-1).then_inc(pset, 1)
                pool.tensor_copy(ones_b[:, :], ones_f[:, :]).then_inc(pset, 1)
                pool.iota(marks[:, :], pattern=[[P, T]], base=0, channel_multiplier=0,
                          allow_small_or_imprecise_dtypes=True).then_inc(pset, 1)
                pool.iota(slot_no[:, :], pattern=[[1, SLOTS]], base=0, channel_multiplier=0,
                          allow_small_or_imprecise_dtypes=True).then_inc(pset, 1)
                pool.iota(number[:, :], pattern=[[1, E]], base=0, channel_multiplier=0,
                          allow_small_or_imprecise_dtypes=True).then_inc(pset, 1)
                pool.iota(plan["pair"][:, :, :, 0:1], pattern=[[0, TOPK], [P, T]], base=0, channel_multiplier=1
                          ).then_inc(pset, 1)
                pool.wait_ge(pset, n + 7)

            @block.tensor
            def _(pe):
                pe.wait_ge(pset, 10)
                pe.wait_ge(c, SEL)
                flat = selb[:, :, :].rearrange("p t e -> p (t e)")
                pe.matmul(ps[:, 0, 0:T * E], before[:, :], flat, start=True, stop=True)
                pe.matmul(ps[:, 1, 0:T * E], ones_b[:, :], flat, start=True, stop=True).then_inc(pre, 1)

            @block.scalar
            def _(act):
                act.wait_ge(c, 2)
                act.activation(ex[:, :, :], lc[:, :, :], ACT.Exp).then_inc(exp_ok, 1)

            @block.vector
            def _(dve):
                count = [0]

                def step(ins):
                    count[0] += 1
                    ins.then_inc(c, 1)
                    dve.wait_ge(c, count[0])

                def te(a):
                    return a.unsqueeze(2).broadcast_to([P, T, E])

                def over_t(a):
                    return a.unsqueeze(1).broadcast_to([P, T, E])

                TT, TS, RED = dve.tensor_tensor, dve.tensor_scalar, dve.tensor_reduce
                dve.wait_ge(const_in, 16)
                dve.wait_ge(pset, 10)
                step(RED(m1[:, :], logits[:, :, :], AXX, ALU.max))
                step(TT(lc[:, :, :], logits[:, :, :], te(m1[:, :]), ALU.subtract))
                dve.wait_ge(exp_ok, 1)
                step(RED(s1[:, :], ex[:, :, :], AXX, ALU.add))
                step(dve.reciprocal(r1[:, :], s1[:, :]))
                step(TT(pr[:, :, :], ex[:, :, :], te(r1[:, :]), ALU.mult))
                step(TT(bp[:, :, :], pr[:, :, :], over_t(bb[:, :]), ALU.add))
                pair = lambda a: a[:, :, :].rearrange("p t (e f) -> p t e f", e=E)
                mine = bp[:, :, :].unsqueeze(3).broadcast_to([P, T, E, E])
                other = bp[:, :, :].unsqueeze(2).broadcast_to([P, T, E, E])
                step(TT(pair(gt), other, mine, ALU.is_gt))
                step(TT(pair(eq), other, mine, ALU.is_equal))
                step(TT(eqt[:, :, :], eq[:, :, :], tri[:, :, :].rearrange("p e f -> p (e f)").unsqueeze(1)
                        .broadcast_to([P, T, E * E]), ALU.mult))
                step(TT(gts[:, :, :], gt[:, :, :], eqt[:, :, :], ALU.add))
                step(RED(rank[:, :, :], pair(gts), AXX, ALU.add))
                step(TS(sel[:, :, :], rank[:, :, :], TOPK - 0.5, None, ALU.is_lt))
                step(dve.tensor_copy(selb[:, :, :], sel[:, :, :]))
                assert count[0] == SEL
                step(TT(sp_[:, :, :], sel[:, :, :], pr[:, :, :], ALU.mult))
                step(RED(s2[:, :], sp_[:, :, :], AXX, ALU.add))
                step(dve.reciprocal(r2[:, :], s2[:, :]))
                step(TT(w[:, :, :], sp_[:, :, :], te(r2[:, :]), ALU.mult))
                dve.wait_ge(pre, 1)
                step(dve.tensor_copy(cum[:, 0, PAD:, :], ps[:, 1, 0:T * E].rearrange("p (t e) -> p t e", e=E)))
                for i in range(4):
                    sh = 1 << i
                    step(TT(cum[:, i + 1, PAD:, :], cum[:, i, PAD:, :], cum[:, i, PAD - sh:PAD + T - sh, :], ALU.add))
                total = cum[:, 4, PAD + T - 1, :]
                step(TT(cnt[:, :, :], total.unsqueeze(2).broadcast_to([P, E, T]),
                        marks[:, :].unsqueeze(1).broadcast_to([P, E, T]), ALU.is_gt))
                step(RED(nt[:, :], cnt[:, :, :], AXX, ALU.add))
                step(TT(ntt[:, :, :], nt[:, :].unsqueeze(1).broadcast_to([P, E, E]), tri[:, :, :], ALU.mult))
                step(RED(base[:, :], ntt[:, :, :], AXX, ALU.add))
                step(TS(base128[:, :], base[:, :], float(P), None, ALU.mult))
                step(TT(off[:, :, :], cum[:, 4, PAD:, :], cum[:, 0, PAD:, :], ALU.subtract))
                step(TT(off2[:, :, :], ps[:, 0, 0:T * E].rearrange("p (t e) -> p t e", e=E), off[:, :, :], ALU.add))
                step(TT(pos[:, :, :], off2[:, :, :], over_t(base128[:, :]), ALU.add))
                for k in range(TOPK):
                    step(TS(is_k[:, k, :, :], rank[:, :, :], float(k), None, ALU.is_equal))
                    step(TT(pos_k[:, k, :, :], is_k[:, k, :, :], pos[:, :, :], ALU.mult))
                    step(RED(plan["row"][:, k, :], pos_k[:, k, :, :], AXX, ALU.add))
                    step(TT(w_k[:, k, :, :], is_k[:, k, :, :], w[:, :, :], ALU.mult))
                    step(RED(plan["pair"][:, k, :, 1:2].bitcast(F32).rearrange("p t o -> p (t o)"),
                             w_k[:, k, :, :], AXX, ALU.add))
                step(TS(some[:, :], nt[:, :], 0.5, None, ALU.is_gt))
                step(TT(sot[:, :, :], some[:, :].unsqueeze(1).broadcast_to([P, E, E]), tri[:, :, :], ALU.mult))
                step(RED(run_of[:, :], sot[:, :, :], AXX, ALU.add))
                step(TT(num_some[:, :], number[:, :], some[:, :], ALU.mult))

                def by_slot(a):
                    return a.unsqueeze(2).broadcast_to([P, SLOTS, E])

                def by_expert(a):
                    return a.unsqueeze(1).broadcast_to([P, SLOTS, E])

                def pick(i, slot_value, expert_value, op, weight, out):
                    step(TT(at[:, i, :, :], by_slot(slot_value), by_expert(expert_value), op))
                    step(TT(at2[:, i, :, :], at[:, i, :, :], by_expert(weight), ALU.mult))
                    step(RED(out, at2[:, i, :, :], AXX, ALU.add))

                pick(0, slot_no[:, :], base[:, :], ALU.is_ge, some[:, :], run1[:, :])
                pick(1, slot_no[:, :], base[:, :], ALU.is_equal, some[:, :], isf[:, :])
                pick(2, run1[:, :], run_of[:, :], ALU.is_equal, num_some[:, :], plan["next"][:, :])
                step(TS(late[:, :], run1[:, :], 1.5, None, ALU.is_gt))
                step(TT(plan["load"][:, :], isf[:, :], late[:, :], ALU.mult))
                step(TS(plan["run"][:, :], run1[:, :], -1.0, None, ALU.add))
                step(TS(s1[:, 0:E], run_of[:, :], 0.0, None, ALU.is_equal))
                step(TT(s2[:, 0:E], s1[:, 0:E], num_some[:, :], ALU.mult))
                step(RED(plan["first"][:, :], s2[:, 0:E], AXX, ALU.add))


SEL = 13


def experts(nc, t, keep, plan, W, stage, routed):
    ident = keep["ident"]
    N = SLOTS if routed else TILES
    pre = "d_" if routed else "s_"
    MATS = 3
    with ExitStack() as ctx:
        sb = lambda n, s, d: ctx.enter_context(nc.sbuf_tensor(pre + n, s, d))
        sem = lambda n: ctx.enter_context(nc.semaphore(pre + n))
        ps = lambda n: ctx.enter_context(nc.psum_tensor(pre + n, [P, HID], F32))
        ps_g, ps_u, ps_x, ps_y, ps_h = ps("ps_g"), ps("ps_u"), ps("ps_x"), ps("ps_y"), ps("ps_h")
        x = sb("x", [P, 2, D], F32)
        xh = sb("xh", [P, 2, D], F32R)
        xl = sb("xl", [P, 2, D], F32R)
        sg = sb("sg", [P, HID], F32)
        hs = sb("hs", [P, HID], F32)
        hh = sb("hh", [P, HID], F32R)
        hl = sb("hl", [P, HID], F32R)
        y = sb("y", [P, 2, D], F32)
        pairs = sb("pairs", [P, 4, 2], I32)
        idx = sb("idx", [P, 2, TOPK], I32)
        sent_pair = sb("sent_pair", [P, 2, TOPK, 2], I32)

        landed = [sem(f"landed{c}") for c in range(MATS)]
        w_hi = sem("w_hi")
        w_lo = sem("w_lo")
        pair_in = [sem(f"pair_in{r}") for r in range(4)]
        x_in = [sem(f"x_in{u}") for u in range(2)]
        x_ps = sem("x_ps")
        xh_ok = sem("xh_ok")
        xl_ok = sem("xl_ok")
        g_ps = sem("g_ps")
        u_ps = sem("u_ps")
        sg_ok = sem("sg_ok")
        hs_ok = sem("hs_ok")
        h_ps = sem("h_ps")
        hh_ok = sem("hh_ok")
        hl_ok = sem("hl_ok")
        y_ps = sem("y_ps")
        y_ok = sem("y_ok")
        held = sem("held")
        added = sem("added")
        y_free = sem("y_free")
        idx_ok = sem("idx_ok")
        sent = [[sem(f"sent{u}{k}") for k in range(TOPK)] for u in range(2)]

        first = 2
        last = 4 if routed else 2
        assert (N - first - last) % 4 == 0

        def steps(eng, body):
            for n in range(first):
                body(n, n, N)
            with eng.Fori(0, (N - first - last) // 4) as i:
                for u in range(4):
                    body(i * 4 + (first + u), (first + u) % 4, N)
            for n in range(N - last, N):
                body(n, n % 4, N - n)

        def uses(n, r, size):
            return (n - r) // size + 1

        def wmat(l, m, part, c):
            if not routed:
                return W[:, 0, m, part, c, :]
            half = (l % 2)
            return W[:, bass.ds(half, 1), m, part, c, :].rearrange("p a n -> p (a n)")

        def wpart(half, m, part):
            return W[:, bass.ds(half, 1), m, part, :, :].rearrange("p a c n -> p (a c n)")

        def load_weights(sp, l, expert):
            for m in range(MATS):
                src = t[("w1", "wg", "w2")[m]][bass.ds(expert, 1), :, :, :] if routed else t[("ws1", "wsg", "ws2")[m]]
                src = src.rearrange("a p c n -> p (a c) n") if routed else src
                sp.dma_start(stage[:, m, :].rearrange("p (c n) -> p c n", c=DC), src).then_inc(landed[m], 16)

        def split_high(act, l):
            for m in range(MATS):
                act.wait_ge(landed[m], l * 16)
                act.activation(wpart(half_of(l), m, 0), stage[:, m, :], ACT.Copy).then_inc(w_hi, 1)

        def split_low(dve, l):
            for m in range(MATS):
                dve.wait_ge(w_hi, (l - 1) * MATS + m + 1)
                dve.tensor_tensor(wpart(half_of(l), m, 1), stage[:, m, :], wpart(half_of(l), m, 0).bitcast(F32),
                                  ALU.subtract).then_inc(w_lo, 1)

        def half_of(l):
            return (l % 2) if routed else 0

        def value(eng, tab, n, lo, hi):
            return eng.value_load(plan[tab][0:1, bass.ds(n, 1)], min_val=lo, max_val=hi)

        with nc.Block() as block:
            @block.sync
            def _(sp):
                def load_pairs(n, r):
                    sp.dma_start(pairs[:, r, :], t["table"][bass.ds(n * P, P), :]).then_inc(pair_in[r], 16)

                def load_x(n, u):
                    sp.dma_start(x[:, u, :], t["xn"][bass.ds(n * P, P), :]).then_inc(x_in[u], 16)

                if routed:
                    load_weights(sp, 1, sp.value_load(plan["first"][0:1, 0:1], min_val=0, max_val=EXPERTS - 1))
                    sp.wait_ge(w_lo, MATS)
                    load_weights(sp, 2, sp.value_load(plan["next"][0:1, 0:1], min_val=0, max_val=EXPERTS - 1))
                    for r in range(3):
                        load_pairs(r, r)
                else:
                    load_weights(sp, 1, 0)
                    load_x(0, 0)
                    load_x(1, 1)

                def body(n, r, left):
                    first_ = isinstance(n, int) and n == 0
                    if not routed:
                        if left > 2:
                            sp.wait_ge(x_ps, n + 1)
                            load_x(n + 2, r % 2)
                        return
                    if left > 3:
                        if not first_:
                            sp.wait_ge(added, n * 16)
                        load_pairs(n + 3, (r + 3) % 4)
                    if first_:
                        return
                    with sp.If(value(sp, "load", n, 0, 1) > 0):
                        run = value(sp, "run", n, 0, EXPERTS - 1) + 1
                        nxt = value(sp, "next", n, 0, EXPERTS - 1)
                        sp.wait_ge(w_lo, run * MATS)
                        load_weights(sp, run + 1, nxt)
                    sp.nop()
                steps(sp, body)

            @block.gpsimd
            def _(pool):
                def gather(n, r):
                    pool.wait_ge(pair_in[r], uses(n, r, 4) * 16)
                    pool.nop().then_inc(held, 1)
                    pool.indirect_dma_start(out=x[:, r % 2, :], out_offset=None, in_=t["xn"],
                                            in_offset=bass.IndirectOffsetOnAxis(ap=pairs[:, r, 0:1], axis=0)
                                            ).then_inc(x_in[r % 2], 16)

                def add(n, r):
                    pool.wait_ge(y_ok, n + 1)
                    if not (isinstance(n, int) and n == 0):
                        pool.wait_ge(added, n * 16)
                        pool.nop().then_inc(y_free, 1)
                    pool.nop().then_inc(held, 1)
                    if routed:
                        pool.indirect_dma_start(out=t["out"], out_offset=bass.IndirectOffsetOnAxis(ap=pairs[:, r, 0:1], axis=0),
                                                in_=y[:, r % 2, :], in_offset=None, compute_op=ALU.add).then_inc(added, 16)
                    else:
                        pool.dma_start(t["out"][bass.ds(n * P, P), :], y[:, r % 2, :], accum_op=ALU.add
                                       ).then_inc(added, 16)

                def scatter(n, u, used):
                    for k in range(TOPK):
                        if not isinstance(used, int):
                            pool.wait_ge(sent[u][k], used * 16)
                    pool.tensor_copy(idx[:, u, :], plan["row"][:, :, bass.ds(n, 1)].rearrange("p k a -> p (k a)")
                                     ).then_inc(idx_ok, 1)
                    pool.tensor_copy(sent_pair[:, u, :, 0:1], plan["pair"][:, :, bass.ds(n, 1), 0:1]
                                     .rearrange("p k a w -> p k (a w)")).then_inc(idx_ok, 1)
                    pool.tensor_copy(sent_pair[:, u, :, 1:2].bitcast(F32),
                                     plan["pair"][:, :, bass.ds(n, 1), 1:2].bitcast(F32)
                                     .rearrange("p k a w -> p k (a w)")).then_inc(idx_ok, 1)
                    pool.wait_ge(idx_ok, n * 3 + 3)
                    pool.nop().then_inc(held, 1)
                    for k in range(TOPK):
                        pool.indirect_dma_start(
                            out=t["table"], out_offset=bass.IndirectOffsetOnAxis(ap=idx[:, u, k:k + 1], axis=0),
                            in_=sent_pair[:, u, k, :], in_offset=None).then_inc(sent[u][k], 16)

                pool.nop().then_inc(y_free, 1)
                if routed:
                    gather(0, 0)
                    gather(1, 1)
                else:
                    for u in range(2):
                        scatter(u, u, 0)
                    with pool.Fori(1, TILES // 2) as i:
                        for u in range(2):
                            scatter(i * 2 + u, u, i)

                def body(n, r, left):
                    first_ = isinstance(n, int) and n == 0
                    if routed and left > 2:
                        pool.wait_ge(x_ps, n + 1)
                        gather(n + 2, (r + 2) % 4)
                    if not first_:
                        add(n - 1, (r - 1) % 4)
                steps(pool, body)
                add(N - 1, (N - 1) % 4)
                pool.wait_ge(added, N * 16)
                if not routed:
                    for u in range(2):
                        for k in range(TOPK):
                            pool.wait_ge(sent[u][k], TILES // 2 * 16)

            @block.tensor
            def _(pe):
                def turn_x(n, u):
                    pe.wait_ge(x_in[u], uses(n, u, 2) * 16)
                    if not (isinstance(n, int) and n == 0):
                        pe.wait_ge(xl_ok, n)
                    for c in range(DC):
                        mm = pe.transpose(ps_x[:, c * P:(c + 1) * P], x[:, u, c * P:(c + 1) * P], ident[:, :])
                    mm.then_inc(x_ps, 1)

                def three(out, ah, al, run, m):
                    return products(pe, out, [(a[:, c * P:(c + 1) * P], wmat(run, m, part, c))
                                              for c in range(DC) for a, part in ((ah, 0), (ah, 1), (al, 0))])

                def run_of(n):
                    return value(pe, "run", n, 0, EXPERTS - 1) + 1 if routed else 1

                def down(n, run):
                    pe.wait_ge(w_lo, run * MATS)
                    pe.wait_ge(hl_ok, n + 1)
                    if not (isinstance(n, int) and n == 0):
                        pe.wait_ge(y_ok, n)
                    three(ps_y[:, :], hh, hl, run, 2).then_inc(y_ps, 1)

                turn_x(0, 0)

                def body(n, r, left):
                    first_ = isinstance(n, int) and n == 0
                    u = r % 2
                    run = run_of(n)
                    pe.wait_ge(w_lo, (run - 1) * MATS + 1)
                    pe.wait_ge(xl_ok, n + 1)
                    if not first_:
                        pe.wait_ge(sg_ok, n)
                    three(ps_g[:, :], xh[:, u, :], xl[:, u, :], run, 0).then_inc(g_ps, 1)
                    pe.wait_ge(w_lo, (run - 1) * MATS + 2)
                    if not first_:
                        pe.wait_ge(hs_ok, n)
                    three(ps_u[:, :], xh[:, u, :], xl[:, u, :], run, 1).then_inc(u_ps, 1)
                    if left > 1:
                        turn_x(n + 1, 1 - u)
                    if not first_:
                        down(n - 1, run_of(n - 1))
                    pe.wait_ge(hs_ok, n + 1)
                    if not first_:
                        pe.wait_ge(hl_ok, n)
                    for c in range(DC):
                        mm = pe.transpose(ps_h[:, c * P:(c + 1) * P], hs[:, c * P:(c + 1) * P], ident[:, :])
                    mm.then_inc(h_ps, 1)
                steps(pe, body)
                down(N - 1, run_of(N - 1))

            @block.scalar
            def _(act):
                def x_high(n, u):
                    act.wait_ge(x_ps, n + 1)
                    act.activation(xh[:, u, :], ps_x[:, :], ACT.Copy).then_inc(xh_ok, 1)

                def out(n, r):
                    act.wait_ge(y_ps, n + 1)
                    if not (isinstance(n, int) and n == 0):
                        act.wait_ge(y_free, n)
                    scale = pairs[:, r, 1:2].bitcast(F32) if routed else 1.0
                    act.activation(y[:, r % 2, :], ps_y[:, :], ACT.Copy, scale=scale).then_inc(y_ok, 1)

                split_high(act, 1)
                if routed:
                    act.wait_ge(w_lo, MATS)
                    split_high(act, 2)
                x_high(0, 0)

                def body(n, r, left):
                    first_ = isinstance(n, int) and n == 0
                    act.wait_ge(g_ps, n + 1)
                    act.activation(sg[:, :], ps_g[:, :], ACT.Silu).then_inc(sg_ok, 1)
                    if left > 1:
                        x_high(n + 1, 1 - r % 2)
                    if not first_:
                        out(n - 1, (r - 1) % 4)
                    act.wait_ge(h_ps, n + 1)
                    act.activation(hh[:, :], ps_h[:, :], ACT.Copy).then_inc(hh_ok, 1)
                    if routed and not first_:
                        with act.If(value(act, "load", n, 0, 1) > 0):
                            split_high(act, value(act, "run", n, 0, EXPERTS - 1) + 2)
                        act.nop()
                steps(act, body)
                out(N - 1, (N - 1) % 4)

            @block.vector
            def _(dve):
                def x_low(n, u):
                    dve.wait_ge(xh_ok, n + 1)
                    dve.tensor_tensor(xl[:, u, :], ps_x[:, :], xh[:, u, :].bitcast(F32), ALU.subtract
                                      ).then_inc(xl_ok, 1)

                split_low(dve, 1)
                if routed:
                    split_low(dve, 2)
                x_low(0, 0)

                def body(n, r, left):
                    first_ = isinstance(n, int) and n == 0
                    dve.wait_ge(sg_ok, n + 1)
                    dve.wait_ge(u_ps, n + 1)
                    dve.tensor_tensor(hs[:, :], ps_u[:, :], sg[:, :], ALU.mult).then_inc(hs_ok, 1)
                    if left > 1:
                        x_low(n + 1, 1 - r % 2)
                    dve.wait_ge(hh_ok, n + 1)
                    dve.tensor_tensor(hl[:, :], ps_h[:, :], hh[:, :].bitcast(F32), ALU.subtract).then_inc(hl_ok, 1)
                    if routed and not first_:
                        with dve.If(value(dve, "load", n, 0, 1) > 0):
                            split_low(dve, value(dve, "run", n, 0, EXPERTS - 1) + 2)
                        dve.nop()
                steps(dve, body)


def setup(nc, t, keep):
    ident, identb, cs = keep["ident"], keep["identb"], keep["cs"]
    with ExitStack() as ctx:
        zeros = ctx.enter_context(nc.sbuf_tensor("zeros", [P, D], F32))
        none = ctx.enter_context(nc.sbuf_tensor("none", [P, SLOTS, 2], I32))
        none_ok = ctx.enter_context(nc.semaphore("none_ok"))
        put = ctx.enter_context(nc.semaphore("put"))
        zero = ctx.enter_context(nc.semaphore("zero"))
        cs_in = ctx.enter_context(nc.semaphore("cs_in"))
        with nc.Block() as block:
            @block.sync
            def _(sp):
                sp.dma_start(cs[:, :, :], t["cs"]).then_inc(cs_in, 16)
                sp.wait_ge(zero, 1)
                sp.dma_start(t["xn"][TOKENS:TOKENS + P, :], zeros[:, :]).then_inc(cs_in, 16)
                sp.dma_start(t["out"][TOKENS:TOKENS + P, :], zeros[:, :]).then_inc(cs_in, 16)
                sp.wait_ge(none_ok, 2)
                sp.dma_start(t["table"].rearrange("(s p) w -> p s w", p=P), none[:, :, :]).then_inc(cs_in, 16)
                sp.wait_ge(cs_in, 64)

            @block.gpsimd
            def _(pool):
                pool.memset(zeros[:, :], 0.0).then_inc(zero, 1)
                pool.wait_ge(zero, 1)
                for out in (ident, identb):
                    pool.affine_select(out=out[:, :], in_=zeros[:, 0:P], compare_op=ALU.not_equal, fill=1.0, base=0,
                                       pattern=[[-1, P]], channel_multiplier=1).then_inc(put, 1)
                pool.affine_select(out=keep["mask_q"][:, :], in_=zeros[:, 0:P], compare_op=ALU.is_ge, fill=NEG, base=0,
                                   pattern=[[-1, P]], channel_multiplier=1).then_inc(put, 1)
                pool.affine_select(out=keep["mask_k"][:, :], in_=zeros[:, 0:P], compare_op=ALU.is_ge, fill=NEG, base=0,
                                   pattern=[[1, P]], channel_multiplier=-1).then_inc(put, 1)
                pool.iota(none[:, :, 0:1], pattern=[[0, SLOTS]], base=TOKENS, channel_multiplier=1).then_inc(none_ok, 1)
                pool.memset(none[:, :, 1:2], 0).then_inc(none_ok, 1)
                pool.wait_ge(put, 4)
                pool.wait_ge(none_ok, 2)


def build(nc, t):
    t = dict(t)
    for w in ("w1", "wg", "w2"):
        t[w] = t[w].rearrange("e (c p) n -> e p c n", p=P)
    for w in ("ws1", "wsg", "ws2"):
        t[w] = t[w].rearrange("(c p) n -> p c n", p=P)
    t["h0"] = nc.dram_tensor("h0", [TOKENS, D], F32).ap()
    t["xn"] = nc.dram_tensor("xn", [TOKENS + P, D], F32).ap()
    t["table"] = nc.dram_tensor("table", [SLOTS * P, 2], I32).ap()
    with ExitStack() as ctx:
        sb = lambda n, s, d: ctx.enter_context(nc.sbuf_tensor(n, s, d))
        keep = {
            "ident": sb("ident", [P, P], F32), "identb": sb("identb", [P, P], BF16),
            "mask_q": sb("mask_q", [P, P], BF16), "mask_k": sb("mask_k", [P, P], BF16),
        }
        logits = sb("logits", [P, TILES, EXPERTS], F32)
        with ExitStack() as c2:
            sb2 = lambda n, s, d: c2.enter_context(nc.sbuf_tensor(n, s, d))
            keep["cs"] = sb2("cs", [P, 2, TILES * DK], F32)
            keep["qk"] = sb2("qk", [P, 2, TILES, D], F32)
            keep["v"] = sb2("v", [P, TILES, D], F32)
            setup(nc, t, keep)
            phase_a(nc, t, keep)
            phase_b(nc, t, keep)
            phase_c(nc, t, keep, logits)
        plan = {
            "row": sb("plan_row", [P, TOPK, TILES], I32), "pair": sb("plan_pair", [P, TOPK, TILES, 2], I32),
            "run": sb("plan_run", [P, SLOTS], I32), "load": sb("plan_load", [P, SLOTS], I32),
            "next": sb("plan_next", [P, SLOTS], I32), "first": sb("plan_first", [P, 1], I32),
        }
        routing(nc, t, keep, logits, plan)
        W = sb("W", [P, 2, 3, 2, DC, HID], F32R)
        stage = sb("stage", [P, 3, DC * HID], F32)
        experts(nc, t, keep, plan, W, stage, routed=False)
        experts(nc, t, keep, plan, W, stage, routed=True)


def rotations():
    import numpy as np
    theta = np.float32(1) / np.float32(10000) ** (np.arange(0, DK, 2, dtype=np.float32) / np.float32(DK))
    angle = np.arange(SEQ, dtype=np.float32)[:, None] * theta.astype(np.float32)[None, :]
    cos, sin = np.cos(angle), np.sin(angle)
    both = np.stack([np.concatenate([cos, cos], 1), np.concatenate([-sin, sin], 1)])
    both = both.reshape(2, TPB, P, DK).transpose(2, 0, 1, 3).reshape(P, 2, 1, TPB * DK)
    return np.ascontiguousarray(np.broadcast_to(both, (P, 2, BATCH, TPB * DK)).reshape(P, 2, TILES * DK), np.float32)


def kernel(x, L0_tok_emb, L0_tok_W, L0_tok_b, L0_attn_W_qkv, L0_attn_b_qkv, L0_attn_W_out, L0_attn_b_out,
           L0_ffn_W1, L0_ffn_Wg, L0_ffn_W2, L0_ffn_Ws1, L0_ffn_Wsg, L0_ffn_Ws2, L0_ffn_gate_w, L0_ffn_gate_b,
           L0_ffn_biases):
    import numpy as np
    import concourse.bacc as bacc
    from concourse.bass_utils import run_bass_kernel_spmd

    a = np.asarray
    arrays = {
        "ids": a(x).reshape(TILES, P).T,
        "emb": a(L0_tok_emb),
        "tok_w": np.concatenate([a(L0_tok_W), a(L0_tok_b)[None]], 0),
        "qkv_w": a(L0_attn_W_qkv).reshape(HEADS, 3, DK, D).transpose(3, 1, 0, 2).reshape(D, 3 * D),
        "qkv_b": a(L0_attn_b_qkv).reshape(HEADS, 3, DK).transpose(1, 0, 2).reshape(3 * D),
        "out_w": a(L0_attn_W_out).T,
        "out_b": a(L0_attn_b_out),
        "w1": a(L0_ffn_W1), "wg": a(L0_ffn_Wg), "w2": a(L0_ffn_W2),
        "ws1": a(L0_ffn_Ws1), "wsg": a(L0_ffn_Wsg), "ws2": a(L0_ffn_Ws2),
        "gate_w": a(L0_ffn_gate_w), "gate_b": a(L0_ffn_gate_b), "biases": a(L0_ffn_biases),
        "cs": rotations(),
    }
    arrays = {f"in_{k}": np.ascontiguousarray(v) for k, v in arrays.items()}
    nc = bacc.Bacc("TRN2", target_bir_lowering=False, num_devices=1)
    t = {k[3:]: nc.dram_tensor(k, v.shape, mybir.dt.from_np(v.dtype), kind="ExternalInput").ap()
         for k, v in arrays.items()}
    t["out"] = nc.dram_tensor("out", [TOKENS + P, D], F32, kind="ExternalOutput").ap()
    build(nc, t)
    r = run_bass_kernel_spmd(nc, [arrays], core_ids=[0])
    return r.results[0]["out"][:TOKENS].reshape(BATCH, SEQ, D)
```

```python
from contextlib import ExitStack

import concourse.bass as bass
from concourse import mybir

ALU = mybir.AluOpType
ACT = mybir.ActivationFunctionType
AXX = mybir.AxisListType.X
F32 = mybir.dt.float32
F32R = mybir.dt.float32r
BF16 = mybir.dt.bfloat16
I32 = mybir.dt.int32

P = 128
BATCH, SEQ = 2, 1024
TOKENS = BATCH * SEQ
TILES = TOKENS // P
TPB = SEQ // P
D = 512
DC = D // P
EMB = 75
HEADS, DK = 16, 32
HPG = P // DK
GROUPS = HEADS // HPG
UNITS = BATCH * GROUPS
KS = 3 * DK
EXPERTS, TOPK = 7, 3
HID = 512
SLOTS = TOKENS * TOPK // P + EXPERTS - 1
LN_EPS = 1e-5
SCALE = float(DK) ** -0.5
NEG = -1.0e30
HF = DK // 2
QB = 512


class Chain:

    def __init__(self, eng, sem, per_iter, base):
        self.eng, self.sem, self.per_iter, self.base, self.n = eng, sem, per_iter, base, 0

    def inc(self, ins):
        self.n += 1
        return ins.then_inc(self.sem, 1)

    def wait(self):
        self.eng.wait_ge(self.sem, self.base * self.per_iter + self.n)

    def done(self):
        assert self.n == self.per_iter, (self.n, self.per_iter)


def split_load(nc, ctx, sb, sem, name, jobs):
    n = len(jobs)
    SL = min(n, 4)
    stage = sb(name + "_stage", [P, SL, max(hi.shape[1] for _, hi, _ in jobs)], F32)
    landed = [sem(f"{name}_landed{u}") for u in range(SL)]
    high = sem(name + "_high")
    low = sem(name + "_low")

    def st(i):
        rows, cols = jobs[i][1].shape
        return stage[0:rows, i % SL, 0:cols]

    with nc.Block() as block:
        @block.sync
        def _(sp):
            for i, (src, hi, lo) in enumerate(jobs):
                if i >= SL:
                    sp.wait_ge(low, i - SL + 1)
                sp.dma_start(st(i), src).then_inc(landed[i % SL], 16)

        @block.scalar
        def _(act):
            for i, (src, hi, lo) in enumerate(jobs):
                act.wait_ge(landed[i % SL], 16 * (i // SL + 1))
                act.activation(hi, st(i), ACT.Copy).then_inc(high, 1)

        @block.vector
        def _(dve):
            for i, (src, hi, lo) in enumerate(jobs):
                dve.wait_ge(high, i + 1)
                dve.tensor_tensor(lo, st(i), hi.bitcast(F32), ALU.subtract).then_inc(low, 1)


def products(pe, out, terms):
    last = None
    for i, (l, r) in enumerate(terms):
        last = pe.matmul(out, l, r, start=(i == 0), stop=(i == len(terms) - 1))
    return last


def phase_a(nc, t, keep):
    qk, v_all, ident, cs = keep["qk"], keep["v"], keep["ident"], keep["cs"]
    with ExitStack() as ctx:
        sb = lambda n, s, d: ctx.enter_context(nc.sbuf_tensor("a_" + n, s, d))
        sem = lambda n: ctx.enter_context(nc.semaphore("a_" + n))
        ps = [ctx.enter_context(nc.psum_tensor(f"a_ps{i}", [P, 512], F32)) for i in range(8)]
        wh = sb("wh", [P, DC, 3 * D], F32R)
        wl = sb("wl", [P, DC, 3 * D], F32R)
        th = sb("th", [EMB + 1, D], F32R)
        tl = sb("tl", [EMB + 1, D], F32R)
        with ExitStack() as c2:
            sb2 = lambda n, s, d: c2.enter_context(nc.sbuf_tensor("a_" + n, s, d))
            jobs = [(t["tok_w"], th[0:EMB + 1, :], tl[0:EMB + 1, :])]
            jobs += [(t["qkv_w"][c * P:(c + 1) * P, :], wh[:, c, :], wl[:, c, :]) for c in range(DC)]
            split_load(nc, c2, sb2, lambda n: c2.enter_context(nc.semaphore("a_" + n)), "w", jobs)
        ids = sb("ids", [P, TILES], I32)
        row_ids = sb("row_ids", [P, 2, 1], I32)
        bias = sb("bias", [P, 3 * D], F32)
        rows = sb("rows", [P, 2, EMB + 1], F32)
        rth = sb("rth", [EMB + 1, P], F32R)
        rtl = sb("rtl", [EMB + 1, P], F32R)
        h = sb("h", [P, 2, D], F32)
        stats = sb("stats", [P, 6], F32)
        mv = sb("mv", [P, 2], F32)
        eps = sb("eps", [P, 1], F32)
        rstd = sb("rstd", [P, 1], F32)
        nhalf = sb("nhalf", [P, 1], F32)
        xn = sb("xn", [P, D], F32)
        xh = sb("xh", [P, 2, D], F32R)
        xl = sb("xl", [P, 2, D], F32R)
        qb = sb("qb", [P, 2, D], F32)
        ra = sb("ra", [P, 2, D], F32)
        rb = sb("rb", [P, 2, D], F32)

        held = sem("held")
        const_in = sem("const_in")
        const_set = sem("const_set")
        ids_ok = sem("ids_ok")
        gathered = [sem(f"gathered{u}") for u in range(2)]
        rows_t = sem("rows_t")
        rth_ok = sem("rth_ok")
        rtl_ok = sem("rtl_ok")
        h_ps = sem("h_ps")
        h_ok = sem("h_ok")
        h_out = [sem(f"h_out{u}") for u in range(2)]
        var_ok = sem("var_ok")
        rstd_ok = sem("rstd_ok")
        xn_ok = sem("xn_ok")
        xt_ps = sem("xt_ps")
        xh_ok = sem("xh_ok")
        xl_ok = sem("xl_ok")
        proj = sem("proj")
        biased = sem("biased")
        v_ok = sem("v_ok")
        turned = sem("turned")
        roped = sem("roped")
        dch = sem("dch")
        PEEL = 4

        def steps(eng, body):
            with eng.Fori(0, (TILES - PEEL) // 2) as i:
                for u in range(2):
                    body(i * 2 + u, u, TILES)
            for n in range(TILES - PEEL, TILES):
                body(n, n % 2, TILES - n)

        def uses(n, u):
            return (n - u) // 2 + 1

        with nc.Block() as block:
            @block.sync
            def _(sp):
                sp.dma_start(ids[:, :], t["ids"]).then_inc(const_in, 16)
                sp.dma_start(bias[:, :], t["qkv_b"].partition_broadcast(P)).then_inc(const_in, 16)
                for u in range(2):
                    sp.nop().then_inc(h_out[u], 16)

                def store(n, u, left):
                    sp.wait_ge(h_ok, n + 1)
                    sp.dma_start(t["h0"][bass.ds(n * P, P), :], h[:, u, :]).then_inc(h_out[u], 16)
                steps(sp, store)
                for u in range(2):
                    sp.wait_ge(h_out[u], 8 * TILES + 16)

            @block.gpsimd
            def _(pool):
                def gather(n, u):
                    pool.tensor_copy(row_ids[:, u, :], ids[:, bass.ds(n, 1)]).then_inc(ids_ok, 1)
                    pool.wait_ge(ids_ok, n + 1)
                    pool.nop().then_inc(held, 1)
                    pool.indirect_dma_start(out=rows[:, u, 0:EMB], out_offset=None, in_=t["emb"],
                                            in_offset=bass.IndirectOffsetOnAxis(ap=row_ids[:, u, :], axis=0)
                                            ).then_inc(gathered[u], 16)

                def root(n):
                    pool.wait_ge(var_ok, n + 1)
                    pool.tensor_tensor(rstd[:, :], mv[:, 1:2], nhalf[:, :], ALU.pow).then_inc(rstd_ok, 1)

                pool.nop().then_inc(roped, 2)
                pool.memset(rows[:, :, :], 1.0).then_inc(const_set, 1)
                pool.memset(eps[:, :], LN_EPS).then_inc(const_set, 1)
                pool.memset(nhalf[:, :], -0.5).then_inc(const_set, 1)
                pool.wait_ge(const_set, 3)
                pool.wait_ge(const_in, 32)
                gather(0, 0)
                gather(1, 1)
                pool.wait_ge(rows_t, 1)
                gather(2, 0)
                root(0)

                def body(n, u, left):
                    if left > 3:
                        pool.wait_ge(rows_t, n + 2)
                        gather(n + 3, 1 - u)
                    if left > 1:
                        root(n + 1)
                    for j in range(2):
                        pool.wait_ge(turned, n * 4 + 2 * j + 2)
                        pool.tensor_tensor(qk[:, j, bass.ds(n, 1), :].rearrange("p a d -> p (a d)"),
                                           ra[:, j, :], rb[:, j, :], ALU.add).then_inc(roped, 1)
                steps(pool, body)
                pool.wait_ge(roped, 2 * TILES + 2)

            @block.tensor
            def _(pe):
                def turn_rows(n, u):
                    pe.wait_ge(gathered[u], uses(n, u) * 16)
                    pe.transpose(ps[0][0:EMB + 1, 0:P], rows[:, u, :], ident[:, :]).then_inc(rows_t, 1)

                def embed(n, u):
                    pe.wait_ge(rtl_ok, n + 1)
                    products(pe, ps[1][:, :], [(rth[:, :], th[:, :]), (rth[:, :], tl[:, :]), (rtl[:, :], th[:, :])]
                             ).then_inc(h_ps, 1)

                def turn_x(n):
                    pe.wait_ge(xn_ok, n + 1)
                    for c in range(DC):
                        mm = pe.transpose(ps[2][:, c * P:(c + 1) * P], xn[:, c * P:(c + 1) * P], ident[:, :])
                    mm.then_inc(xt_ps, 1)

                def project(n, u, j):
                    products(pe, ps[3 + j][:, :],
                             [(a[:, u, c * P:(c + 1) * P], w[:, c, j * D:(j + 1) * D])
                              for c in range(DC) for a, w in ((xh, wh), (xh, wl), (xl, wh))]).then_inc(proj, 1)

                turn_rows(0, 0)
                embed(0, 0)
                turn_rows(1, 1)
                turn_x(0)

                def body(n, u, left):
                    if left > 1:
                        pe.wait_ge(h_ok, n + 1)
                        embed(n + 1, 1 - u)
                    if left > 2:
                        turn_rows(n + 2, u)
                    pe.wait_ge(xl_ok, n + 1)
                    pe.wait_ge(biased, n * 2 + 1)
                    project(n, u, 0)
                    if left > 1:
                        turn_x(n + 1)
                    pe.wait_ge(biased, n * 2 + 2)
                    project(n, u, 1)
                    pe.wait_ge(v_ok, n + 1)
                    project(n, u, 2)
                steps(pe, body)

            @block.scalar
            def _(act):
                def rows_high(n):
                    act.wait_ge(rows_t, n + 1)
                    act.activation(rth[:, :], ps[0][0:EMB + 1, 0:P], ACT.Copy).then_inc(rth_ok, 1)

                def scale_h(n, u):
                    act.wait_ge(h_ps, n + 1)
                    act.wait_ge(h_out[u], uses(n, u) * 16)
                    act.activation(h[:, u, :], ps[1][:, :], ACT.Copy, scale=float(D) ** 0.5).then_inc(h_ok, 1)

                def x_high(n, u):
                    act.wait_ge(xt_ps, n + 1)
                    act.activation(xh[:, u, :], ps[2][:, :], ACT.Copy).then_inc(xh_ok, 1)

                rows_high(0)
                scale_h(0, 0)
                rows_high(1)
                x_high(0, 0)

                def body(n, u, left):
                    if left > 1:
                        scale_h(n + 1, 1 - u)
                    if left > 2:
                        rows_high(n + 2)
                    if left > 1:
                        x_high(n + 1, 1 - u)
                steps(act, body)

            @block.vector
            def _(dve):
                def rows_low(n):
                    dve.wait_ge(rth_ok, n + 1)
                    dve.tensor_tensor(rtl[:, :], ps[0][0:EMB + 1, 0:P], rth[:, :].bitcast(F32), ALU.subtract
                                      ).then_inc(rtl_ok, 1)

                def normalise(n, u):
                    ch = Chain(dve, dch, 2, n)
                    dve.wait_ge(h_ok, n + 1)
                    ch.inc(dve.bn_stats(stats[:, :], h[:, u, :]))
                    ch.wait()
                    dve.nop().then_inc(held, 1)
                    ch.inc(dve.bn_aggr(mv[:, :], stats[:, :]))
                    ch.wait()
                    ch.done()
                    dve.tensor_scalar(mv[:, 1:2], mv[:, 1:2], eps[:, 0:1], None, ALU.add).then_inc(var_ok, 1)
                    dve.wait_ge(rstd_ok, n + 1)
                    dve.tensor_scalar(xn[:, :], h[:, u, :], mv[:, 0:1], rstd[:, 0:1], ALU.subtract, ALU.mult
                                      ).then_inc(xn_ok, 1)

                def x_low(n, u):
                    dve.wait_ge(xh_ok, n + 1)
                    dve.tensor_tensor(xl[:, u, :], ps[2][:, :], xh[:, u, :].bitcast(F32), ALU.subtract
                                      ).then_inc(xl_ok, 1)

                def rotate(n, j):
                    dve.wait_ge(proj, n * 3 + j + 1)
                    dve.tensor_tensor(qb[:, j, :], ps[3 + j][:, :], bias[:, j * D:(j + 1) * D], ALU.add
                                      ).then_inc(biased, 1)
                    dve.wait_ge(biased, n * 2 + j + 3)
                    dve.wait_ge(roped, n * 2 + j + 1)
                    src = qb[:, j, :].rearrange("p (a d) -> p a d", a=HEADS)
                    cos = cs[:, 0, bass.ds(n * DK, DK)]
                    dve.tensor_tensor(ra[:, j, :].rearrange("p (a d) -> p a d", a=HEADS), src,
                                      cos.unsqueeze(1).broadcast_to([P, HEADS, DK]), ALU.mult).then_inc(turned, 1)
                    dst = rb[:, j, :].rearrange("p (a d) -> p a d", a=HEADS)
                    for k in range(2):
                        sin = cs[:, 1, bass.ds(n * DK + k * HF, HF)]
                        ins = dve.tensor_tensor(dst[:, :, k * HF:(k + 1) * HF], src[:, :, (1 - k) * HF:(2 - k) * HF],
                                                sin.unsqueeze(1).broadcast_to([P, HEADS, HF]), ALU.mult)
                    ins.then_inc(turned, 1)

                dve.nop().then_inc(biased, 2)
                dve.nop().then_inc(v_ok, 1)
                dve.wait_ge(const_in, 32)
                dve.wait_ge(const_set, 3)
                rows_low(0)
                normalise(0, 0)
                rows_low(1)
                x_low(0, 0)

                def body(n, u, left):
                    if left > 1:
                        normalise(n + 1, 1 - u)
                    if left > 2:
                        rows_low(n + 2)
                    rotate(n, 0)
                    if left > 1:
                        x_low(n + 1, 1 - u)
                    rotate(n, 1)
                    dve.wait_ge(proj, n * 3 + 3)
                    dve.tensor_tensor(v_all[:, bass.ds(n, 1), :].rearrange("p a d -> p (a d)"),
                                      ps[5][:, :], bias[:, 2 * D:3 * D], ALU.add).then_inc(v_ok, 1)
                steps(dve, body)
                dve.wait_ge(v_ok, TILES + 1)


def phase_b(nc, t, keep):
    qk, v_all, ident, identb = keep["qk"], keep["v"], keep["ident"], keep["identb"]
    with ExitStack() as ctx:
        sb = lambda n, s, d: ctx.enter_context(nc.sbuf_tensor("b_" + n, s, d))
        sem = lambda n: ctx.enter_context(nc.semaphore("b_" + n))
        bank = lambda n: ctx.enter_context(nc.psum_tensor("b_" + n, [P, QB], F32))
        sc_t = [bank(f"sc_t{i}") for i in range(2)]
        RING = 4
        ring = [bank(f"ring{i}") for i in range(RING)]
        acc = [bank("acc_v"), bank("acc_1")]
        q3 = sb("q3", [P, 2, HPG, KS], F32R)
        k3 = sb("k3", [P, 2, HPG, KS], F32R)
        q3t = sb("q3t", [KS + 1, BATCH, HPG, SEQ], F32R)
        k3t = sb("k3t", [KS + 1, BATCH, HPG, SEQ], F32R)
        vu = sb("vu", [P, BATCH, TPB, P], F32)
        ones = sb("ones", [P, DK], F32)
        SPB = QB // P
        mx = sb("mx", [P, HPG, TPB], F32)
        mx2 = sb("mx2", [P, 2, HPG, TPB - SPB], F32)
        mxt = sb("mxt", [HPG * TPB, P], F32R)
        e = sb("e", [P, 2 * HPG, QB], F32)
        pvs = sb("pvs", [P, QB], F32)
        sums = sb("sums", [P, QB], F32)
        rec = sb("rec", [P, QB], F32)

        set_ = sem("set")
        high = sem("high")
        low = sem("low")
        turned = sem("turned")
        t_in = sem("t_in")
        v_in = sem("v_in")
        smax = sem("smax")
        mx_ok = sem("mx_ok")
        mx_all = sem("mx_all")
        mxt_ps = sem("mxt_ps")
        mxt_ok = sem("mxt_ok")
        row_in = sem("row_in")
        st = sem("st")
        ex = sem("ex")
        pv = sem("pv")
        pv_out = sem("pv_out")
        sum_out = sem("sum_out")
        rec_ok = sem("rec_ok")
        norm = sem("norm")

        blocks = [(Q, kt) for Q in range(SEQ // QB) for kt in range((Q + 1) * SPB)]
        NB = len(blocks)
        NQ = SEQ // QB
        NH = HPG * NB
        RECS = 8
        pieces = [(qt, h, s) for qt in range(TPB) for h in range(HPG) for s in range(0, (qt + 1) * P, QB)]
        NM = len(pieces)

        def offset(i):
            Q, kt = blocks[i]
            return max(0, kt * P - Q * QB)

        def prepare():
            out = [(1.0, ("turn", 0))]
            for qt in range(TPB):
                if qt + 1 < TPB:
                    out.append((1.0, ("turn", qt + 1)))
                for p, (t_, h, s) in enumerate(pieces):
                    if t_ == qt:
                        out.append((0.1 + min(QB, (qt + 1) * P - s) * 1.05e-3, ("score", p)))
            return out + [(0.0, ("maxima", 0))]

        def attend(with_next, with_split):
            FROM, TO = 0.02, 0.93
            ready = prepare() if with_next else []
            total = sum(c for c, _ in ready)
            work = sum(QB - offset(i) for i in range(NB))
            plan, done, at, parts = [], 0.0, 0.0, []
            for i in range(NB):
                for h in range(HPG):
                    plan.append(("score_t", i * HPG + h))
                    at += (QB - offset(i)) / HPG / work
                    while ready and done + ready[0][0] <= total * (at - FROM) / (TO - FROM) + 1e-6:
                        c, s = ready.pop(0)
                        done += c
                        plan.append(s)
                    if h == 1 and i > 0:
                        plan.append(("weigh", i - 1))
                        if blocks[i][1] == 0:
                            parts = [("norm", (blocks[i - 1][0], r)) for r in range(RECS)]
                    elif parts:
                        plan.append(parts.pop(0))
            assert not ready
            if with_split:
                plan += [("split", 0)]
            plan += parts + [("weigh", NB - 1)] + [("norm", (NQ - 1, r)) for r in range(RECS)]
            return plan

        users = []
        for _, (kind, what) in prepare():
            users += [("turn", 2 * what), ("turn", 2 * what + 1)] if kind == "turn" else [(kind, what)]

        def ring_bank(user):
            return ring[users.index(user) % RING]

        def units(eng, begin, step):
            def unit(now, after, later):
                if begin and after:
                    begin(*after)
                for kind, what in attend(after is not None, later is not None):
                    step(kind, what, *(later if kind == "split" else
                                       now if kind in ("score_t", "weigh", "norm") else after))

            if begin:
                begin(0, 0, 0)
            step("split", 0, 0, 0, 0)
            for _, (kind, what) in prepare():
                step(kind, what, 0, 0, 0)
            step("split", 0, 1, 1, 0)
            with eng.Fori(0, GROUPS - 1) as g:
                unit((g * 2, 0, g), (g * 2 + 1, 1, g), (g * 2 + 2, 0, g + 1))
                unit((g * 2 + 1, 1, g), (g * 2 + 2, 0, g + 1), (g * 2 + 3, 1, g + 1))
            g = GROUPS - 1
            unit((g * 2, 0, g), (g * 2 + 1, 1, g), None)
            unit((g * 2 + 1, 1, g), None, None)

        def chunk(j, b, g, k):
            a = qk[:, j, b * TPB + k, bass.ds(g * P, P)]
            return a.rearrange("p (h d) -> p h d", h=HPG)

        assert BATCH == 2

        with nc.Block() as block:
            @block.sync
            def _(sp):
                def step(kind, what, n, b, g):
                    if kind == "maxima":
                        sp.wait_ge(mxt_ok, n + 2)
                        sp.dma_start(q3t[KS:KS + 1, b, :, :].rearrange("o h (k q) -> o (h k) q", q=P).bitcast(F32),
                                     mxt[:, :].bitcast(F32)).then_inc(row_in, 16)
                units(sp, None, step)
                sp.wait_ge(row_in, 16 * UNITS)

            @block.gpsimd
            def _(pool):
                pool.memset(ones[:, :], 1.0).then_inc(set_, 1)
                pool.wait_ge(set_, 1)
                pool.nop().then_inc(norm, 1)

                def values(n, b, g):
                    if not (isinstance(n, int) and n == 0):
                        pool.wait_ge(pv, n * NB)
                    pool.tensor_copy(vu[:, b, :, :], v_all[:, b * TPB:(b + 1) * TPB, bass.ds(g * P, P)]).then_inc(v_in, 1)

                def step(kind, what, n, b, g):
                    if kind == "norm" and what[1] == RECS - 1:
                        Q = what[0]
                        pool.wait_ge(rec_ok, (n * NQ + Q + 2) * RECS)
                        pool.wait_ge(pv_out, n * NQ + Q + 2)
                        pool.tensor_tensor(qk[:, 0, b * TPB + Q * SPB:b * TPB + (Q + 1) * SPB, bass.ds(g * P, P)],
                                           pvs[:, :].rearrange("p (a q) -> p a q", q=P),
                                           rec[:, :].rearrange("p (a q) -> p a q", q=P), ALU.mult).then_inc(norm, 1)
                    elif kind == "split" and what == 0 and isinstance(n, int) and n == 0:
                        pool.wait_ge(v_in, 1)
                        pool.memset(k3t[KS:KS + 1, :, :, :].bitcast(F32), 1.0).then_inc(set_, 1)
                        pool.wait_ge(set_, 2)
                units(pool, values, step)
                pool.wait_ge(norm, UNITS * NQ + 1)

            @block.tensor
            def _(pe):
                pe.nop().then_inc(turned, 4)
                pe.nop().then_inc(pv, NB)

                def free(n, user):
                    at = users.index(user)
                    own = at >= RING
                    kind, i = users[at - RING] if own else users[(len(users) - 1 - at) // RING * RING + at]
                    done_, per = {"turn": (t_in, 2 * TPB), "score": (mx_ok, NM), "maxima": (mxt_ok, 1)}[kind]
                    pe.wait_ge(done_, n * per + per * own + i + 1)

                def turn(n, b, k):
                    for j, src in enumerate((q3, k3)):
                        user = ("turn", 2 * k + j)
                        pe.wait_ge(low, n * 2 * TPB + 2 * k + j + 1)
                        free(n, user)
                        for h in range(HPG):
                            mm = pe.transpose(ring_bank(user)[0:KS, h * P:(h + 1) * P],
                                              src[:, k % 2, h, :].bitcast(F32), ident[:, :])
                        mm.then_inc(turned, 1)

                def score(n, b, p):
                    qt, h, s = pieces[p]
                    out = ring_bank(("score", p))
                    if h == 0 and s == 0:
                        pe.wait_ge(t_in, n * 2 * TPB + 2 * TPB + 2 * qt + 2)
                    free(n, ("score", p))
                    w = min(QB, (qt + 1) * P - s)
                    diag = s + w == (qt + 1) * P
                    mm = pe.matmul(out[:, 0:w], q3t[0:KS, b, h, qt * P:(qt + 1) * P], k3t[0:KS, b, h, s:s + w],
                                   start=True, stop=not diag)
                    if diag:
                        mm = pe.matmul(out[:, w - P:w], identb[:, :], keep["mask_q"][:, :], start=False, stop=True)
                    mm.then_inc(smax, 1)

                def maxima(n, b):
                    pe.wait_ge(mx_all, n + 1)
                    free(n, ("maxima", 0))
                    pe.transpose(ring_bank(("maxima", 0))[0:HPG * TPB, 0:P], mx[:, :, :].rearrange("p h k -> p (h k)"),
                                 ident[:, :]).then_inc(mxt_ps, 1)

                def score_t(n, b, j):
                    i, h = divmod(j, HPG)
                    (Q, kt), off = blocks[i], offset(i)
                    if j == 0:
                        pe.wait_ge(set_, 2)
                        pe.wait_ge(row_in, n * 16 + 16)
                    pe.wait_ge(ex, n * NH + j + 1)
                    diag = kt * P >= Q * QB
                    mm = pe.matmul(sc_t[j % 2][:, 0:QB - off], k3t[:, b, h, kt * P:(kt + 1) * P],
                                   q3t[:, b, h, Q * QB + off:(Q + 1) * QB], start=True, stop=not diag)
                    if diag:
                        mm = pe.matmul(sc_t[j % 2][:, 0:P], identb[:, :], keep["mask_k"][:, :], start=False, stop=True)
                    mm.then_inc(st, 1)

                def weigh(n, b, i):
                    (Q, kt), off = blocks[i], offset(i)
                    if i == 0:
                        pe.wait_ge(v_in, n + 1)
                    if kt == 0:
                        pe.wait_ge(pv_out, n * NQ + Q + 1)
                        pe.wait_ge(sum_out, n * NQ + Q + 1)
                    pe.wait_ge(ex, n * NH + (i + 1) * HPG + 2)
                    ends = kt == (Q + 1) * SPB - 1
                    for which in range(2):
                        for h in range(HPG):
                            lhs = vu[:, b, kt, h * DK:(h + 1) * DK] if which == 0 else ones[:, :]
                            mm = pe.matmul(acc[which][h * DK:(h + 1) * DK, off:QB], lhs,
                                           e[:, (HPG * i + h) % (2 * HPG), 0:QB - off], start=(kt == 0), stop=ends)
                    mm.then_inc(pv, 1)

                def step(kind, what, n, b, g):
                    if kind == "turn":
                        turn(n, b, what)
                    elif kind == "score":
                        score(n, b, what)
                    elif kind == "maxima":
                        maxima(n, b)
                    elif kind == "score_t":
                        score_t(n, b, what)
                    elif kind == "weigh":
                        weigh(n, b, what)
                units(pe, None, step)

            @block.scalar
            def _(act):
                act.nop().then_inc(t_in, 2 * TPB)
                act.nop().then_inc(ex, 2)
                act.nop().then_inc(mxt_ok, 1)
                act.nop().then_inc(pv_out, 1)

                def highs(n, b, g, k):
                    act.wait_ge(turned, n * 2 * TPB + 2 * k + 2)
                    for j, (dst, at) in enumerate(((q3, slice(0, 2 * DK)), (k3, slice(0, KS)))):
                        out = dst[:, k % 2, :, at].rearrange("p h (r d) -> p h r d", d=DK)
                        out = out if j == 0 else out[:, :, 0:3:2, :]
                        act.activation(out, chunk(j, b, g, k).unsqueeze(2).broadcast_to([P, HPG, 2, DK]), ACT.Copy
                                       ).then_inc(high, 1)

                def step(kind, what, n, b, g):
                    if kind == "turn":
                        k = what
                        for j, dst in enumerate((q3t, k3t)):
                            act.wait_ge(turned, n * 2 * TPB + 2 * k + j + 1 + 4)
                            act.activation(dst[0:KS, b, :, k * P:(k + 1) * P], ring_bank(("turn", 2 * k + j))[0:KS, :]
                                           .rearrange("p (h q) -> p h q", h=HPG), ACT.Copy).then_inc(t_in, 1)
                        if k + 2 < TPB:
                            highs(n, b, g, k + 2)
                    elif kind == "split":
                        highs(n, b, g, 0)
                        highs(n, b, g, 1)
                    elif kind == "maxima":
                        act.wait_ge(mxt_ps, n + 1)
                        act.activation(mxt[:, :], ring_bank(("maxima", 0))[0:HPG * TPB, 0:P], ACT.Copy, scale=-1.0).then_inc(mxt_ok, 1)
                    elif kind == "score_t":
                        j = what
                        w = QB - offset(j // HPG)
                        act.wait_ge(st, n * NH + j + 1)
                        if j % HPG == 0:
                            act.wait_ge(pv, n * NB + NB + j // HPG - 1)
                        act.activation(e[:, j % (2 * HPG), 0:w], sc_t[j % 2][:, 0:w], ACT.Exp, scale=SCALE
                                       ).then_inc(ex, 1)
                    elif kind == "weigh" and (what == NB - 1 or blocks[what + 1][1] == 0):
                        Q = blocks[what][0]
                        act.wait_ge(pv, n * NB + NB + what + 1)
                        act.wait_ge(norm, n * NQ + Q + 1)
                        act.activation(pvs[:, :], acc[0][:, :], ACT.Copy).then_inc(pv_out, 1)
                units(act, None, step)

            @block.vector
            def _(dve):
                dve.nop().then_inc(mx_ok, NM)
                dve.nop().then_inc(sum_out, 1)
                dve.nop().then_inc(rec_ok, RECS)

                def lows(n, b, g, k):
                    for j, (dst, hi, lo) in enumerate(((q3, 0, 2), (k3, 0, 1))):
                        dve.wait_ge(high, n * 2 * TPB + 2 * k + j + 1)
                        dve.tensor_tensor(dst[:, k % 2, :, lo * DK:(lo + 1) * DK], chunk(j, b, g, k),
                                          dst[:, k % 2, :, hi * DK:(hi + 1) * DK].bitcast(F32), ALU.subtract
                                          ).then_inc(low, 1)

                def step(kind, what, n, b, g):
                    if kind == "turn" and what + 2 < TPB:
                        lows(n, b, g, what + 2)
                    elif kind == "split":
                        lows(n, b, g, 0)
                        lows(n, b, g, 1)
                    elif kind == "score":
                        qt, h, s = pieces[what]
                        dve.wait_ge(smax, n * NM + what + 1)
                        if what == 0 and not (isinstance(n, int) and n == 0):
                            dve.wait_ge(mxt_ps, n)
                        w = min(QB, (qt + 1) * P - s)
                        out = mx[:, h, qt:qt + 1] if qt < SPB else mx2[:, s // QB, h, qt - SPB:qt - SPB + 1]
                        dve.tensor_reduce(out, ring_bank(("score", what))[:, 0:w], AXX, ALU.max).then_inc(mx_ok, 1)
                    elif kind == "maxima":
                        dve.wait_ge(mx_ok, n * NM + 2 * NM)
                        dve.tensor_tensor(mx[:, :, SPB:], mx2[:, 0, :, :], mx2[:, 1, :, :], ALU.max).then_inc(mx_all, 1)
                    elif kind == "weigh" and (what == NB - 1 or blocks[what + 1][1] == 0):
                        Q = blocks[what][0]
                        dve.wait_ge(pv, n * NB + NB + what + 1)
                        dve.wait_ge(rec_ok, (n * NQ + Q + 1) * RECS)
                        dve.tensor_copy(sums[:, :], acc[1][:, :]).then_inc(sum_out, 1)
                    elif kind == "norm":
                        Q, r = what
                        w = QB // RECS
                        if r == 0:
                            dve.wait_ge(sum_out, n * NQ + Q + 2)
                            dve.wait_ge(norm, n * NQ + Q + 1)
                        dve.reciprocal(rec[:, r * w:(r + 1) * w], sums[:, r * w:(r + 1) * w]).then_inc(rec_ok, 1)
                units(dve, None, step)


def phase_c(nc, t, keep, logits):
    qk, ident = keep["qk"], keep["ident"]
    with ExitStack() as ctx:
        sb = lambda n, s, d: ctx.enter_context(nc.sbuf_tensor("c_" + n, s, d))
        sem = lambda n: ctx.enter_context(nc.semaphore("c_" + n))
        pair = lambda n: [ctx.enter_context(nc.psum_tensor(f"c_{n}{u}", [P, D], F32)) for u in range(2)]
        ps_o, ps_x, ps_g = pair("ps_o"), pair("ps_x"), pair("ps_g")
        wh = sb("wh", [P, DC, D], F32R)
        wl = sb("wl", [P, DC, D], F32R)
        with ExitStack() as c2:
            split_load(nc, c2, lambda n, s, d: c2.enter_context(nc.sbuf_tensor("c_" + n, s, d)),
                       lambda n: c2.enter_context(nc.semaphore("c_" + n)), "w",
                       [(t["out_w"][c * P:(c + 1) * P, :], wh[:, c, :], wl[:, c, :]) for c in range(DC)])
        gw = sb("gw", [P, DC, EXPERTS], F32)
        gb = sb("gb", [P, EXPERTS], F32)
        ob = sb("ob", [P, D], F32)
        hin = sb("hin", [P, 2, D], F32)
        hb = sb("hb", [P, 2, D], F32)
        ah = sb("ah", [P, 2, D], F32R)
        al = sb("al", [P, 2, D], F32R)
        h = sb("h", [P, 2, D], F32)
        xn = sb("xn", [P, 2, D], F32)
        xt = sb("xt", [P, 2, D], F32)
        stats = sb("stats", [P, 2, 6], F32)
        mv = sb("mv", [P, 2, 2], F32)
        rstd = sb("rstd", [P, 2, 1], F32)
        nhalf = sb("nhalf", [P, 1], F32)

        FREE = 2
        held = sem("held")
        const_in = sem("const_in")
        const_set = sem("const_set")
        h_in = [sem(f"h_in{u}") for u in range(2)]
        hb_ok = sem("hb_ok")
        ah_ok = sem("ah_ok")
        al_ok = sem("al_ok")
        proj = sem("proj")
        h_ok = sem("h_ok")
        h_out = [sem(f"h_out{u}") for u in range(2)]
        x_out = [sem(f"x_out{u}") for u in range(2)]
        stat_ok = sem("stat_ok")
        aggr_ok = sem("aggr_ok")
        var_ok = sem("var_ok")
        rstd_ok = sem("rstd_ok")
        xn_ok = sem("xn_ok")
        xt_ps = sem("xt_ps")
        xt_ok = sem("xt_ok")
        gate = sem("gate")
        gate_ok = sem("gate_ok")

        def steps(eng, *stages):
            FIRST, LOOP, END = -4, 1, TILES + 1
            count = (TILES - 4 - LOOP) // 2

            def one(n):
                for f, lead in stages:
                    if 0 <= n + lead < TILES:
                        f(n + lead, (n + lead) % 2)
            for n in range(FIRST, LOOP):
                one(n)
            with eng.Fori(0, count) as i:
                for u in range(2):
                    for f, lead in stages:
                        f(i * 2 + (LOOP + u + lead), (LOOP + u + lead) % 2)
            for n in range(LOOP + 2 * count, END):
                one(n)

        def uses(m, u):
            return (m - u) // 2 + 1

        with nc.Block() as block:
            @block.sync
            def _(sp):
                sp.dma_start(gw[:, :, :], t["gate_w"].rearrange("(c p) e -> p c e", p=P)).then_inc(const_in, 16)
                sp.dma_start(gb[:, :], t["gate_b"].partition_broadcast(P)).then_inc(const_in, 16)
                sp.dma_start(ob[:, :], t["out_b"].partition_broadcast(P)).then_inc(const_in, 16)
                for u in range(2):
                    sp.nop().then_inc(h_out[u], 16)
                    sp.nop().then_inc(x_out[u], 16)

                def load(m, u):
                    if not isinstance(m, int) or m >= 2:
                        sp.wait_ge(hb_ok, m - 1)
                    sp.dma_start(hin[:, u, :], t["h0"][bass.ds(m * P, P), :]).then_inc(h_in[u], 16)

                def store_h(m, u):
                    sp.wait_ge(h_ok, m + 1 + FREE)
                    sp.dma_start(t["out"][bass.ds(m * P, P), :], h[:, u, :]).then_inc(h_out[u], 16)

                def store_x(m, u):
                    sp.wait_ge(xn_ok, m + 1 + FREE)
                    sp.dma_start(t["xn"][bass.ds(m * P, P), :], xn[:, u, :]).then_inc(x_out[u], 16)

                steps(sp, (load, 4), (store_h, 1), (store_x, 0))
                for u in range(2):
                    sp.wait_ge(h_out[u], 8 * TILES + 16)
                    sp.wait_ge(x_out[u], 8 * TILES + 16)

            @block.gpsimd
            def _(pool):
                pool.memset(nhalf[:, :], -0.5).then_inc(const_set, 1)
                pool.wait_ge(const_set, 1)
                pool.wait_ge(const_in, 48)

                def bias(m, u):
                    pool.wait_ge(h_in[u], uses(m, u) * 16)
                    pool.wait_ge(h_ok, m + 1)
                    pool.tensor_tensor(hb[:, u, :], hin[:, u, :], ob[:, :], ALU.add).then_inc(hb_ok, 1)

                def root(m, u):
                    pool.wait_ge(var_ok, m + 1)
                    pool.tensor_tensor(rstd[:, u, :], mv[:, u, 1:2], nhalf[:, :], ALU.pow).then_inc(rstd_ok, 1)

                steps(pool, (bias, 2), (root, 1))

            @block.tensor
            def _(pe):
                pe.wait_ge(const_in, 48)
                for s in (proj, xt_ps, gate):
                    pe.nop().then_inc(s, FREE)

                def project(m, u):
                    pe.wait_ge(al_ok, m + 1)
                    pe.wait_ge(h_ok, m + 1)
                    products(pe, ps_o[u][:, :], [(a[:, u, c * P:(c + 1) * P], w[:, c, :])
                                                 for c in range(DC) for a, w in ((ah, wh), (ah, wl), (al, wh))]
                             ).then_inc(proj, 1)

                def turn(m, u):
                    pe.wait_ge(xn_ok, m + 1 + FREE)
                    pe.wait_ge(xt_ok, m + 1)
                    for c in range(DC):
                        mm = pe.transpose(ps_x[u][:, c * P:(c + 1) * P], xn[:, u, c * P:(c + 1) * P], ident[:, :])
                    mm.then_inc(xt_ps, 1)

                def weigh(m, u):
                    pe.wait_ge(xt_ok, m + 1 + FREE)
                    pe.wait_ge(gate_ok, m + 1)
                    products(pe, ps_g[u][:, 0:EXPERTS], [(xt[:, u, c * P:(c + 1) * P], gw[:, c, :]) for c in range(DC)]
                             ).then_inc(gate, 1)

                steps(pe, (project, 2), (weigh, -1), (turn, 0))

            @block.scalar
            def _(act):
                act.nop().then_inc(xt_ok, FREE)

                def high(m, u):
                    act.wait_ge(proj, m + 1)
                    act.activation(ah[:, u, :], qk[:, 0, bass.ds(m, 1), :].rearrange("p a d -> p (a d)"), ACT.Copy
                                   ).then_inc(ah_ok, 1)

                def out(m, u):
                    act.wait_ge(xt_ps, m + 1 + FREE)
                    act.wait_ge(gate, m + 1)
                    act.activation(xt[:, u, :], ps_x[u][:, :], ACT.Copy).then_inc(xt_ok, 1)

                steps(act, (high, 3), (out, 0))

            @block.vector
            def _(dve):
                for s in (h_ok, xn_ok, gate_ok):
                    dve.nop().then_inc(s, FREE)
                dve.wait_ge(const_in, 48)

                def low(m, u):
                    dve.wait_ge(ah_ok, m + 1)
                    dve.tensor_tensor(al[:, u, :], qk[:, 0, bass.ds(m, 1), :].rearrange("p a d -> p (a d)"),
                                      ah[:, u, :].bitcast(F32), ALU.subtract).then_inc(al_ok, 1)

                def add(m, u):
                    dve.wait_ge(proj, m + 1 + FREE)
                    dve.wait_ge(hb_ok, m + 1)
                    dve.wait_ge(h_out[u], uses(m, u) * 16)
                    dve.wait_ge(xn_ok, m + 1)
                    dve.tensor_tensor(h[:, u, :], ps_o[u][:, :], hb[:, u, :], ALU.add).then_inc(h_ok, 1)
                    dve.wait_ge(h_ok, m + 1 + FREE)
                    dve.bn_stats(stats[:, u, :], h[:, u, :]).then_inc(stat_ok, 1)
                    dve.wait_ge(stat_ok, m + 1)
                    dve.nop().then_inc(held, 1)
                    dve.bn_aggr(mv[:, u, :], stats[:, u, :]).then_inc(aggr_ok, 1)
                    dve.wait_ge(aggr_ok, m + 1)
                    dve.tensor_scalar(mv[:, u, 1:2], mv[:, u, 1:2], LN_EPS, None, ALU.add).then_inc(var_ok, 1)

                def normalise(m, u):
                    dve.wait_ge(rstd_ok, m + 1)
                    dve.wait_ge(x_out[u], uses(m, u) * 16)
                    dve.wait_ge(xt_ps, m + 1)
                    dve.tensor_scalar(xn[:, u, :], h[:, u, :], mv[:, u, 0:1], rstd[:, u, 0:1], ALU.subtract, ALU.mult
                                      ).then_inc(xn_ok, 1)

                def logit(m, u):
                    dve.wait_ge(gate, m + 1 + FREE)
                    dve.tensor_tensor(logits[:, bass.ds(m, 1), :].rearrange("p a e -> p (a e)"), ps_g[u][:, 0:EXPERTS],
                                      gb[:, :], ALU.add).then_inc(gate_ok, 1)

                steps(dve, (normalise, 0), (add, 1), (low, 3), (logit, -1))
                dve.wait_ge(gate_ok, TILES + FREE)


def routing(nc, t, keep, logits, plan):
    E, T = EXPERTS, TILES
    PAD = 8
    with ExitStack() as ctx:
        sb = lambda n, s, d=F32: ctx.enter_context(nc.sbuf_tensor("r_" + n, s, d))
        sem = lambda n: ctx.enter_context(nc.semaphore("r_" + n))
        ps = ctx.enter_context(nc.psum_tensor("r_ps", [P, 2, 512], F32))
        bb = sb("bb", [P, E])
        tri = sb("tri", [P, E, E])
        ones_f = sb("ones_f", [P, P])
        before = sb("before", [P, P], BF16)
        ones_b = sb("ones_b", [P, P], BF16)
        marks = sb("marks", [P, T])
        slot_no = sb("slot_no", [P, SLOTS])
        number = sb("number", [P, E])
        m1 = sb("m1", [P, T])
        lc = sb("lc", [P, T, E])
        ex = sb("ex", [P, T, E])
        s1 = sb("s1", [P, T])
        r1 = sb("r1", [P, T])
        pr = sb("pr", [P, T, E])
        bp = sb("bp", [P, T, E])
        gt = sb("gt", [P, T, E * E])
        eq = sb("eq", [P, T, E * E])
        eqt = sb("eqt", [P, T, E * E])
        gts = sb("gts", [P, T, E * E])
        rank = sb("rank", [P, T, E])
        sel = sb("sel", [P, T, E])
        selb = sb("selb", [P, T, E], BF16)
        sp_ = sb("sp", [P, T, E])
        s2 = sb("s2", [P, T])
        r2 = sb("r2", [P, T])
        w = sb("w", [P, T, E])
        cum = sb("cum", [P, 5, PAD + T, E])
        cnt = sb("cnt", [P, E, T])
        nt = sb("nt", [P, E])
        ntt = sb("ntt", [P, E, E])
        base = sb("base", [P, E])
        end = sb("end", [P, E])
        base128 = sb("base128", [P, E])
        off = sb("off", [P, T, E])
        off2 = sb("off2", [P, T, E])
        pos = sb("pos", [P, T, E])
        is_k = sb("is_k", [P, TOPK, T, E])
        pos_k = sb("pos_k", [P, TOPK, T, E])
        w_k = sb("w_k", [P, TOPK, T, E])
        some = sb("some", [P, E])
        sot = sb("sot", [P, E, E])
        run_of = sb("run_of", [P, E])
        at = sb("at", [P, 3, SLOTS, E])
        at2 = sb("at2", [P, 3, SLOTS, E])
        run1 = sb("run1", [P, SLOTS])
        runp = sb("runp", [P, SLOTS])
        isf = sb("isf", [P, SLOTS])
        late = sb("late", [P, SLOTS])
        num_some = sb("num_some", [P, E])

        const_in = sem("const_in")
        pset = sem("pset")
        c = sem("c")
        exp_ok = sem("exp_ok")
        pre = sem("pre")

        with nc.allow_low_precision(reason="whole numbers, written as int32"), nc.Block() as block:
            @block.sync
            def _(sp):
                sp.dma_start(bb[:, :], t["biases"].partition_broadcast(P)).then_inc(const_in, 16)
                sp.wait_ge(const_in, 16)

            @block.gpsimd
            def _(pool):
                n = 0
                for a, val in ((tri, 1.0), (ones_f, 1.0), (cum, 0.0)):
                    pool.memset(a[:], val).then_inc(pset, 1)
                    n += 1
                pool.wait_ge(pset, n)
                pool.affine_select(out=tri[:, :, :], in_=tri[:, :, :], compare_op=ALU.is_gt, fill=0.0, base=0,
                                   pattern=[[1, E], [-1, E]], channel_multiplier=0).then_inc(pset, 1)
                pool.affine_select(out=before[:, :], in_=ones_f[:, :], compare_op=ALU.is_gt, fill=0.0, base=0,
                                   pattern=[[1, P]], channel_multiplier=-1).then_inc(pset, 1)
                pool.tensor_copy(ones_b[:, :], ones_f[:, :]).then_inc(pset, 1)
                pool.iota(marks[:, :], pattern=[[P, T]], base=0, channel_multiplier=0,
                          allow_small_or_imprecise_dtypes=True).then_inc(pset, 1)
                pool.iota(slot_no[:, :], pattern=[[1, SLOTS]], base=0, channel_multiplier=0,
                          allow_small_or_imprecise_dtypes=True).then_inc(pset, 1)
                pool.iota(number[:, :], pattern=[[1, E]], base=0, channel_multiplier=0,
                          allow_small_or_imprecise_dtypes=True).then_inc(pset, 1)
                pool.iota(plan["pair"][:, :, :, 0:1], pattern=[[0, TOPK], [P, T]], base=0, channel_multiplier=1
                          ).then_inc(pset, 1)
                pool.wait_ge(pset, n + 7)

            @block.tensor
            def _(pe):
                pe.wait_ge(pset, 10)
                pe.wait_ge(c, SEL)
                flat = selb[:, :, :].rearrange("p t e -> p (t e)")
                pe.matmul(ps[:, 0, 0:T * E], before[:, :], flat, start=True, stop=True)
                pe.matmul(ps[:, 1, 0:T * E], ones_b[:, :], flat, start=True, stop=True).then_inc(pre, 1)

            @block.scalar
            def _(act):
                act.wait_ge(c, 2)
                act.activation(ex[:, :, :], lc[:, :, :], ACT.Exp).then_inc(exp_ok, 1)

            @block.vector
            def _(dve):
                count = [0]

                def step(ins):
                    count[0] += 1
                    ins.then_inc(c, 1)
                    dve.wait_ge(c, count[0])

                def te(a):
                    return a.unsqueeze(2).broadcast_to([P, T, E])

                def over_t(a):
                    return a.unsqueeze(1).broadcast_to([P, T, E])

                TT, TS, RED = dve.tensor_tensor, dve.tensor_scalar, dve.tensor_reduce
                dve.wait_ge(const_in, 16)
                dve.wait_ge(pset, 10)
                step(RED(m1[:, :], logits[:, :, :], AXX, ALU.max))
                step(TT(lc[:, :, :], logits[:, :, :], te(m1[:, :]), ALU.subtract))
                dve.wait_ge(exp_ok, 1)
                step(RED(s1[:, :], ex[:, :, :], AXX, ALU.add))
                step(dve.reciprocal(r1[:, :], s1[:, :]))
                step(TT(pr[:, :, :], ex[:, :, :], te(r1[:, :]), ALU.mult))
                step(TT(bp[:, :, :], pr[:, :, :], over_t(bb[:, :]), ALU.add))
                pair = lambda a: a[:, :, :].rearrange("p t (e f) -> p t e f", e=E)
                mine = bp[:, :, :].unsqueeze(3).broadcast_to([P, T, E, E])
                other = bp[:, :, :].unsqueeze(2).broadcast_to([P, T, E, E])
                step(TT(pair(gt), other, mine, ALU.is_gt))
                step(TT(pair(eq), other, mine, ALU.is_equal))
                step(TT(eqt[:, :, :], eq[:, :, :], tri[:, :, :].rearrange("p e f -> p (e f)").unsqueeze(1)
                        .broadcast_to([P, T, E * E]), ALU.mult))
                step(TT(gts[:, :, :], gt[:, :, :], eqt[:, :, :], ALU.add))
                step(RED(rank[:, :, :], pair(gts), AXX, ALU.add))
                step(TS(sel[:, :, :], rank[:, :, :], TOPK - 0.5, None, ALU.is_lt))
                step(dve.tensor_copy(selb[:, :, :], sel[:, :, :]))
                assert count[0] == SEL
                step(TT(sp_[:, :, :], sel[:, :, :], pr[:, :, :], ALU.mult))
                step(RED(s2[:, :], sp_[:, :, :], AXX, ALU.add))
                step(dve.reciprocal(r2[:, :], s2[:, :]))
                step(TT(w[:, :, :], sp_[:, :, :], te(r2[:, :]), ALU.mult))
                dve.wait_ge(pre, 1)
                step(dve.tensor_copy(cum[:, 0, PAD:, :], ps[:, 1, 0:T * E].rearrange("p (t e) -> p t e", e=E)))
                for i in range(4):
                    sh = 1 << i
                    step(TT(cum[:, i + 1, PAD:, :], cum[:, i, PAD:, :], cum[:, i, PAD - sh:PAD + T - sh, :], ALU.add))
                total = cum[:, 4, PAD + T - 1, :]
                step(TT(cnt[:, :, :], total.unsqueeze(2).broadcast_to([P, E, T]),
                        marks[:, :].unsqueeze(1).broadcast_to([P, E, T]), ALU.is_gt))
                step(RED(nt[:, :], cnt[:, :, :], AXX, ALU.add))
                step(TT(ntt[:, :, :], nt[:, :].unsqueeze(1).broadcast_to([P, E, E]), tri[:, :, :], ALU.mult))
                step(RED(base[:, :], ntt[:, :, :], AXX, ALU.add))
                step(TS(base128[:, :], base[:, :], float(P), None, ALU.mult))
                step(TT(off[:, :, :], cum[:, 4, PAD:, :], cum[:, 0, PAD:, :], ALU.subtract))
                step(TT(off2[:, :, :], ps[:, 0, 0:T * E].rearrange("p (t e) -> p t e", e=E), off[:, :, :], ALU.add))
                step(TT(pos[:, :, :], off2[:, :, :], over_t(base128[:, :]), ALU.add))
                for k in range(TOPK):
                    step(TS(is_k[:, k, :, :], rank[:, :, :], float(k), None, ALU.is_equal))
                    step(TT(pos_k[:, k, :, :], is_k[:, k, :, :], pos[:, :, :], ALU.mult))
                    step(RED(plan["row"][:, k, :], pos_k[:, k, :, :], AXX, ALU.add))
                    step(TT(w_k[:, k, :, :], is_k[:, k, :, :], w[:, :, :], ALU.mult))
                    step(RED(plan["pair"][:, k, :, 1:2].bitcast(F32).rearrange("p t o -> p (t o)"),
                             w_k[:, k, :, :], AXX, ALU.add))
                step(TS(some[:, :], nt[:, :], 0.5, None, ALU.is_gt))
                step(TT(sot[:, :, :], some[:, :].unsqueeze(1).broadcast_to([P, E, E]), tri[:, :, :], ALU.mult))
                step(RED(run_of[:, :], sot[:, :, :], AXX, ALU.add))
                step(TT(num_some[:, :], number[:, :], some[:, :], ALU.mult))

                def by_slot(a):
                    return a.unsqueeze(2).broadcast_to([P, SLOTS, E])

                def by_expert(a):
                    return a.unsqueeze(1).broadcast_to([P, SLOTS, E])

                def pick(i, slot_value, expert_value, op, weight, out):
                    step(TT(at[:, i, :, :], by_slot(slot_value), by_expert(expert_value), op))
                    step(TT(at2[:, i, :, :], at[:, i, :, :], by_expert(weight), ALU.mult))
                    step(RED(out, at2[:, i, :, :], AXX, ALU.add))

                pick(0, slot_no[:, :], base[:, :], ALU.is_ge, some[:, :], run1[:, :])
                pick(1, slot_no[:, :], base[:, :], ALU.is_equal, some[:, :], isf[:, :])
                pick(2, run1[:, :], run_of[:, :], ALU.is_equal, num_some[:, :], plan["next"][:, :])
                step(TS(late[:, :], run1[:, :], 1.5, None, ALU.is_gt))
                step(TT(plan["load"][:, :], isf[:, :], late[:, :], ALU.mult))
                step(TS(plan["run"][:, :], run1[:, :], -1.0, None, ALU.add))
                step(TS(s1[:, 0:E], run_of[:, :], 0.0, None, ALU.is_equal))
                step(TT(s2[:, 0:E], s1[:, 0:E], num_some[:, :], ALU.mult))
                step(RED(plan["first"][:, :], s2[:, 0:E], AXX, ALU.add))


SEL = 13


def experts(nc, t, keep, plan, W, stage, routed):
    ident = keep["ident"]
    N = SLOTS if routed else TILES
    pre = "d_" if routed else "s_"
    MATS = 3
    with ExitStack() as ctx:
        sb = lambda n, s, d: ctx.enter_context(nc.sbuf_tensor(pre + n, s, d))
        sem = lambda n: ctx.enter_context(nc.semaphore(pre + n))
        ps = lambda n: ctx.enter_context(nc.psum_tensor(pre + n, [P, HID], F32))
        ps_g, ps_u, ps_x, ps_y, ps_h = ps("ps_g"), ps("ps_u"), ps("ps_x"), ps("ps_y"), ps("ps_h")
        x = sb("x", [P, 2, D], F32)
        xh = sb("xh", [P, 2, D], F32R)
        xl = sb("xl", [P, 2, D], F32R)
        sg = sb("sg", [P, HID], F32)
        hs = sb("hs", [P, HID], F32)
        hh = sb("hh", [P, HID], F32R)
        hl = sb("hl", [P, HID], F32R)
        y = sb("y", [P, 2, D], F32)
        pairs = sb("pairs", [P, 4, 2], I32)
        idx = sb("idx", [P, 2, TOPK], I32)
        sent_pair = sb("sent_pair", [P, 2, TOPK, 2], I32)

        landed = [sem(f"landed{c}") for c in range(MATS)]
        w_hi = sem("w_hi")
        w_lo = sem("w_lo")
        pair_in = [sem(f"pair_in{r}") for r in range(4)]
        x_in = [sem(f"x_in{u}") for u in range(2)]
        x_ps = sem("x_ps")
        xh_ok = sem("xh_ok")
        xl_ok = sem("xl_ok")
        g_ps = sem("g_ps")
        u_ps = sem("u_ps")
        sg_ok = sem("sg_ok")
        hs_ok = sem("hs_ok")
        h_ps = sem("h_ps")
        hh_ok = sem("hh_ok")
        hl_ok = sem("hl_ok")
        y_ps = sem("y_ps")
        y_ok = sem("y_ok")
        held = sem("held")
        added = sem("added")
        y_free = sem("y_free")
        idx_ok = sem("idx_ok")
        sent = [[sem(f"sent{u}{k}") for k in range(TOPK)] for u in range(2)]

        first = 2
        last = 4 if routed else 2
        assert (N - first - last) % 4 == 0

        def steps(eng, body):
            for n in range(first):
                body(n, n, N)
            with eng.Fori(0, (N - first - last) // 4) as i:
                for u in range(4):
                    body(i * 4 + (first + u), (first + u) % 4, N)
            for n in range(N - last, N):
                body(n, n % 4, N - n)

        def uses(n, r, size):
            return (n - r) // size + 1

        def wmat(l, m, part, c):
            if not routed:
                return W[:, 0, m, part, c, :]
            half = (l % 2)
            return W[:, bass.ds(half, 1), m, part, c, :].rearrange("p a n -> p (a n)")

        def wpart(half, m, part):
            return W[:, bass.ds(half, 1), m, part, :, :].rearrange("p a c n -> p (a c n)")

        def load_weights(sp, l, expert):
            for m in range(MATS):
                src = t[("w1", "wg", "w2")[m]][bass.ds(expert, 1), :, :, :] if routed else t[("ws1", "wsg", "ws2")[m]]
                src = src.rearrange("a p c n -> p (a c) n") if routed else src
                sp.dma_start(stage[:, m, :].rearrange("p (c n) -> p c n", c=DC), src).then_inc(landed[m], 16)

        def split_high(act, l):
            for m in range(MATS):
                act.wait_ge(landed[m], l * 16)
                act.activation(wpart(half_of(l), m, 0), stage[:, m, :], ACT.Copy).then_inc(w_hi, 1)

        def split_low(dve, l):
            for m in range(MATS):
                dve.wait_ge(w_hi, (l - 1) * MATS + m + 1)
                dve.tensor_tensor(wpart(half_of(l), m, 1), stage[:, m, :], wpart(half_of(l), m, 0).bitcast(F32),
                                  ALU.subtract).then_inc(w_lo, 1)

        def half_of(l):
            return (l % 2) if routed else 0

        def value(eng, tab, n, lo, hi):
            return eng.value_load(plan[tab][0:1, bass.ds(n, 1)], min_val=lo, max_val=hi)

        with nc.Block() as block:
            @block.sync
            def _(sp):
                def load_pairs(n, r):
                    sp.dma_start(pairs[:, r, :], t["table"][bass.ds(n * P, P), :]).then_inc(pair_in[r], 16)

                def load_x(n, u):
                    sp.dma_start(x[:, u, :], t["xn"][bass.ds(n * P, P), :]).then_inc(x_in[u], 16)

                if routed:
                    load_weights(sp, 1, sp.value_load(plan["first"][0:1, 0:1], min_val=0, max_val=EXPERTS - 1))
                    sp.wait_ge(w_lo, MATS)
                    load_weights(sp, 2, sp.value_load(plan["next"][0:1, 0:1], min_val=0, max_val=EXPERTS - 1))
                    for r in range(3):
                        load_pairs(r, r)
                else:
                    load_weights(sp, 1, 0)
                    load_x(0, 0)
                    load_x(1, 1)

                def body(n, r, left):
                    first_ = isinstance(n, int) and n == 0
                    if not routed:
                        if left > 2:
                            sp.wait_ge(x_ps, n + 1)
                            load_x(n + 2, r % 2)
                        return
                    if left > 3:
                        if not first_:
                            sp.wait_ge(added, n * 16)
                        load_pairs(n + 3, (r + 3) % 4)
                    if first_:
                        return
                    with sp.If(value(sp, "load", n, 0, 1) > 0):
                        run = value(sp, "run", n, 0, EXPERTS - 1) + 1
                        nxt = value(sp, "next", n, 0, EXPERTS - 1)
                        sp.wait_ge(w_lo, run * MATS)
                        load_weights(sp, run + 1, nxt)
                    sp.nop()
                steps(sp, body)

            @block.gpsimd
            def _(pool):
                def gather(n, r):
                    pool.wait_ge(pair_in[r], uses(n, r, 4) * 16)
                    pool.nop().then_inc(held, 1)
                    pool.indirect_dma_start(out=x[:, r % 2, :], out_offset=None, in_=t["xn"],
                                            in_offset=bass.IndirectOffsetOnAxis(ap=pairs[:, r, 0:1], axis=0)
                                            ).then_inc(x_in[r % 2], 16)

                def add(n, r):
                    pool.wait_ge(y_ok, n + 1)
                    if not (isinstance(n, int) and n == 0):
                        pool.wait_ge(added, n * 16)
                        pool.nop().then_inc(y_free, 1)
                    pool.nop().then_inc(held, 1)
                    if routed:
                        pool.indirect_dma_start(out=t["out"], out_offset=bass.IndirectOffsetOnAxis(ap=pairs[:, r, 0:1], axis=0),
                                                in_=y[:, r % 2, :], in_offset=None, compute_op=ALU.add).then_inc(added, 16)
                    else:
                        pool.dma_start(t["out"][bass.ds(n * P, P), :], y[:, r % 2, :], accum_op=ALU.add
                                       ).then_inc(added, 16)

                def scatter(n, u, used):
                    for k in range(TOPK):
                        if not isinstance(used, int):
                            pool.wait_ge(sent[u][k], used * 16)
                    pool.tensor_copy(idx[:, u, :], plan["row"][:, :, bass.ds(n, 1)].rearrange("p k a -> p (k a)")
                                     ).then_inc(idx_ok, 1)
                    pool.tensor_copy(sent_pair[:, u, :, 0:1], plan["pair"][:, :, bass.ds(n, 1), 0:1]
                                     .rearrange("p k a w -> p k (a w)")).then_inc(idx_ok, 1)
                    pool.tensor_copy(sent_pair[:, u, :, 1:2].bitcast(F32),
                                     plan["pair"][:, :, bass.ds(n, 1), 1:2].bitcast(F32)
                                     .rearrange("p k a w -> p k (a w)")).then_inc(idx_ok, 1)
                    pool.wait_ge(idx_ok, n * 3 + 3)
                    pool.nop().then_inc(held, 1)
                    for k in range(TOPK):
                        pool.indirect_dma_start(
                            out=t["table"], out_offset=bass.IndirectOffsetOnAxis(ap=idx[:, u, k:k + 1], axis=0),
                            in_=sent_pair[:, u, k, :], in_offset=None).then_inc(sent[u][k], 16)

                pool.nop().then_inc(y_free, 1)
                if routed:
                    gather(0, 0)
                    gather(1, 1)
                else:
                    for u in range(2):
                        scatter(u, u, 0)
                    with pool.Fori(1, TILES // 2) as i:
                        for u in range(2):
                            scatter(i * 2 + u, u, i)

                def body(n, r, left):
                    first_ = isinstance(n, int) and n == 0
                    if routed and left > 2:
                        pool.wait_ge(x_ps, n + 1)
                        gather(n + 2, (r + 2) % 4)
                    if not first_:
                        add(n - 1, (r - 1) % 4)
                steps(pool, body)
                add(N - 1, (N - 1) % 4)
                pool.wait_ge(added, N * 16)
                if not routed:
                    for u in range(2):
                        for k in range(TOPK):
                            pool.wait_ge(sent[u][k], TILES // 2 * 16)

            @block.tensor
            def _(pe):
                def turn_x(n, u):
                    pe.wait_ge(x_in[u], uses(n, u, 2) * 16)
                    if not (isinstance(n, int) and n == 0):
                        pe.wait_ge(xl_ok, n)
                    for c in range(DC):
                        mm = pe.transpose(ps_x[:, c * P:(c + 1) * P], x[:, u, c * P:(c + 1) * P], ident[:, :])
                    mm.then_inc(x_ps, 1)

                def three(out, ah, al, run, m):
                    return products(pe, out, [(a[:, c * P:(c + 1) * P], wmat(run, m, part, c))
                                              for c in range(DC) for a, part in ((ah, 0), (ah, 1), (al, 0))])

                def run_of(n):
                    return value(pe, "run", n, 0, EXPERTS - 1) + 1 if routed else 1

                def down(n, run):
                    pe.wait_ge(w_lo, run * MATS)
                    pe.wait_ge(hl_ok, n + 1)
                    if not (isinstance(n, int) and n == 0):
                        pe.wait_ge(y_ok, n)
                    three(ps_y[:, :], hh, hl, run, 2).then_inc(y_ps, 1)

                turn_x(0, 0)

                def body(n, r, left):
                    first_ = isinstance(n, int) and n == 0
                    u = r % 2
                    run = run_of(n)
                    pe.wait_ge(w_lo, (run - 1) * MATS + 1)
                    pe.wait_ge(xl_ok, n + 1)
                    if not first_:
                        pe.wait_ge(sg_ok, n)
                    three(ps_g[:, :], xh[:, u, :], xl[:, u, :], run, 0).then_inc(g_ps, 1)
                    pe.wait_ge(w_lo, (run - 1) * MATS + 2)
                    if not first_:
                        pe.wait_ge(hs_ok, n)
                    three(ps_u[:, :], xh[:, u, :], xl[:, u, :], run, 1).then_inc(u_ps, 1)
                    if left > 1:
                        turn_x(n + 1, 1 - u)
                    if not first_:
                        down(n - 1, run_of(n - 1))
                    pe.wait_ge(hs_ok, n + 1)
                    if not first_:
                        pe.wait_ge(hl_ok, n)
                    for c in range(DC):
                        mm = pe.transpose(ps_h[:, c * P:(c + 1) * P], hs[:, c * P:(c + 1) * P], ident[:, :])
                    mm.then_inc(h_ps, 1)
                steps(pe, body)
                down(N - 1, run_of(N - 1))

            @block.scalar
            def _(act):
                def x_high(n, u):
                    act.wait_ge(x_ps, n + 1)
                    act.activation(xh[:, u, :], ps_x[:, :], ACT.Copy).then_inc(xh_ok, 1)

                def out(n, r):
                    act.wait_ge(y_ps, n + 1)
                    if not (isinstance(n, int) and n == 0):
                        act.wait_ge(y_free, n)
                    scale = pairs[:, r, 1:2].bitcast(F32) if routed else 1.0
                    act.activation(y[:, r % 2, :], ps_y[:, :], ACT.Copy, scale=scale).then_inc(y_ok, 1)

                split_high(act, 1)
                if routed:
                    act.wait_ge(w_lo, MATS)
                    split_high(act, 2)
                x_high(0, 0)

                def body(n, r, left):
                    first_ = isinstance(n, int) and n == 0
                    act.wait_ge(g_ps, n + 1)
                    act.activation(sg[:, :], ps_g[:, :], ACT.Silu).then_inc(sg_ok, 1)
                    if left > 1:
                        x_high(n + 1, 1 - r % 2)
                    if not first_:
                        out(n - 1, (r - 1) % 4)
                    act.wait_ge(h_ps, n + 1)
                    act.activation(hh[:, :], ps_h[:, :], ACT.Copy).then_inc(hh_ok, 1)
                    if routed and not first_:
                        with act.If(value(act, "load", n, 0, 1) > 0):
                            split_high(act, value(act, "run", n, 0, EXPERTS - 1) + 2)
                        act.nop()
                steps(act, body)
                out(N - 1, (N - 1) % 4)

            @block.vector
            def _(dve):
                def x_low(n, u):
                    dve.wait_ge(xh_ok, n + 1)
                    dve.tensor_tensor(xl[:, u, :], ps_x[:, :], xh[:, u, :].bitcast(F32), ALU.subtract
                                      ).then_inc(xl_ok, 1)

                split_low(dve, 1)
                if routed:
                    split_low(dve, 2)
                x_low(0, 0)

                def body(n, r, left):
                    first_ = isinstance(n, int) and n == 0
                    dve.wait_ge(sg_ok, n + 1)
                    dve.wait_ge(u_ps, n + 1)
                    dve.tensor_tensor(hs[:, :], ps_u[:, :], sg[:, :], ALU.mult).then_inc(hs_ok, 1)
                    if left > 1:
                        x_low(n + 1, 1 - r % 2)
                    dve.wait_ge(hh_ok, n + 1)
                    dve.tensor_tensor(hl[:, :], ps_h[:, :], hh[:, :].bitcast(F32), ALU.subtract).then_inc(hl_ok, 1)
                    if routed and not first_:
                        with dve.If(value(dve, "load", n, 0, 1) > 0):
                            split_low(dve, value(dve, "run", n, 0, EXPERTS - 1) + 2)
                        dve.nop()
                steps(dve, body)


def setup(nc, t, keep):
    ident, identb, cs = keep["ident"], keep["identb"], keep["cs"]
    with ExitStack() as ctx:
        zeros = ctx.enter_context(nc.sbuf_tensor("zeros", [P, D], F32))
        none = ctx.enter_context(nc.sbuf_tensor("none", [P, SLOTS, 2], I32))
        none_ok = ctx.enter_context(nc.semaphore("none_ok"))
        put = ctx.enter_context(nc.semaphore("put"))
        zero = ctx.enter_context(nc.semaphore("zero"))
        cs_in = ctx.enter_context(nc.semaphore("cs_in"))
        with nc.Block() as block:
            @block.sync
            def _(sp):
                sp.dma_start(cs[:, :, :], t["cs"]).then_inc(cs_in, 16)
                sp.wait_ge(zero, 1)
                sp.dma_start(t["xn"][TOKENS:TOKENS + P, :], zeros[:, :]).then_inc(cs_in, 16)
                sp.dma_start(t["out"][TOKENS:TOKENS + P, :], zeros[:, :]).then_inc(cs_in, 16)
                sp.wait_ge(none_ok, 2)
                sp.dma_start(t["table"].rearrange("(s p) w -> p s w", p=P), none[:, :, :]).then_inc(cs_in, 16)
                sp.wait_ge(cs_in, 64)

            @block.gpsimd
            def _(pool):
                pool.memset(zeros[:, :], 0.0).then_inc(zero, 1)
                pool.wait_ge(zero, 1)
                for out in (ident, identb):
                    pool.affine_select(out=out[:, :], in_=zeros[:, 0:P], compare_op=ALU.not_equal, fill=1.0, base=0,
                                       pattern=[[-1, P]], channel_multiplier=1).then_inc(put, 1)
                pool.affine_select(out=keep["mask_q"][:, :], in_=zeros[:, 0:P], compare_op=ALU.is_ge, fill=NEG, base=0,
                                   pattern=[[-1, P]], channel_multiplier=1).then_inc(put, 1)
                pool.affine_select(out=keep["mask_k"][:, :], in_=zeros[:, 0:P], compare_op=ALU.is_ge, fill=NEG, base=0,
                                   pattern=[[1, P]], channel_multiplier=-1).then_inc(put, 1)
                pool.iota(none[:, :, 0:1], pattern=[[0, SLOTS]], base=TOKENS, channel_multiplier=1).then_inc(none_ok, 1)
                pool.memset(none[:, :, 1:2], 0).then_inc(none_ok, 1)
                pool.wait_ge(put, 4)
                pool.wait_ge(none_ok, 2)


def build(nc, t):
    t = dict(t)
    for w in ("w1", "wg", "w2"):
        t[w] = t[w].rearrange("e (c p) n -> e p c n", p=P)
    for w in ("ws1", "wsg", "ws2"):
        t[w] = t[w].rearrange("(c p) n -> p c n", p=P)
    t["h0"] = nc.dram_tensor("h0", [TOKENS, D], F32).ap()
    t["xn"] = nc.dram_tensor("xn", [TOKENS + P, D], F32).ap()
    t["table"] = nc.dram_tensor("table", [SLOTS * P, 2], I32).ap()
    with ExitStack() as ctx:
        sb = lambda n, s, d: ctx.enter_context(nc.sbuf_tensor(n, s, d))
        keep = {
            "ident": sb("ident", [P, P], F32), "identb": sb("identb", [P, P], BF16),
            "mask_q": sb("mask_q", [P, P], BF16), "mask_k": sb("mask_k", [P, P], BF16),
        }
        logits = sb("logits", [P, TILES, EXPERTS], F32)
        with ExitStack() as c2:
            sb2 = lambda n, s, d: c2.enter_context(nc.sbuf_tensor(n, s, d))
            keep["qk"] = sb2("qk", [P, 2, TILES, D], F32)
            keep["v"] = sb2("v", [P, TILES, D], F32)
            with nc.sbuf_tensor("cs", [P, 2, TILES * DK], F32) as keep["cs"]:
                setup(nc, t, keep)
                phase_a(nc, t, keep)
            phase_b(nc, t, keep)
            phase_c(nc, t, keep, logits)
        plan = {
            "row": sb("plan_row", [P, TOPK, TILES], I32), "pair": sb("plan_pair", [P, TOPK, TILES, 2], I32),
            "run": sb("plan_run", [P, SLOTS], I32), "load": sb("plan_load", [P, SLOTS], I32),
            "next": sb("plan_next", [P, SLOTS], I32), "first": sb("plan_first", [P, 1], I32),
        }
        routing(nc, t, keep, logits, plan)
        W = sb("W", [P, 2, 3, 2, DC, HID], F32R)
        stage = sb("stage", [P, 3, DC * HID], F32)
        experts(nc, t, keep, plan, W, stage, routed=False)
        experts(nc, t, keep, plan, W, stage, routed=True)


def rotations():
    import numpy as np
    theta = np.float32(1) / np.float32(10000) ** (np.arange(0, DK, 2, dtype=np.float32) / np.float32(DK))
    angle = np.arange(SEQ, dtype=np.float32)[:, None] * theta.astype(np.float32)[None, :]
    cos, sin = np.cos(angle), np.sin(angle)
    both = np.stack([np.concatenate([cos, cos], 1), np.concatenate([-sin, sin], 1)])
    both = both.reshape(2, TPB, P, DK).transpose(2, 0, 1, 3).reshape(P, 2, 1, TPB * DK)
    return np.ascontiguousarray(np.broadcast_to(both, (P, 2, BATCH, TPB * DK)).reshape(P, 2, TILES * DK), np.float32)


def kernel(x, L0_tok_emb, L0_tok_W, L0_tok_b, L0_attn_W_qkv, L0_attn_b_qkv, L0_attn_W_out, L0_attn_b_out,
           L0_ffn_W1, L0_ffn_Wg, L0_ffn_W2, L0_ffn_Ws1, L0_ffn_Wsg, L0_ffn_Ws2, L0_ffn_gate_w, L0_ffn_gate_b,
           L0_ffn_biases):
    import numpy as np
    import concourse.bacc as bacc
    from concourse.bass_utils import run_bass_kernel_spmd

    a = np.asarray
    arrays = {
        "ids": a(x).reshape(TILES, P).T,
        "emb": a(L0_tok_emb),
        "tok_w": np.concatenate([a(L0_tok_W), a(L0_tok_b)[None]], 0),
        "qkv_w": a(L0_attn_W_qkv).reshape(HEADS, 3, DK, D).transpose(3, 1, 0, 2).reshape(D, 3 * D),
        "qkv_b": a(L0_attn_b_qkv).reshape(HEADS, 3, DK).transpose(1, 0, 2).reshape(3 * D),
        "out_w": a(L0_attn_W_out).T,
        "out_b": a(L0_attn_b_out),
        "w1": a(L0_ffn_W1), "wg": a(L0_ffn_Wg), "w2": a(L0_ffn_W2),
        "ws1": a(L0_ffn_Ws1), "wsg": a(L0_ffn_Wsg), "ws2": a(L0_ffn_Ws2),
        "gate_w": a(L0_ffn_gate_w), "gate_b": a(L0_ffn_gate_b), "biases": a(L0_ffn_biases),
        "cs": rotations(),
    }
    arrays = {f"in_{k}": np.ascontiguousarray(v) for k, v in arrays.items()}
    nc = bacc.Bacc("TRN2", target_bir_lowering=False, num_devices=1)
    t = {k[3:]: nc.dram_tensor(k, v.shape, mybir.dt.from_np(v.dtype), kind="ExternalInput").ap()
         for k, v in arrays.items()}
    t["out"] = nc.dram_tensor("out", [TOKENS + P, D], F32, kind="ExternalOutput").ap()
    build(nc, t)
    r = run_bass_kernel_spmd(nc, [arrays], core_ids=[0])
    return r.results[0]["out"][:TOKENS].reshape(BATCH, SEQ, D)
```

```python
from contextlib import ExitStack

import concourse.bass as bass
from concourse import mybir

ALU = mybir.AluOpType
ACT = mybir.ActivationFunctionType
AXX = mybir.AxisListType.X
F32 = mybir.dt.float32
F32R = mybir.dt.float32r
BF16 = mybir.dt.bfloat16
I32 = mybir.dt.int32

P = 128
BATCH, SEQ = 2, 1024
TOKENS = BATCH * SEQ
TILES = TOKENS // P
TPB = SEQ // P
D = 512
DC = D // P
EMB = 75
HEADS, DK = 16, 32
HPG = P // DK
GROUPS = HEADS // HPG
UNITS = BATCH * GROUPS
KS = 3 * DK
EXPERTS, TOPK = 7, 3
HID = 512
SLOTS = TOKENS * TOPK // P + EXPERTS - 1
LN_EPS = 1e-5
SCALE = float(DK) ** -0.5
NEG = -1.0e30
HF = DK // 2
QB = 512


class Chain:

    def __init__(self, eng, sem, per_iter, base):
        self.eng, self.sem, self.per_iter, self.base, self.n = eng, sem, per_iter, base, 0

    def inc(self, ins):
        self.n += 1
        return ins.then_inc(self.sem, 1)

    def wait(self):
        self.eng.wait_ge(self.sem, self.base * self.per_iter + self.n)

    def done(self):
        assert self.n == self.per_iter, (self.n, self.per_iter)


def products(pe, out, terms, before=None):
    last = None
    for i, (l, r) in enumerate(terms):
        if before:
            before(i)
        last = pe.matmul(out, l, r, start=(i == 0), stop=(i == len(terms) - 1))
    return last


def phase_a(nc, t, keep):
    qk, v_all, ident, cs = (keep["q"], keep["k"]), keep["v"], keep["ident"], keep["cs"]
    with ExitStack() as ctx:
        sb = lambda n, s, d: ctx.enter_context(nc.sbuf_tensor("a_" + n, s, d))
        sem = lambda n: ctx.enter_context(nc.semaphore("a_" + n))
        ps = [ctx.enter_context(nc.psum_tensor(f"a_ps{i}", [P, 512], F32)) for i in range(8)]
        wh = sb("wh", [P, DC, 3 * D], F32R)
        wl = sb("wl", [P, DC, 3 * D], F32R)
        th = sb("th", [EMB + 1, D], F32R)
        tl = sb("tl", [EMB + 1, D], F32R)
        v_flat = v_all[:, :, :].rearrange("p t d -> p (t d)")
        W3 = 3 * D
        weights = [(t["tok_w"], v_flat[0:EMB + 1, DC * W3:DC * W3 + D], th[:, :], tl[:, :])]
        weights += [(t["qkv_w"][c * P:(c + 1) * P, :], v_flat[:, c * W3:(c + 1) * W3], wh[:, c, :], wl[:, c, :])
                    for c in range(DC)]
        w_in = [sem(f"w_in{i}") for i in range(len(weights))]
        w_high = sem("w_high")
        w_low = sem("w_low")
        const = setup(nc, ctx, t, keep)
        ids = sb("ids", [P, TILES], I32)
        row_ids = sb("row_ids", [P, 2, 1], I32)
        bias = sb("bias", [P, 3 * D], F32)
        rows = sb("rows", [P, 2, EMB + 1], F32)
        rth = sb("rth", [EMB + 1, P], F32R)
        rtl = sb("rtl", [EMB + 1, P], F32R)
        h = sb("h", [P, 2, D], F32)
        stats = sb("stats", [P, 6], F32)
        mv = sb("mv", [P, 2], F32)
        eps = sb("eps", [P, 1], F32)
        rstd = sb("rstd", [P, 1], F32)
        nhalf = sb("nhalf", [P, 1], F32)
        xn = sb("xn", [P, D], F32)
        xh = sb("xh", [P, 2, D], F32R)
        xl = sb("xl", [P, 2, D], F32R)
        qb = sb("qb", [P, 2, D], F32)
        ra = sb("ra", [P, 2, D], F32)
        rb = sb("rb", [P, 2, D], F32)

        held = sem("held")
        const_in = sem("const_in")
        const_set = sem("const_set")
        ids_in = sem("ids_in")
        ids_ok = sem("ids_ok")
        gathered = [sem(f"gathered{u}") for u in range(2)]
        rows_t = sem("rows_t")
        rth_ok = sem("rth_ok")
        rtl_ok = sem("rtl_ok")
        h_ps = sem("h_ps")
        h_ok = sem("h_ok")
        h_out = [sem(f"h_out{u}") for u in range(2)]
        var_ok = sem("var_ok")
        rstd_ok = sem("rstd_ok")
        xn_ok = sem("xn_ok")
        xt_ps = sem("xt_ps")
        xh_ok = sem("xh_ok")
        xl_ok = sem("xl_ok")
        proj = sem("proj")
        biased = sem("biased")
        v_ok = sem("v_ok")
        turned = sem("turned")
        roped = sem("roped")
        dch = sem("dch")
        PEEL = 4

        def steps(eng, body):
            with eng.Fori(0, (TILES - PEEL) // 2) as i:
                for u in range(2):
                    body(i * 2 + u, u, TILES)
            for n in range(TILES - PEEL, TILES):
                body(n, n % 2, TILES - n)

        def uses(n, u):
            return (n - u) // 2 + 1

        with nc.Block() as block:
            @block.sync
            def _(sp):
                sp.dma_start(ids[:, :], t["ids"]).then_inc(ids_in, 16)
                for i, (src, room, high, low) in enumerate(weights):
                    if i == 1:
                        sp.wait_ge(gathered[0], 16)
                    sp.dma_start(room, src).then_inc(w_in[i], 16)
                sp.dma_start(bias[:, :], t["qkv_b"].partition_broadcast(P)).then_inc(const_in, 16)
                const["load"](sp)
                for u in range(2):
                    sp.nop().then_inc(h_out[u], 16)

                def store(n, u, left):
                    sp.wait_ge(h_ok, n + 1)
                    sp.dma_start(t["h0"][bass.ds(n * P, P), :], h[:, u, :]).then_inc(h_out[u], 16)
                steps(sp, store)
                for u in range(2):
                    sp.wait_ge(h_out[u], 8 * TILES + 16)
                const["end"](sp)

            @block.gpsimd
            def _(pool):
                def gather(n, u):
                    pool.tensor_copy(row_ids[:, u, :], ids[:, bass.ds(n, 1)]).then_inc(ids_ok, 1)
                    pool.wait_ge(ids_ok, n + 1)
                    pool.nop().then_inc(held, 1)
                    pool.indirect_dma_start(out=rows[:, u, 0:EMB], out_offset=None, in_=t["emb"],
                                            in_offset=bass.IndirectOffsetOnAxis(ap=row_ids[:, u, :], axis=0)
                                            ).then_inc(gathered[u], 16)

                def root(n):
                    pool.wait_ge(var_ok, n + 1)
                    pool.tensor_tensor(rstd[:, :], mv[:, 1:2], nhalf[:, :], ALU.pow).then_inc(rstd_ok, 1)

                const["make"](pool)
                pool.nop().then_inc(roped, 2)
                pool.memset(rows[:, :, :], 1.0).then_inc(const_set, 1)
                pool.memset(eps[:, :], LN_EPS).then_inc(const_set, 1)
                pool.memset(nhalf[:, :], -0.5).then_inc(const_set, 1)
                pool.wait_ge(const_set, 3)
                pool.wait_ge(ids_in, 16)
                gather(0, 0)
                gather(1, 1)
                pool.wait_ge(rows_t, 1)
                gather(2, 0)
                root(0)

                def body(n, u, left):
                    if left > 3:
                        pool.wait_ge(rows_t, n + 2)
                        gather(n + 3, 1 - u)
                    if left > 1:
                        root(n + 1)
                    for j in range(2):
                        pool.wait_ge(turned, n * 4 + 2 * j + 2)
                        pool.tensor_tensor(qk[j][:, bass.ds(n, 1), :].rearrange("p a d -> p (a d)"),
                                           ra[:, j, :], rb[:, j, :], ALU.add).then_inc(roped, 1)
                steps(pool, body)
                pool.wait_ge(roped, 2 * TILES + 2)

            @block.tensor
            def _(pe):
                def turn_rows(n, u):
                    pe.wait_ge(gathered[u], uses(n, u) * 16)
                    pe.transpose(ps[0][0:EMB + 1, 0:P], rows[:, u, :], ident[:, :]).then_inc(rows_t, 1)

                def embed(n, u):
                    pe.wait_ge(rtl_ok, n + 1)
                    products(pe, ps[1][:, :], [(rth[:, :], th[:, :]), (rth[:, :], tl[:, :]), (rtl[:, :], th[:, :])]
                             ).then_inc(h_ps, 1)

                def turn_x(n):
                    pe.wait_ge(xn_ok, n + 1)
                    for c in range(DC):
                        mm = pe.transpose(ps[2][:, c * P:(c + 1) * P], xn[:, c * P:(c + 1) * P], ident[:, :])
                    mm.then_inc(xt_ps, 1)

                def project(n, u, j):
                    products(pe, ps[3 + j][:, :],
                             [(a[:, u, c * P:(c + 1) * P], w[:, c, j * D:(j + 1) * D])
                              for c in range(DC) for a, w in ((xh, wh), (xh, wl), (xl, wh))]).then_inc(proj, 1)

                pe.wait_ge(const["made"], 2)
                turn_rows(0, 0)
                pe.wait_ge(w_low, 1)
                embed(0, 0)
                turn_rows(1, 1)
                turn_x(0)
                pe.wait_ge(w_low, len(weights))

                def body(n, u, left):
                    if left > 1:
                        pe.wait_ge(h_ok, n + 1)
                        embed(n + 1, 1 - u)
                    if left > 2:
                        turn_rows(n + 2, u)
                    pe.wait_ge(xl_ok, n + 1)
                    pe.wait_ge(biased, n * 2 + 1)
                    project(n, u, 0)
                    pe.wait_ge(biased, n * 2 + 2)
                    project(n, u, 1)
                    if left > 1:
                        turn_x(n + 1)
                    pe.wait_ge(v_ok, n + 1)
                    project(n, u, 2)
                steps(pe, body)

            @block.scalar
            def _(act):
                def rows_high(n):
                    act.wait_ge(rows_t, n + 1)
                    act.activation(rth[:, :], ps[0][0:EMB + 1, 0:P], ACT.Copy).then_inc(rth_ok, 1)

                def scale_h(n, u):
                    act.wait_ge(h_ps, n + 1)
                    act.wait_ge(h_out[u], uses(n, u) * 16)
                    act.activation(h[:, u, :], ps[1][:, :], ACT.Copy, scale=float(D) ** 0.5).then_inc(h_ok, 1)

                def x_high(n, u):
                    act.wait_ge(xt_ps, n + 1)
                    act.activation(xh[:, u, :], ps[2][:, :], ACT.Copy).then_inc(xh_ok, 1)

                def weight_high(i):
                    src, room, high, low = weights[i]
                    act.wait_ge(w_in[i], 16)
                    act.activation(high, room, ACT.Copy).then_inc(w_high, 1)

                weight_high(0)
                rows_high(0)
                scale_h(0, 0)
                rows_high(1)
                for i in range(1, len(weights)):
                    weight_high(i)
                x_high(0, 0)

                def body(n, u, left):
                    if left > 1:
                        scale_h(n + 1, 1 - u)
                    if left > 2:
                        rows_high(n + 2)
                    if left > 1:
                        x_high(n + 1, 1 - u)
                steps(act, body)

            @block.vector
            def _(dve):
                def rows_low(n):
                    dve.wait_ge(rth_ok, n + 1)
                    dve.tensor_tensor(rtl[:, :], ps[0][0:EMB + 1, 0:P], rth[:, :].bitcast(F32), ALU.subtract
                                      ).then_inc(rtl_ok, 1)

                def normalise(n, u):
                    ch = Chain(dve, dch, 2, n)
                    dve.wait_ge(h_ok, n + 1)
                    ch.inc(dve.bn_stats(stats[:, :], h[:, u, :]))
                    ch.wait()
                    dve.nop().then_inc(held, 1)
                    ch.inc(dve.bn_aggr(mv[:, :], stats[:, :]))
                    ch.wait()
                    ch.done()
                    dve.tensor_scalar(mv[:, 1:2], mv[:, 1:2], eps[:, 0:1], None, ALU.add).then_inc(var_ok, 1)
                    dve.wait_ge(rstd_ok, n + 1)
                    dve.tensor_scalar(xn[:, :], h[:, u, :], mv[:, 0:1], rstd[:, 0:1], ALU.subtract, ALU.mult
                                      ).then_inc(xn_ok, 1)

                def x_low(n, u):
                    dve.wait_ge(xh_ok, n + 1)
                    dve.tensor_tensor(xl[:, u, :], ps[2][:, :], xh[:, u, :].bitcast(F32), ALU.subtract
                                      ).then_inc(xl_ok, 1)

                def rotate(n, j):
                    dve.wait_ge(proj, n * 3 + j + 1)
                    dve.tensor_tensor(qb[:, j, :], ps[3 + j][:, :], bias[:, j * D:(j + 1) * D], ALU.add
                                      ).then_inc(biased, 1)
                    dve.wait_ge(biased, n * 2 + j + 3)
                    dve.wait_ge(roped, n * 2 + j + 1)
                    src = qb[:, j, :].rearrange("p (a d) -> p a d", a=HEADS)
                    cos = cs[:, 0, bass.ds(n * DK, DK)]
                    dve.tensor_tensor(ra[:, j, :].rearrange("p (a d) -> p a d", a=HEADS), src,
                                      cos.unsqueeze(1).broadcast_to([P, HEADS, DK]), ALU.mult).then_inc(turned, 1)
                    dst = rb[:, j, :].rearrange("p (a d) -> p a d", a=HEADS)
                    for k in range(2):
                        sin = cs[:, 1, bass.ds(n * DK + k * HF, HF)]
                        ins = dve.tensor_tensor(dst[:, :, k * HF:(k + 1) * HF], src[:, :, (1 - k) * HF:(2 - k) * HF],
                                                sin.unsqueeze(1).broadcast_to([P, HEADS, HF]), ALU.mult)
                    ins.then_inc(turned, 1)

                dve.nop().then_inc(biased, 2)
                dve.nop().then_inc(v_ok, 1)
                def weight_low(i):
                    src, room, high, low = weights[i]
                    dve.wait_ge(w_high, i + 1)
                    dve.tensor_tensor(low, room, high.bitcast(F32), ALU.subtract).then_inc(w_low, 1)

                dve.wait_ge(const_set, 3)
                weight_low(0)
                rows_low(0)
                normalise(0, 0)
                rows_low(1)
                for i in range(1, len(weights)):
                    weight_low(i)
                dve.wait_ge(const_in, 16)
                dve.wait_ge(const["cs_in"], 16)
                dve.wait_ge(w_low, len(weights))
                x_low(0, 0)

                def body(n, u, left):
                    if left > 1:
                        normalise(n + 1, 1 - u)
                    if left > 2:
                        rows_low(n + 2)
                    rotate(n, 0)
                    rotate(n, 1)
                    if left > 1:
                        x_low(n + 1, 1 - u)
                    dve.wait_ge(proj, n * 3 + 3)
                    dve.tensor_tensor(v_all[:, bass.ds(n, 1), :].rearrange("p a d -> p (a d)"),
                                      ps[5][:, :], bias[:, 2 * D:3 * D], ALU.add).then_inc(v_ok, 1)
                steps(dve, body)
                dve.wait_ge(v_ok, TILES + 1)


def phase_b(nc, t, keep):
    qk, v_all, ident, identb = (keep["q"], keep["k"]), keep["v"], keep["ident"], keep["identb"]
    with ExitStack() as ctx:
        sb = lambda n, s, d: ctx.enter_context(nc.sbuf_tensor("b_" + n, s, d))
        sem = lambda n: ctx.enter_context(nc.semaphore("b_" + n))
        bank = lambda n: ctx.enter_context(nc.psum_tensor("b_" + n, [P, QB], F32))
        ST, RING = 2, 4
        sc_t = [bank(f"sc_t{i}") for i in range(ST)]
        ring = [bank(f"ring{i}") for i in range(RING)]
        acc = [bank("acc_v"), bank("acc_1")]
        q3 = sb("q3", [P, 2, HPG, KS], F32R)
        k3 = sb("k3", [P, 2, HPG, KS], F32R)
        q3t = sb("q3t", [KS + 1, BATCH, HPG, SEQ], F32R)
        k3t = sb("k3t", [KS + 1, BATCH, HPG, SEQ], F32R)
        vu = sb("vu", [P, BATCH, TPB, P], F32)
        ones = sb("ones", [P, DK], F32)
        SPB = QB // P
        mx = sb("mx", [P, HPG, TPB], F32)
        mx2 = sb("mx2", [P, 2, HPG, TPB - SPB], F32)
        mxt = sb("mxt", [HPG * TPB, P], F32R)
        e = sb("e", [P, 2 * HPG, QB], F32)
        pvs = sb("pvs", [P, QB], F32)
        sums = sb("sums", [P, QB], F32)
        rec = sb("rec", [P, QB], F32)

        set_ = sem("set")
        high = sem("high")
        low = sem("low")
        turned = sem("turned")
        t_in = sem("t_in")
        v_in = sem("v_in")
        smax = sem("smax")
        mx_ok = sem("mx_ok")
        mx_all = sem("mx_all")
        mxt_ps = sem("mxt_ps")
        mxt_ok = sem("mxt_ok")
        row_in = sem("row_in")
        st = sem("st")
        ex = sem("ex")
        pv = sem("pv")
        pv_out = sem("pv_out")
        sum_out = sem("sum_out")
        rec_ok = sem("rec_ok")
        norm = sem("norm")

        blocks = [(Q, kt) for Q in range(SEQ // QB) for kt in range((Q + 1) * SPB)]
        NB = len(blocks)
        NQ = SEQ // QB
        NH = HPG * NB
        RECS = 8
        pieces = [(qt, h, s) for qt in range(TPB) for h in range(HPG) for s in range(0, (qt + 1) * P, QB)]
        NM = len(pieces)

        def offset(i):
            Q, kt = blocks[i]
            return max(0, kt * P - Q * QB)

        def prepare():
            AHEAD = 2
            out = [(1.0, ("turn", k)) for k in range(AHEAD)]
            for qt in range(TPB):
                if qt + AHEAD < TPB:
                    out.append((1.0, ("turn", qt + AHEAD)))
                for p, (t_, h, s) in enumerate(pieces):
                    if t_ == qt:
                        out.append((0.1 + min(QB, (qt + 1) * P - s) * 1.05e-3, ("score", p)))
            return out + [(0.3, ("combine", 0)), (1.5, ("maxima", 0))]

        def attend(with_next, with_split):
            FROM, TO = 0.08, 0.93
            ready = prepare() if with_next else []
            total = sum(c for c, _ in ready)
            work = sum(QB - offset(i) for i in range(NB))
            plan, done, at, parts = [], 0.0, 0.0, []
            for i in range(NB):
                for h in range(HPG):
                    plan.append(("score_t", i * HPG + h))
                    at += (QB - offset(i)) / HPG / work
                    while ready and done + ready[0][0] <= total * (at - FROM) / (TO - FROM) + 1e-6:
                        c, s = ready.pop(0)
                        done += c
                        plan.append(s)
                    if h == 1 and i > 0:
                        plan.append(("weigh", i - 1))
                    elif h == HPG - 1 and i > 0:
                        plan.append(("sum", i - 1))
                        if blocks[i][1] == 0:
                            parts = [("norm", (blocks[i - 1][0], r)) for r in range(RECS)]
                    elif parts:
                        plan.append(parts.pop(0))
            assert not ready
            if with_split:
                plan += [("split", 0)]
            plan += parts + [("weigh", NB - 1), ("sum", NB - 1)] + [("norm", (NQ - 1, r)) for r in range(RECS)]
            return plan

        users = []
        for _, (kind, what) in prepare():
            if kind == "combine":
                continue
            users += [("turn", 2 * what), ("turn", 2 * what + 1)] if kind == "turn" else [(kind, what)]

        def ring_bank(user):
            return ring[users.index(user) % RING]

        def units(eng, begin, step):
            def unit(now, after, later):
                if begin and after:
                    begin(*after)
                for kind, what in attend(after is not None, later is not None):
                    step(kind, what, *(later if kind == "split" else
                                       now if kind in ("score_t", "weigh", "sum", "norm") else after))

            if begin:
                begin(0, 0, 0)
            step("split", 0, 0, 0, 0)
            for _, (kind, what) in prepare():
                step(kind, what, 0, 0, 0)
            step("split", 0, 1, 1, 0)
            with eng.Fori(0, GROUPS - 1) as g:
                unit((g * 2, 0, g), (g * 2 + 1, 1, g), (g * 2 + 2, 0, g + 1))
                unit((g * 2 + 1, 1, g), (g * 2 + 2, 0, g + 1), (g * 2 + 3, 1, g + 1))
            g = GROUPS - 1
            unit((g * 2, 0, g), (g * 2 + 1, 1, g), None)
            unit((g * 2 + 1, 1, g), None, None)

        def chunk(j, b, g, k):
            a = qk[j][:, b * TPB + k, bass.ds(g * P, P)]
            return a.rearrange("p (h d) -> p h d", h=HPG)

        assert BATCH == 2

        with nc.Block() as block:
            @block.sync
            def _(sp):
                def step(kind, what, n, b, g):
                    if kind == "maxima":
                        sp.wait_ge(mxt_ok, n + 2)
                        sp.dma_start(q3t[KS:KS + 1, b, :, :].rearrange("o h (k q) -> o (h k) q", q=P).bitcast(F32),
                                     mxt[:, :].bitcast(F32)).then_inc(row_in, 16)
                sp.dma_start(keep["out_w"][:, :, :], t["out_w"].rearrange("(c p) n -> p c n", p=P)
                             ).then_inc(keep["out_w_in"], 16)
                units(sp, None, step)
                sp.wait_ge(row_in, 16 * UNITS)
                sp.wait_ge(keep["out_w_in"], 16)

            @block.gpsimd
            def _(pool):
                pool.memset(ones[:, :], 1.0).then_inc(set_, 1)
                pool.wait_ge(set_, 1)
                pool.nop().then_inc(norm, 1)

                def values(n, b, g):
                    if not (isinstance(n, int) and n == 0):
                        pool.wait_ge(pv, n * NB)
                    pool.tensor_copy(vu[:, b, :, :], v_all[:, b * TPB:(b + 1) * TPB, bass.ds(g * P, P)]).then_inc(v_in, 1)

                def step(kind, what, n, b, g):
                    if kind == "norm" and what[1] == RECS - 1:
                        Q = what[0]
                        pool.wait_ge(rec_ok, (n * NQ + Q + 2) * RECS)
                        pool.wait_ge(pv_out, n * NQ + Q + 2)
                        pool.tensor_tensor(qk[0][:, b * TPB + Q * SPB:b * TPB + (Q + 1) * SPB, bass.ds(g * P, P)],
                                           pvs[:, :].rearrange("p (a q) -> p a q", q=P),
                                           rec[:, :].rearrange("p (a q) -> p a q", q=P), ALU.mult).then_inc(norm, 1)
                    elif kind == "split" and what == 0 and isinstance(n, int) and n == 0:
                        pool.wait_ge(v_in, 1)
                        pool.memset(k3t[KS:KS + 1, :, :, :].bitcast(F32), 1.0).then_inc(set_, 1)
                        pool.wait_ge(set_, 2)
                units(pool, values, step)
                pool.wait_ge(norm, UNITS * NQ + 1)

            @block.tensor
            def _(pe):
                pe.nop().then_inc(turned, 4)
                pe.nop().then_inc(pv, NB)

                def free(n, user):
                    at = users.index(user)
                    own = at >= RING
                    kind, i = users[at - RING] if own else users[(len(users) - 1 - at) // RING * RING + at]
                    done_, per = {"turn": (t_in, 2 * TPB), "score": (mx_ok, NM), "maxima": (mxt_ok, 1)}[kind]
                    pe.wait_ge(done_, n * per + per * own + i + 1)

                def turn(n, b, k):
                    for j, src in enumerate((q3, k3)):
                        user = ("turn", 2 * k + j)
                        pe.wait_ge(low, n * 2 * TPB + 2 * k + j + 1)
                        free(n, user)
                        for h in range(HPG):
                            mm = pe.transpose(ring_bank(user)[0:KS, h * P:(h + 1) * P],
                                              src[:, k % 2, h, :].bitcast(F32), ident[:, :])
                        mm.then_inc(turned, 1)

                def score(n, b, p):
                    qt, h, s = pieces[p]
                    out = ring_bank(("score", p))
                    if h == 0 and s == 0:
                        pe.wait_ge(t_in, n * 2 * TPB + 2 * TPB + 2 * qt + 2)
                    free(n, ("score", p))
                    w = min(QB, (qt + 1) * P - s)
                    diag = s + w == (qt + 1) * P
                    mm = pe.matmul(out[:, 0:w], q3t[0:KS, b, h, qt * P:(qt + 1) * P], k3t[0:KS, b, h, s:s + w],
                                   start=True, stop=not diag)
                    if diag:
                        mm = pe.matmul(out[:, w - P:w], identb[:, :], keep["mask_q"][:, :], start=False, stop=True)
                    mm.then_inc(smax, 1)

                def maxima(n, b):
                    pe.wait_ge(mx_all, n + 1)
                    free(n, ("maxima", 0))
                    pe.transpose(ring_bank(("maxima", 0))[0:HPG * TPB, 0:P], mx[:, :, :].rearrange("p h k -> p (h k)"),
                                 ident[:, :]).then_inc(mxt_ps, 1)

                def score_t(n, b, j):
                    i, h = divmod(j, HPG)
                    (Q, kt), off = blocks[i], offset(i)
                    if j == 0:
                        pe.wait_ge(set_, 2)
                        pe.wait_ge(row_in, n * 16 + 16)
                    pe.wait_ge(ex, n * NH + j + 1)
                    diag = kt * P >= Q * QB
                    mm = pe.matmul(sc_t[j % ST][:, 0:QB - off], k3t[:, b, h, kt * P:(kt + 1) * P],
                                   q3t[:, b, h, Q * QB + off:(Q + 1) * QB], start=True, stop=not diag)
                    if diag:
                        mm = pe.matmul(sc_t[j % ST][:, 0:P], identb[:, :], keep["mask_k"][:, :], start=False, stop=True)
                    mm.then_inc(st, 1)

                def weigh(n, b, i, which):
                    (Q, kt), off = blocks[i], offset(i)
                    if which == 0:
                        if i == 0:
                            pe.wait_ge(v_in, n + 1)
                        pe.wait_ge(ex, n * NH + (i + 1) * HPG + ST)
                    if kt == 0:
                        pe.wait_ge((pv_out, sum_out)[which], n * NQ + Q + 1)
                    ends = kt == (Q + 1) * SPB - 1
                    for h in range(HPG):
                        lhs = vu[:, b, kt, h * DK:(h + 1) * DK] if which == 0 else ones[:, :]
                        mm = pe.matmul(acc[which][h * DK:(h + 1) * DK, off:QB], lhs,
                                       e[:, (HPG * i + h) % (2 * HPG), 0:QB - off], start=(kt == 0), stop=ends)
                    if which == 1:
                        mm.then_inc(pv, 1)

                def step(kind, what, n, b, g):
                    if kind == "turn":
                        turn(n, b, what)
                    elif kind == "score":
                        score(n, b, what)
                    elif kind == "maxima":
                        maxima(n, b)
                    elif kind == "score_t":
                        score_t(n, b, what)
                    elif kind in ("weigh", "sum"):
                        weigh(n, b, what, int(kind == "sum"))
                units(pe, None, step)

            @block.scalar
            def _(act):
                act.nop().then_inc(t_in, 2 * TPB)
                act.nop().then_inc(ex, ST)
                act.nop().then_inc(mxt_ok, 1)
                act.nop().then_inc(pv_out, 1)

                def highs(n, b, g, k):
                    act.wait_ge(turned, n * 2 * TPB + 2 * k + 2)
                    for j, (dst, at) in enumerate(((q3, slice(0, 2 * DK)), (k3, slice(0, KS)))):
                        out = dst[:, k % 2, :, at].rearrange("p h (r d) -> p h r d", d=DK)
                        out = out if j == 0 else out[:, :, 0:3:2, :]
                        act.activation(out, chunk(j, b, g, k).unsqueeze(2).broadcast_to([P, HPG, 2, DK]), ACT.Copy
                                       ).then_inc(high, 1)

                def step(kind, what, n, b, g):
                    if kind == "turn":
                        k = what
                        for j, dst in enumerate((q3t, k3t)):
                            act.wait_ge(turned, n * 2 * TPB + 2 * k + j + 1 + 4)
                            act.activation(dst[0:KS, b, :, k * P:(k + 1) * P], ring_bank(("turn", 2 * k + j))[0:KS, :]
                                           .rearrange("p (h q) -> p h q", h=HPG), ACT.Copy).then_inc(t_in, 1)
                        if k + 2 < TPB:
                            highs(n, b, g, k + 2)
                    elif kind == "split":
                        highs(n, b, g, 0)
                        highs(n, b, g, 1)
                    elif kind == "maxima":
                        act.wait_ge(mxt_ps, n + 1)
                        act.activation(mxt[:, :], ring_bank(("maxima", 0))[0:HPG * TPB, 0:P], ACT.Copy, scale=-1.0).then_inc(mxt_ok, 1)
                    elif kind == "score_t":
                        j = what
                        w = QB - offset(j // HPG)
                        act.wait_ge(st, n * NH + j + 1)
                        if j % HPG == 0:
                            act.wait_ge(pv, n * NB + NB + j // HPG - 1)
                        act.activation(e[:, j % (2 * HPG), 0:w], sc_t[j % ST][:, 0:w], ACT.Exp, scale=SCALE
                                       ).then_inc(ex, 1)
                    elif kind == "sum" and (what == NB - 1 or blocks[what + 1][1] == 0):
                        Q = blocks[what][0]
                        act.wait_ge(pv, n * NB + NB + what + 1)
                        act.wait_ge(norm, n * NQ + Q + 1)
                        act.activation(pvs[:, :], acc[0][:, :], ACT.Copy).then_inc(pv_out, 1)
                units(act, None, step)

            @block.vector
            def _(dve):
                dve.nop().then_inc(mx_ok, NM)
                dve.nop().then_inc(sum_out, 1)
                dve.nop().then_inc(rec_ok, RECS)

                def lows(n, b, g, k):
                    for j, (dst, hi, lo) in enumerate(((q3, 0, 2), (k3, 0, 1))):
                        dve.wait_ge(high, n * 2 * TPB + 2 * k + j + 1)
                        dve.tensor_tensor(dst[:, k % 2, :, lo * DK:(lo + 1) * DK], chunk(j, b, g, k),
                                          dst[:, k % 2, :, hi * DK:(hi + 1) * DK].bitcast(F32), ALU.subtract
                                          ).then_inc(low, 1)

                def step(kind, what, n, b, g):
                    if kind == "turn" and what + 2 < TPB:
                        lows(n, b, g, what + 2)
                    elif kind == "split":
                        lows(n, b, g, 0)
                        lows(n, b, g, 1)
                    elif kind == "score":
                        qt, h, s = pieces[what]
                        dve.wait_ge(smax, n * NM + what + 1)
                        if what == 0 and not (isinstance(n, int) and n == 0):
                            dve.wait_ge(mxt_ps, n)
                        w = min(QB, (qt + 1) * P - s)
                        out = mx[:, h, qt:qt + 1] if qt < SPB else mx2[:, s // QB, h, qt - SPB:qt - SPB + 1]
                        dve.tensor_reduce(out, ring_bank(("score", what))[:, 0:w], AXX, ALU.max).then_inc(mx_ok, 1)
                    elif kind == "combine":
                        dve.wait_ge(mx_ok, n * NM + 2 * NM)
                        dve.tensor_tensor(mx[:, :, SPB:], mx2[:, 0, :, :], mx2[:, 1, :, :], ALU.max).then_inc(mx_all, 1)
                    elif kind == "sum" and (what == NB - 1 or blocks[what + 1][1] == 0):
                        Q = blocks[what][0]
                        dve.wait_ge(pv, n * NB + NB + what + 1)
                        dve.wait_ge(rec_ok, (n * NQ + Q + 1) * RECS)
                        dve.tensor_copy(sums[:, :], acc[1][:, :]).then_inc(sum_out, 1)
                    elif kind == "norm":
                        Q, r = what
                        w = QB // RECS
                        if r == 0:
                            dve.wait_ge(sum_out, n * NQ + Q + 2)
                            dve.wait_ge(norm, n * NQ + Q + 1)
                        dve.reciprocal(rec[:, r * w:(r + 1) * w], sums[:, r * w:(r + 1) * w]).then_inc(rec_ok, 1)
                units(dve, None, step)


MATS = 3


class Weights:

    def __init__(self, nc, ctx, t):
        self.t = t
        self.W = ctx.enter_context(nc.sbuf_tensor("W", [P, 2, MATS, 2, DC, HID], F32R))
        self.stage = ctx.enter_context(nc.sbuf_tensor("stage", [P, MATS, DC * HID], F32))
        self.landed = [ctx.enter_context(nc.semaphore(f"w_landed{m}")) for m in range(MATS)]
        self.w_hi = ctx.enter_context(nc.semaphore("w_hi"))
        self.w_lo = ctx.enter_context(nc.semaphore("w_lo"))

    def part(self, l, m, part):
        return self.W[:, bass.ds(l % 2, 1), m, part, :, :].rearrange("p a c n -> p (a c n)")

    def chunk(self, l, m, part, c):
        return self.W[:, bass.ds(l % 2, 1), m, part, c, :].rearrange("p a n -> p (a n)")

    def load(self, sp, l, expert=None):
        if not (isinstance(l, int) and l == 0):
            sp.wait_ge(self.w_lo, l * MATS)
        for m in range(MATS):
            src = self.t[("ws1", "wsg", "ws2")[m]] if expert is None else \
                self.t[("w1", "wg", "w2")[m]][bass.ds(expert, 1), :, :, :].rearrange("a p c n -> p (a c) n")
            sp.dma_start(self.stage[:, m, :].rearrange("p (c n) -> p c n", c=DC), src).then_inc(self.landed[m], 16)

    def split_high(self, act, l, m):
        act.wait_ge(self.landed[m], l * 16 + 16)
        act.activation(self.part(l, m, 0), self.stage[:, m, :], ACT.Copy).then_inc(self.w_hi, 1)

    def split_low(self, dve, l, m):
        dve.wait_ge(self.w_hi, l * MATS + m + 1)
        dve.tensor_tensor(self.part(l, m, 1), self.stage[:, m, :], self.part(l, m, 0).bitcast(F32),
                          ALU.subtract).then_inc(self.w_lo, 1)

    def wait(self, pe, l, m):
        pe.wait_ge(self.w_lo, l * MATS + m + 1)


def phase_c(nc, t, keep, logits, weights):
    heads, ident = keep["q"], keep["ident"]
    with ExitStack() as ctx:
        sb = lambda n, s, d: ctx.enter_context(nc.sbuf_tensor("c_" + n, s, d))
        sem = lambda n: ctx.enter_context(nc.semaphore("c_" + n))
        pair = lambda n: [ctx.enter_context(nc.psum_tensor(f"c_{n}{u}", [P, D], F32)) for u in range(2)]
        ps_o, ps_x, ps_g = pair("ps_o"), pair("ps_x"), pair("ps_g")
        wh = sb("wh", [P, DC, D], F32R)
        wl = sb("wl", [P, DC, D], F32R)
        gw = sb("gw", [P, DC, EXPERTS], F32)
        gb = sb("gb", [P, EXPERTS], F32)
        ob = sb("ob", [P, D], F32)
        hin = sb("hin", [P, 2, D], F32)
        hb = sb("hb", [P, 2, D], F32)
        ah = sb("ah", [P, 2, D], F32R)
        al = sb("al", [P, 2, D], F32R)
        h = sb("h", [P, 2, D], F32)
        xn = sb("xn", [P, 2, D], F32)
        xt = keep["out_w"][:, 0:2, :]
        stats = sb("stats", [P, 2, 6], F32)
        mv = sb("mv", [P, 2, 2], F32)
        rstd = sb("rstd", [P, 2, 1], F32)
        nhalf = sb("nhalf", [P, 1], F32)

        FREE = 2
        FIRST_SPLIT = 10
        held = sem("held")
        const_in = sem("const_in")
        const_set = sem("const_set")
        h_in = [sem(f"h_in{u}") for u in range(2)]
        wh_ok = sem("wh_ok")
        wl_ok = sem("wl_ok")
        hb_ok = sem("hb_ok")
        ah_ok = sem("ah_ok")
        al_ok = sem("al_ok")
        proj = sem("proj")
        h_ok = sem("h_ok")
        h_out = [sem(f"h_out{u}") for u in range(2)]
        x_out = [sem(f"x_out{u}") for u in range(2)]
        stat_ok = sem("stat_ok")
        aggr_ok = sem("aggr_ok")
        var_ok = sem("var_ok")
        rstd_ok = sem("rstd_ok")
        xn_ok = sem("xn_ok")
        xt_ps = sem("xt_ps")
        xt_ok = sem("xt_ok")
        gate = sem("gate")
        gate_ok = sem("gate_ok")

        def steps(eng, *stages):
            FIRST, LOOP, END = -4, 1, TILES + 1
            count = (TILES - 6 - LOOP) // 2

            def one(n):
                for f, lead in stages:
                    if 0 <= n + lead < TILES:
                        f(n + lead, (n + lead) % 2)
            for n in range(FIRST, LOOP):
                one(n)
            with eng.Fori(0, count) as i:
                for u in range(2):
                    for f, lead in stages:
                        f(i * 2 + (LOOP + u + lead), (LOOP + u + lead) % 2)
            for n in range(LOOP + 2 * count, END):
                one(n)

        def uses(m, u):
            return (m - u) // 2 + 1

        with nc.Block() as block:
            @block.sync
            def _(sp):
                sp.dma_start(gw[:, :, :], t["gate_w"].rearrange("(c p) e -> p c e", p=P)).then_inc(const_in, 16)
                sp.dma_start(gb[:, :], t["gate_b"].partition_broadcast(P)).then_inc(const_in, 16)
                sp.dma_start(ob[:, :], t["out_b"].partition_broadcast(P)).then_inc(const_in, 16)
                for u in range(2):
                    sp.nop().then_inc(h_out[u], 16)
                    sp.nop().then_inc(x_out[u], 16)

                def load(m, u):
                    if not isinstance(m, int) or m >= 2:
                        sp.wait_ge(hb_ok, m - 1)
                    sp.dma_start(hin[:, u, :], t["h0"][bass.ds(m * P, P), :]).then_inc(h_in[u], 16)
                    if isinstance(m, int) and m == 1:
                        weights.load(sp, 0)

                def store_h(m, u):
                    sp.wait_ge(h_ok, m + 1 + FREE)
                    sp.dma_start(t["out"][bass.ds(m * P, P), :], h[:, u, :]).then_inc(h_out[u], 16)

                def store_x(m, u):
                    sp.wait_ge(xn_ok, m + 1 + FREE)
                    sp.dma_start(t["xn"][bass.ds(m * P, P), :], xn[:, u, :]).then_inc(x_out[u], 16)

                steps(sp, (load, 4), (store_h, 1), (store_x, 0))
                for u in range(2):
                    sp.wait_ge(h_out[u], 8 * TILES + 16)
                    sp.wait_ge(x_out[u], 8 * TILES + 16)

            @block.gpsimd
            def _(pool):
                pool.memset(nhalf[:, :], -0.5).then_inc(const_set, 1)
                pool.wait_ge(const_set, 1)
                pool.wait_ge(const_in, 48)

                def bias(m, u):
                    pool.wait_ge(h_in[u], uses(m, u) * 16)
                    pool.wait_ge(h_ok, m + 1)
                    pool.tensor_tensor(hb[:, u, :], hin[:, u, :], ob[:, :], ALU.add).then_inc(hb_ok, 1)

                def root(m, u):
                    pool.wait_ge(var_ok, m + 1)
                    pool.tensor_tensor(rstd[:, u, :], mv[:, u, 1:2], nhalf[:, :], ALU.pow).then_inc(rstd_ok, 1)

                steps(pool, (bias, 2), (root, 1))

            @block.tensor
            def _(pe):
                for s in (proj, xt_ps, gate):
                    pe.nop().then_inc(s, FREE)

                def weights_in(i):
                    if i % 3 == 0:
                        pe.wait_ge(wl_ok, i // 3 + 1)

                def project(m, u):
                    pe.wait_ge(al_ok, m + 1)
                    pe.wait_ge(h_ok, m + 1)
                    products(pe, ps_o[u][:, :], [(a[:, u, c * P:(c + 1) * P], w[:, c, :])
                                                 for c in range(DC) for a, w in ((ah, wh), (ah, wl), (al, wh))],
                             weights_in if isinstance(m, int) and m == 0 else None).then_inc(proj, 1)

                def turn(m, u):
                    pe.wait_ge(xn_ok, m + 1 + FREE)
                    pe.wait_ge(xt_ok, m + 1)
                    for c in range(DC):
                        mm = pe.transpose(ps_x[u][:, c * P:(c + 1) * P], xn[:, u, c * P:(c + 1) * P], ident[:, :])
                    mm.then_inc(xt_ps, 1)

                def weigh(m, u):
                    pe.wait_ge(const_in, 48)
                    pe.wait_ge(xt_ok, m + 1 + FREE)
                    pe.wait_ge(gate_ok, m + 1)
                    products(pe, ps_g[u][:, 0:EXPERTS], [(xt[:, u, c * P:(c + 1) * P], gw[:, c, :]) for c in range(DC)]
                             ).then_inc(gate, 1)

                steps(pe, (project, 2), (weigh, -1), (turn, 0))

            @block.scalar
            def _(act):
                act.nop().then_inc(xt_ok, FREE)

                def high(m, u):
                    act.wait_ge(proj, m + 1)
                    act.activation(ah[:, u, :], heads[:, bass.ds(m, 1), :].rearrange("p a d -> p (a d)"), ACT.Copy
                                   ).then_inc(ah_ok, 1)
                    if isinstance(m, int) and m == 0:
                        act.wait_ge(keep["out_w_in"], 16)
                        for c in range(DC):
                            act.activation(wh[:, c, :], keep["out_w"][:, c, :], ACT.Copy).then_inc(wh_ok, 1)

                def out(m, u):
                    act.wait_ge(xt_ps, m + 1 + FREE)
                    act.wait_ge(gate, m + 1)
                    act.activation(xt[:, u, :], ps_x[u][:, :], ACT.Copy).then_inc(xt_ok, 1)

                def split(m, u):
                    if isinstance(m, int) and 0 <= m - FIRST_SPLIT < MATS:
                        weights.split_high(act, 0, m - FIRST_SPLIT)

                steps(act, (high, 3), (out, 0), (split, 0))

            @block.vector
            def _(dve):
                for s in (h_ok, xn_ok, gate_ok):
                    dve.nop().then_inc(s, FREE)
                def low(m, u):
                    dve.wait_ge(ah_ok, m + 1)
                    dve.tensor_tensor(al[:, u, :], heads[:, bass.ds(m, 1), :].rearrange("p a d -> p (a d)"),
                                      ah[:, u, :].bitcast(F32), ALU.subtract).then_inc(al_ok, 1)
                    if isinstance(m, int) and m == 0:
                        for c in range(DC):
                            dve.wait_ge(wh_ok, c + 1)
                            dve.tensor_tensor(wl[:, c, :], keep["out_w"][:, c, :], wh[:, c, :].bitcast(F32),
                                              ALU.subtract).then_inc(wl_ok, 1)

                def add(m, u):
                    dve.wait_ge(proj, m + 1 + FREE)
                    dve.wait_ge(hb_ok, m + 1)
                    dve.wait_ge(h_out[u], uses(m, u) * 16)
                    dve.wait_ge(xn_ok, m + 1)
                    dve.tensor_tensor(h[:, u, :], ps_o[u][:, :], hb[:, u, :], ALU.add).then_inc(h_ok, 1)
                    dve.wait_ge(h_ok, m + 1 + FREE)
                    dve.bn_stats(stats[:, u, :], h[:, u, :]).then_inc(stat_ok, 1)
                    dve.wait_ge(stat_ok, m + 1)
                    dve.nop().then_inc(held, 1)
                    dve.bn_aggr(mv[:, u, :], stats[:, u, :]).then_inc(aggr_ok, 1)
                    dve.wait_ge(aggr_ok, m + 1)
                    dve.tensor_scalar(mv[:, u, 1:2], mv[:, u, 1:2], LN_EPS, None, ALU.add).then_inc(var_ok, 1)

                def normalise(m, u):
                    dve.wait_ge(rstd_ok, m + 1)
                    dve.wait_ge(x_out[u], uses(m, u) * 16)
                    dve.wait_ge(xt_ps, m + 1)
                    dve.tensor_scalar(xn[:, u, :], h[:, u, :], mv[:, u, 0:1], rstd[:, u, 0:1], ALU.subtract, ALU.mult
                                      ).then_inc(xn_ok, 1)

                def logit(m, u):
                    dve.wait_ge(const_in, 48)
                    dve.wait_ge(gate, m + 1 + FREE)
                    dve.tensor_tensor(logits[:, bass.ds(m, 1), :].rearrange("p a e -> p (a e)"), ps_g[u][:, 0:EXPERTS],
                                      gb[:, :], ALU.add).then_inc(gate_ok, 1)

                def split(m, u):
                    if isinstance(m, int) and 0 <= m - FIRST_SPLIT < MATS:
                        weights.split_low(dve, 0, m - FIRST_SPLIT)

                steps(dve, (low, 3), (normalise, 0), (add, 1), (logit, -1), (split, 0))
                dve.wait_ge(gate_ok, TILES + FREE)


def routing(nc, ctx, t, logits, plan):
    E, T = EXPERTS, TILES
    PAD = 8
    sb = lambda n, s, d=F32: ctx.enter_context(nc.sbuf_tensor("r_" + n, s, d))
    sem = lambda n: ctx.enter_context(nc.semaphore("r_" + n))
    ps = ctx.enter_context(nc.psum_tensor("r_ps", [P, 2, 512], F32))
    bb = sb("bb", [P, E])
    tri = sb("tri", [P, E, E])
    ones_f = sb("ones_f", [P, P])
    before = sb("before", [P, P], BF16)
    ones_b = sb("ones_b", [P, P], BF16)
    marks = sb("marks", [P, T])
    slot_no = sb("slot_no", [P, SLOTS])
    number = sb("number", [P, E])
    m1 = sb("m1", [P, T])
    lc = sb("lc", [P, T, E])
    ex = sb("ex", [P, T, E])
    s1 = sb("s1", [P, T])
    r1 = sb("r1", [P, T])
    pr = sb("pr", [P, T, E])
    bp = sb("bp", [P, T, E])
    gt = sb("gt", [P, T, E * E])
    eq = sb("eq", [P, T, E * E])
    eqt = sb("eqt", [P, T, E * E])
    gts = sb("gts", [P, T, E * E])
    rank = sb("rank", [P, T, E])
    sel = sb("sel", [P, T, E])
    selb = sb("selb", [P, T, E], BF16)
    sp_ = sb("sp", [P, T, E])
    s2 = sb("s2", [P, T])
    r2 = sb("r2", [P, T])
    w = sb("w", [P, T, E])
    cum = sb("cum", [P, 5, PAD + T, E])
    cnt = sb("cnt", [P, E, T])
    nt = sb("nt", [P, E])
    ntt = sb("ntt", [P, E, E])
    base = sb("base", [P, E])
    base128 = sb("base128", [P, E])
    off = sb("off", [P, T, E])
    off2 = sb("off2", [P, T, E])
    pos = sb("pos", [P, T, E])
    is_k = sb("is_k", [P, TOPK, T, E])
    pos_k = sb("pos_k", [P, TOPK, T, E])
    w_k = sb("w_k", [P, TOPK, T, E])
    some = sb("some", [P, E])
    sot = sb("sot", [P, E, E])
    run_of = sb("run_of", [P, E])
    at = sb("at", [P, SLOTS, E])
    at2 = sb("at2", [P, SLOTS, E])
    run1 = sb("run1", [P, SLOTS])
    isf = sb("isf", [P, SLOTS])
    later = sb("later", [P, SLOTS])
    num_some = sb("num_some", [P, E])

    const_in = sem("const_in")
    pset = sem("pset")
    c = sem("c")
    exp_ok = sem("exp_ok")
    pre = sem("pre")

    count = [0]

    def step(dve, ins):
        count[0] += 1
        ins.then_inc(c, 1)
        dve.wait_ge(c, count[0])

    def te(a):
        return a.unsqueeze(2).broadcast_to([P, T, E])

    def over_t(a):
        return a.unsqueeze(1).broadcast_to([P, T, E])

    def load(sp):
        sp.dma_start(bb[:, :], t["biases"].partition_broadcast(P)).then_inc(const_in, 16)

    def constants(pool):
        n = 0
        for a, val in ((tri, 1.0), (ones_f, 1.0), (cum, 0.0)):
            pool.memset(a[:], val).then_inc(pset, 1)
            n += 1
        pool.wait_ge(pset, n)
        pool.affine_select(out=tri[:, :, :], in_=tri[:, :, :], compare_op=ALU.is_gt, fill=0.0, base=0,
                           pattern=[[1, E], [-1, E]], channel_multiplier=0).then_inc(pset, 1)
        pool.affine_select(out=before[:, :], in_=ones_f[:, :], compare_op=ALU.is_gt, fill=0.0, base=0,
                           pattern=[[1, P]], channel_multiplier=-1).then_inc(pset, 1)
        pool.tensor_copy(ones_b[:, :], ones_f[:, :]).then_inc(pset, 1)
        pool.iota(marks[:, :], pattern=[[P, T]], base=0, channel_multiplier=0,
                  allow_small_or_imprecise_dtypes=True).then_inc(pset, 1)
        pool.iota(slot_no[:, :], pattern=[[1, SLOTS]], base=0, channel_multiplier=0,
                  allow_small_or_imprecise_dtypes=True).then_inc(pset, 1)
        pool.iota(number[:, :], pattern=[[1, E]], base=0, channel_multiplier=0,
                  allow_small_or_imprecise_dtypes=True).then_inc(pset, 1)
        pool.iota(plan["pair"][:, :, :, 0:1], pattern=[[0, TOPK], [P, T]], base=0, channel_multiplier=1
                  ).then_inc(pset, 1)
        pool.wait_ge(pset, n + 7)

    def exponentials(act):
        act.wait_ge(c, 2)
        act.activation(ex[:, :, :], lc[:, :, :], ACT.Exp).then_inc(exp_ok, 1)

    def prefixes(pe):
        pe.wait_ge(pset, 10)
        pe.wait_ge(c, SELECTED)
        flat = selb[:, :, :].rearrange("p t e -> p (t e)")
        pe.matmul(ps[:, 0, 0:T * E], before[:, :], flat, start=True, stop=True)
        pe.matmul(ps[:, 1, 0:T * E], ones_b[:, :], flat, start=True, stop=True).then_inc(pre, 1)

    def select(dve):
        TT, TS, RED = dve.tensor_tensor, dve.tensor_scalar, dve.tensor_reduce
        dve.wait_ge(const_in, 16)
        dve.wait_ge(pset, 10)
        step(dve, RED(m1[:, :], logits[:, :, :], AXX, ALU.max))
        step(dve, TT(lc[:, :, :], logits[:, :, :], te(m1[:, :]), ALU.subtract))
        dve.wait_ge(exp_ok, 1)
        step(dve, RED(s1[:, :], ex[:, :, :], AXX, ALU.add))
        step(dve, dve.reciprocal(r1[:, :], s1[:, :]))
        step(dve, TT(pr[:, :, :], ex[:, :, :], te(r1[:, :]), ALU.mult))
        step(dve, TT(bp[:, :, :], pr[:, :, :], over_t(bb[:, :]), ALU.add))
        pair = lambda a: a[:, :, :].rearrange("p t (e f) -> p t e f", e=E)
        mine = bp[:, :, :].unsqueeze(3).broadcast_to([P, T, E, E])
        other = bp[:, :, :].unsqueeze(2).broadcast_to([P, T, E, E])
        step(dve, TT(pair(gt), other, mine, ALU.is_gt))
        step(dve, TT(pair(eq), other, mine, ALU.is_equal))
        step(dve, TT(eqt[:, :, :], eq[:, :, :], tri[:, :, :].rearrange("p e f -> p (e f)").unsqueeze(1)
                .broadcast_to([P, T, E * E]), ALU.mult))
        step(dve, TT(gts[:, :, :], gt[:, :, :], eqt[:, :, :], ALU.add))
        step(dve, RED(rank[:, :, :], pair(gts), AXX, ALU.add))
        step(dve, TS(sel[:, :, :], rank[:, :, :], TOPK - 0.5, None, ALU.is_lt))
        step(dve, dve.tensor_copy(selb[:, :, :], sel[:, :, :]))
        assert count[0] == SELECTED

    def rows(dve):
        TT, TS, RED = dve.tensor_tensor, dve.tensor_scalar, dve.tensor_reduce
        step(dve, TT(sp_[:, :, :], sel[:, :, :], pr[:, :, :], ALU.mult))
        step(dve, RED(s2[:, :], sp_[:, :, :], AXX, ALU.add))
        step(dve, dve.reciprocal(r2[:, :], s2[:, :]))
        step(dve, TT(w[:, :, :], sp_[:, :, :], te(r2[:, :]), ALU.mult))
        dve.wait_ge(pre, 1)
        step(dve, dve.tensor_copy(cum[:, 0, PAD:, :], ps[:, 1, 0:T * E].rearrange("p (t e) -> p t e", e=E)))
        for i in range(4):
            sh = 1 << i
            step(dve, TT(cum[:, i + 1, PAD:, :], cum[:, i, PAD:, :], cum[:, i, PAD - sh:PAD + T - sh, :], ALU.add))
        total = cum[:, 4, PAD + T - 1, :]
        step(dve, TT(cnt[:, :, :], total.unsqueeze(2).broadcast_to([P, E, T]),
                marks[:, :].unsqueeze(1).broadcast_to([P, E, T]), ALU.is_gt))
        step(dve, RED(nt[:, :], cnt[:, :, :], AXX, ALU.add))
        step(dve, TT(ntt[:, :, :], nt[:, :].unsqueeze(1).broadcast_to([P, E, E]), tri[:, :, :], ALU.mult))
        step(dve, RED(base[:, :], ntt[:, :, :], AXX, ALU.add))
        step(dve, TS(base128[:, :], base[:, :], float(P), None, ALU.mult))
        step(dve, TT(off[:, :, :], cum[:, 4, PAD:, :], cum[:, 0, PAD:, :], ALU.subtract))
        step(dve, TT(off2[:, :, :], ps[:, 0, 0:T * E].rearrange("p (t e) -> p t e", e=E), off[:, :, :], ALU.add))
        step(dve, TT(pos[:, :, :], off2[:, :, :], over_t(base128[:, :]), ALU.add))

    def place(dve):
        TT, TS, RED = dve.tensor_tensor, dve.tensor_scalar, dve.tensor_reduce
        for k in range(TOPK):
            step(dve, TS(is_k[:, k, :, :], rank[:, :, :], float(k), None, ALU.is_equal))
            step(dve, TT(pos_k[:, k, :, :], is_k[:, k, :, :], pos[:, :, :], ALU.mult))
            step(dve, RED(plan["row"][:, k, :], pos_k[:, k, :, :], AXX, ALU.add))
            step(dve, TT(w_k[:, k, :, :], is_k[:, k, :, :], w[:, :, :], ALU.mult))
            step(dve, RED(plan["pair"][:, k, :, 1:2].bitcast(F32).rearrange("p t o -> p (t o)"),
                     w_k[:, k, :, :], AXX, ALU.add))
        assert count[0] == PLACED

    def by_slot(a):
        return a.unsqueeze(2).broadcast_to([P, SLOTS, E])

    def by_expert(a):
        return a.unsqueeze(1).broadcast_to([P, SLOTS, E])

    def pick(dve, slot_value, expert_value, op, weight, out):
        step(dve, dve.tensor_tensor(at[:, :, :], by_slot(slot_value), by_expert(expert_value), op))
        step(dve, dve.tensor_tensor(at2[:, :, :], at[:, :, :], by_expert(weight), ALU.mult))
        step(dve, dve.tensor_reduce(out, at2[:, :, :], AXX, ALU.add))

    def runs(dve):
        TT, TS, RED = dve.tensor_tensor, dve.tensor_scalar, dve.tensor_reduce
        step(dve, TS(some[:, :], nt[:, :], 0.5, None, ALU.is_gt))
        step(dve, TT(sot[:, :, :], some[:, :].unsqueeze(1).broadcast_to([P, E, E]), tri[:, :, :], ALU.mult))
        step(dve, RED(run_of[:, :], sot[:, :, :], AXX, ALU.add))
        step(dve, TT(num_some[:, :], number[:, :], some[:, :], ALU.mult))
        pick(dve, slot_no[:, :], base[:, :], ALU.is_ge, some[:, :], run1[:, :])
        pick(dve, slot_no[:, :], base[:, :], ALU.is_equal, some[:, :], isf[:, :])

    def loads(dve):
        TT, TS, RED = dve.tensor_tensor, dve.tensor_scalar, dve.tensor_reduce
        step(dve, TS(later[:, :], run1[:, :], 1.0, None, ALU.add))
        pick(dve, later[:, :], run_of[:, :], ALU.is_equal, num_some[:, :], plan["next"][:, :])
        step(dve, dve.tensor_copy(plan["load"][:, :], isf[:, :]))
        step(dve, TS(plan["run"][:, :], run1[:, :], -1.0, None, ALU.add))
        for r in range(2):
            step(dve, TS(s1[:, 0:E], run_of[:, :], float(r), None, ALU.is_equal))
            step(dve, TT(s2[:, 0:E], s1[:, 0:E], num_some[:, :], ALU.mult))
            step(dve, RED(plan["first"][:, r:r + 1], s2[:, 0:E], AXX, ALU.add))
        assert count[0] == ROUTED

    return {"load": load, "constants": constants, "exponentials": exponentials, "prefixes": prefixes,
            "dve": (select, rows, place, runs, loads), "steps": c, "constants_ok": pset}


SELECTED, PLACED, ROUTED = 13, 45, 67


class Step:

    def __init__(self, n, at, r, routed):
        self.n, self.at, self.r, self.u, self.routed = n, at, r % 4, r % 2, routed
        self.known = isinstance(n, int)
        self.first = self.known and n == 0

    @staticmethod
    def of(n):
        return Step(n, n - TILES if n >= TILES else n, n, n >= TILES)

    def near(self, k):
        if self.known:
            return Step.of(self.n + k) if self.n + k < TILES + SLOTS else None
        return Step(self.n + k, self.at + k, self.r + k, self.routed)

    def uses(self, size):
        return (self.at - self.r % size) // size + 1


def experts(nc, t, keep, logits, plan, weights):
    ident = keep["ident"]
    N = TILES + SLOTS
    assert TILES % 4 == 0 and D == HID
    with ExitStack() as ctx:
        sb = lambda n, s, d: ctx.enter_context(nc.sbuf_tensor("e_" + n, s, d))
        sem = lambda n: ctx.enter_context(nc.semaphore("e_" + n))
        ps = lambda n: ctx.enter_context(nc.psum_tensor("e_" + n, [P, HID], F32))
        ps_g, ps_u, ps_x, ps_y, ps_h = ps("ps_g"), ps("ps_u"), ps("ps_x"), ps("ps_y"), ps("ps_h")
        x, y, sg, hs = keep["q"][:, 0:2, :], keep["q"][:, 2:4, :], keep["q"][:, 4, :], keep["q"][:, 5, :]
        xh = sb("xh", [P, 2, D], F32R)
        xl = sb("xl", [P, 2, D], F32R)
        hh = sb("hh", [P, HID], F32R)
        hl = sb("hl", [P, HID], F32R)
        pairs = sb("pairs", [P, 4, 2], I32)
        idx = sb("idx", [P, 2, TOPK], I32)
        sent_pair = sb("sent_pair", [P, 2, TOPK, 2], I32)

        pair_in = [sem(f"pair_in{r}") for r in range(4)]
        x_in = [sem(f"x_in{u}") for u in range(2)]
        xg_in = [sem(f"xg_in{u}") for u in range(2)]
        x_ps = sem("x_ps")
        xh_ok = sem("xh_ok")
        xl_ok = sem("xl_ok")
        g_ps = sem("g_ps")
        u_ps = sem("u_ps")
        sg_ok = sem("sg_ok")
        hs_ok = sem("hs_ok")
        h_ps = sem("h_ps")
        hh_ok = sem("hh_ok")
        hl_ok = sem("hl_ok")
        y_ps = sem("y_ps")
        y_ok = sem("y_ok")
        held = sem("held")
        added = sem("added")
        y_free = sem("y_free")
        idx_ok = sem("idx_ok")
        sent = [[sem(f"sent{u}{k}") for k in range(TOPK)] for u in range(2)]

        route = routing(nc, ctx, t, logits, plan)
        RUNS_KNOWN = 5
        SEND = 4
        split_at = {TILES - 4: (0, 1), TILES - 3: (2,)}

        def steps(eng, body):
            for start, end, first, last, unroll in ((0, TILES, 6, 4, 2), (TILES, N, 2, 4, 4)):
                count, rest = divmod(end - start - first - last, unroll)
                assert rest == 0
                for n in range(start, start + first):
                    body(Step.of(n))
                with eng.Fori(0, count) as i:
                    for u in range(unroll):
                        body(Step(i * unroll + (start + first + u), i * unroll + (first + u), first + u, start > 0))
                for n in range(end - last, end):
                    body(Step.of(n))

        def value(eng, tab, slot, lo, hi):
            return eng.value_load(plan[tab][0:1, bass.ds(slot, 1)], min_val=lo, max_val=hi)

        def run_of(eng, a):
            return value(eng, "run", a.at, 0, EXPERTS - 1)

        with nc.allow_low_precision(reason="whole numbers, written as int32"), nc.Block() as block:
            @block.sync
            def _(sp):
                def load_pairs(a):
                    sp.dma_start(pairs[:, a.r, :], t["table"][bass.ds(a.at * P, P), :]).then_inc(pair_in[a.r], 16)

                def load_x(a):
                    sp.dma_start(x[:, a.u, :], t["xn"][bass.ds(a.at * P, P), :]).then_inc(x_in[a.u], 16)

                def load_first(r):
                    weights.load(sp, r + 1, sp.value_load(plan["first"][0:1, r:r + 1], min_val=0, max_val=EXPERTS - 1))

                load_x(Step.of(0))
                load_x(Step.of(1))
                route["load"](sp)

                def body(a):
                    rows, pair = a.near(2), a.near(3)
                    if rows and not rows.routed:
                        sp.wait_ge(x_ps, a.n + 1)
                        load_x(rows)
                    if pair and pair.routed:
                        if pair.known and pair.at == 0:
                            for u in range(2):
                                for k in range(TOPK):
                                    sp.wait_ge(sent[u][k], TILES // 2 * 16)
                        if not a.first and a.near(-1).routed:
                            sp.wait_ge(added, a.n * 16)
                        load_pairs(pair)
                    if a.known and a.n == RUNS_KNOWN:
                        sp.wait_ge(route["steps"], ROUTED)
                        load_first(0)
                    if a.known and a.n == TILES - 3:
                        load_first(1)
                    if a.routed and a.known and a.at == 0:
                        weights.load(sp, 3, value(sp, "next", 0, 0, EXPERTS - 1))
                    elif a.routed:
                        with sp.If(value(sp, "load", a.at, 0, 1) > 0):
                            weights.load(sp, run_of(sp, a) + 3, value(sp, "next", a.at, 0, EXPERTS - 1))
                        sp.nop()
                steps(sp, body)
                runs = run_of(sp, Step.of(N - 1))
                for m in range(MATS):
                    sp.wait_ge(weights.landed[m], runs * 16 + 64)
                    sp.nop().then_inc(held, 1)

            @block.gpsimd
            def _(pool):
                def gather(a):
                    pool.wait_ge(pair_in[a.r], a.uses(4) * 16)
                    pool.nop().then_inc(held, 1)
                    pool.indirect_dma_start(out=x[:, a.u, :], out_offset=None, in_=t["xn"],
                                            in_offset=bass.IndirectOffsetOnAxis(ap=pairs[:, a.r, 0:1], axis=0)
                                            ).then_inc(xg_in[a.u], 16)

                def add(a):
                    pool.wait_ge(y_ok, a.n + 1)
                    if not a.first:
                        pool.wait_ge(added, a.n * 16)
                        pool.nop().then_inc(y_free, 1)
                    pool.nop().then_inc(held, 1)
                    if a.routed:
                        pool.indirect_dma_start(out=t["out"],
                                                out_offset=bass.IndirectOffsetOnAxis(ap=pairs[:, a.r, 0:1], axis=0),
                                                in_=y[:, a.u, :], in_offset=None, compute_op=ALU.add
                                                ).then_inc(added, 16)
                    else:
                        pool.dma_start(t["out"][bass.ds(a.at * P, P), :], y[:, a.u, :], accum_op=ALU.add
                                       ).then_inc(added, 16)

                def send(tile, u):
                    for k in range(TOPK):
                        if not isinstance(tile, int) or tile >= 2:
                            pool.wait_ge(sent[u][k], (tile - u) // 2 * 16)
                    pool.tensor_copy(idx[:, u, :], plan["row"][:, :, bass.ds(tile, 1)].rearrange("p k a -> p (k a)")
                                     ).then_inc(idx_ok, 1)
                    pool.tensor_copy(sent_pair[:, u, :, 0:1], plan["pair"][:, :, bass.ds(tile, 1), 0:1]
                                     .rearrange("p k a w -> p k (a w)")).then_inc(idx_ok, 1)
                    pool.tensor_copy(sent_pair[:, u, :, 1:2].bitcast(F32),
                                     plan["pair"][:, :, bass.ds(tile, 1), 1:2].bitcast(F32)
                                     .rearrange("p k a w -> p k (a w)")).then_inc(idx_ok, 1)
                    pool.wait_ge(idx_ok, tile * 3 + 3)
                    pool.nop().then_inc(held, 1)
                    for k in range(TOPK):
                        pool.indirect_dma_start(
                            out=t["table"], out_offset=bass.IndirectOffsetOnAxis(ap=idx[:, u, k:k + 1], axis=0),
                            in_=sent_pair[:, u, k, :], in_offset=None).then_inc(sent[u][k], 16)

                pool.nop().then_inc(y_free, 1)
                route["constants"](pool)

                def body(a):
                    rows = a.near(2)
                    if rows and rows.routed:
                        pool.wait_ge(x_ps, a.n + 1)
                        gather(rows)
                    if not a.first:
                        add(a.near(-1))
                    if a.known and a.n == SEND:
                        pool.wait_ge(route["steps"], PLACED)
                    if not a.routed and (not a.known or SEND <= a.n < SEND + TILES // 2):
                        for u in range(2):
                            send(a.at * 2 + (u - 2 * SEND), u)
                steps(pool, body)
                add(Step.of(N - 1))
                pool.wait_ge(added, N * 16)

            @block.tensor
            def _(pe):
                def turn_x(a):
                    pe.wait_ge((xg_in if a.routed else x_in)[a.u], a.uses(2) * 16)
                    if not a.first:
                        pe.wait_ge(xl_ok, a.n)
                    for c in range(DC):
                        mm = pe.transpose(ps_x[:, c * P:(c + 1) * P], x[:, a.u, c * P:(c + 1) * P], ident[:, :])
                    mm.then_inc(x_ps, 1)

                def three(out, ah, al, l, m):
                    return products(pe, out, [(a[:, c * P:(c + 1) * P], weights.chunk(l, m, part, c))
                                              for c in range(DC) for a, part in ((ah, 0), (ah, 1), (al, 0))])

                def load_of(a):
                    return run_of(pe, a) + 1 if a.routed else 0

                def down(a):
                    l = load_of(a)
                    weights.wait(pe, l, 2)
                    pe.wait_ge(hl_ok, a.n + 1)
                    if not a.first:
                        pe.wait_ge(y_ok, a.n)
                    three(ps_y[:, :], hh, hl, l, 2).then_inc(y_ps, 1)

                turn_x(Step.of(0))

                def body(a):
                    l = load_of(a)
                    weights.wait(pe, l, 0)
                    pe.wait_ge(xl_ok, a.n + 1)
                    if not a.first:
                        pe.wait_ge(sg_ok, a.n)
                    three(ps_g[:, :], xh[:, a.u, :], xl[:, a.u, :], l, 0).then_inc(g_ps, 1)
                    weights.wait(pe, l, 1)
                    if not a.first:
                        pe.wait_ge(hs_ok, a.n)
                    three(ps_u[:, :], xh[:, a.u, :], xl[:, a.u, :], l, 1).then_inc(u_ps, 1)
                    if a.near(1):
                        turn_x(a.near(1))
                    if not a.first:
                        down(a.near(-1))
                    pe.wait_ge(hs_ok, a.n + 1)
                    if not a.first:
                        pe.wait_ge(hl_ok, a.n)
                    for c in range(DC):
                        mm = pe.transpose(ps_h[:, c * P:(c + 1) * P], hs[:, c * P:(c + 1) * P], ident[:, :])
                    mm.then_inc(h_ps, 1)
                    if a.known and a.n == 2:
                        route["prefixes"](pe)
                steps(pe, body)
                down(Step.of(N - 1))

            @block.scalar
            def _(act):
                def x_high(a):
                    act.wait_ge(x_ps, a.n + 1)
                    act.activation(xh[:, a.u, :], ps_x[:, :], ACT.Copy).then_inc(xh_ok, 1)

                def out(a):
                    act.wait_ge(y_ps, a.n + 1)
                    if not a.first:
                        act.wait_ge(y_free, a.n)
                    scale = pairs[:, a.r, 1:2].bitcast(F32) if a.routed else 1.0
                    act.activation(y[:, a.u, :], ps_y[:, :], ACT.Copy, scale=scale).then_inc(y_ok, 1)

                def split(a, mats):
                    if a.routed and a.known and a.at == 0:
                        for m in mats:
                            weights.split_high(act, 2, m)
                    elif a.routed:
                        with act.If(value(act, "load", a.at, 0, 1) > 0):
                            for m in mats:
                                weights.split_high(act, run_of(act, a) + 2, m)
                        act.nop()

                x_high(Step.of(0))

                def body(a):
                    act.wait_ge(g_ps, a.n + 1)
                    act.activation(sg[:, :], ps_g[:, :], ACT.Silu).then_inc(sg_ok, 1)
                    if a.near(1):
                        x_high(a.near(1))
                    if not a.first:
                        out(a.near(-1))
                    split(a, (0,))
                    act.wait_ge(h_ps, a.n + 1)
                    act.activation(hh[:, :], ps_h[:, :], ACT.Copy).then_inc(hh_ok, 1)
                    if a.known and a.n == 1:
                        route["exponentials"](act)
                    for m in split_at.get(a.n, ()) if a.known else ():
                        weights.split_high(act, 1, m)
                    split(a, (1, 2))
                steps(act, body)
                out(Step.of(N - 1))

            @block.vector
            def _(dve):
                def x_low(a):
                    dve.wait_ge(xh_ok, a.n + 1)
                    dve.tensor_tensor(xl[:, a.u, :], ps_x[:, :], xh[:, a.u, :].bitcast(F32), ALU.subtract
                                      ).then_inc(xl_ok, 1)

                def split(a, mats):
                    if a.routed and a.known and a.at == 0:
                        for m in mats:
                            weights.split_low(dve, 2, m)
                    elif a.routed:
                        with dve.If(value(dve, "load", a.at, 0, 1) > 0):
                            for m in mats:
                                weights.split_low(dve, run_of(dve, a) + 2, m)
                        dve.nop()

                x_low(Step.of(0))

                def body(a):
                    dve.wait_ge(sg_ok, a.n + 1)
                    dve.wait_ge(u_ps, a.n + 1)
                    dve.tensor_tensor(hs[:, :], ps_u[:, :], sg[:, :], ALU.mult).then_inc(hs_ok, 1)
                    if a.near(1):
                        x_low(a.near(1))
                    split(a, (0,))
                    dve.wait_ge(hh_ok, a.n + 1)
                    dve.tensor_tensor(hl[:, :], ps_h[:, :], hh[:, :].bitcast(F32), ALU.subtract).then_inc(hl_ok, 1)
                    if a.known and 1 <= a.n <= len(route["dve"]):
                        route["dve"][a.n - 1](dve)
                    for m in split_at.get(a.n, ()) if a.known else ():
                        weights.split_low(dve, 1, m)
                    split(a, (1, 2))
                steps(dve, body)


def setup(nc, ctx, t, keep):
    ident, identb, cs = keep["ident"], keep["identb"], keep["cs"]
    zeros = ctx.enter_context(nc.sbuf_tensor("zeros", [P, D], F32))
    none = ctx.enter_context(nc.sbuf_tensor("none", [P, SLOTS, 2], I32))
    none_ok = ctx.enter_context(nc.semaphore("none_ok"))
    made = ctx.enter_context(nc.semaphore("made"))
    zero = ctx.enter_context(nc.semaphore("zero"))
    cs_in = ctx.enter_context(nc.semaphore("cs_in"))
    cleared = ctx.enter_context(nc.semaphore("cleared"))

    def load(sp):
        sp.dma_start(cs[:, :, :], t["cs"]).then_inc(cs_in, 16)
        sp.wait_ge(zero, 1)
        sp.dma_start(t["xn"][TOKENS:TOKENS + P, :], zeros[:, :]).then_inc(cleared, 16)
        sp.dma_start(t["out"][TOKENS:TOKENS + P, :], zeros[:, :]).then_inc(cleared, 16)
        sp.wait_ge(none_ok, 2)
        sp.dma_start(t["table"].rearrange("(s p) w -> p s w", p=P), none[:, :, :]).then_inc(cleared, 16)

    def end(sp):
        sp.wait_ge(cs_in, 16)
        sp.wait_ge(cleared, 48)

    def make(pool):
        pool.memset(zeros[:, :], 0.0).then_inc(zero, 1)
        pool.wait_ge(zero, 1)
        for out in (ident, identb):
            pool.affine_select(out=out[:, :], in_=zeros[:, 0:P], compare_op=ALU.not_equal, fill=1.0, base=0,
                               pattern=[[-1, P]], channel_multiplier=1).then_inc(made, 1)
        pool.affine_select(out=keep["mask_q"][:, :], in_=zeros[:, 0:P], compare_op=ALU.is_ge, fill=NEG, base=0,
                           pattern=[[-1, P]], channel_multiplier=1).then_inc(made, 1)
        pool.affine_select(out=keep["mask_k"][:, :], in_=zeros[:, 0:P], compare_op=ALU.is_ge, fill=NEG, base=0,
                           pattern=[[1, P]], channel_multiplier=-1).then_inc(made, 1)
        pool.iota(none[:, :, 0:1], pattern=[[0, SLOTS]], base=TOKENS, channel_multiplier=1).then_inc(none_ok, 1)
        pool.memset(none[:, :, 1:2], 0).then_inc(none_ok, 1)
        pool.wait_ge(made, 4)
        pool.wait_ge(none_ok, 2)

    return {"load": load, "end": end, "make": make, "made": made, "cs_in": cs_in}


def build(nc, t):
    t = dict(t)
    for w in ("w1", "wg", "w2"):
        t[w] = t[w].rearrange("e (c p) n -> e p c n", p=P)
    for w in ("ws1", "wsg", "ws2"):
        t[w] = t[w].rearrange("(c p) n -> p c n", p=P)
    t["h0"] = nc.dram_tensor("h0", [TOKENS, D], F32).ap()
    t["xn"] = nc.dram_tensor("xn", [TOKENS + P, D], F32).ap()
    t["table"] = nc.dram_tensor("table", [SLOTS * P, 2], I32).ap()
    with ExitStack() as ctx:
        sb = lambda n, s, d: ctx.enter_context(nc.sbuf_tensor(n, s, d))
        keep = {
            "ident": sb("ident", [P, P], F32), "identb": sb("identb", [P, P], BF16),
            "mask_q": sb("mask_q", [P, P], BF16), "mask_k": sb("mask_k", [P, P], BF16),
        }
        logits = sb("logits", [P, TILES, EXPERTS], F32)
        plan = {
            "row": sb("plan_row", [P, TOPK, TILES], I32), "pair": sb("plan_pair", [P, TOPK, TILES, 2], I32),
            "run": sb("plan_run", [P, SLOTS], I32), "load": sb("plan_load", [P, SLOTS], I32),
            "next": sb("plan_next", [P, SLOTS], I32), "first": sb("plan_first", [P, 2], I32),
        }
        keep["q"] = sb("q", [P, TILES, D], F32)
        keep["out_w"] = sb("out_w", [P, DC, D], F32)
        keep["out_w_in"] = ctx.enter_context(nc.semaphore("out_w_in"))
        with ExitStack() as c2:
            sb2 = lambda n, s, d: c2.enter_context(nc.sbuf_tensor(n, s, d))
            keep["k"] = sb2("k", [P, TILES, D], F32)
            keep["v"] = sb2("v", [P, TILES, D], F32)
            with nc.sbuf_tensor("cs", [P, 2, TILES * DK], F32) as keep["cs"]:
                phase_a(nc, t, keep)
            phase_b(nc, t, keep)
        weights = Weights(nc, ctx, t)
        phase_c(nc, t, keep, logits, weights)
        experts(nc, t, keep, logits, plan, weights)


def rotations():
    import numpy as np
    theta = np.float32(1) / np.float32(10000) ** (np.arange(0, DK, 2, dtype=np.float32) / np.float32(DK))
    angle = np.arange(SEQ, dtype=np.float32)[:, None] * theta.astype(np.float32)[None, :]
    cos, sin = np.cos(angle), np.sin(angle)
    both = np.stack([np.concatenate([cos, cos], 1), np.concatenate([-sin, sin], 1)])
    both = both.reshape(2, TPB, P, DK).transpose(2, 0, 1, 3).reshape(P, 2, 1, TPB * DK)
    return np.ascontiguousarray(np.broadcast_to(both, (P, 2, BATCH, TPB * DK)).reshape(P, 2, TILES * DK), np.float32)


def kernel(x, L0_tok_emb, L0_tok_W, L0_tok_b, L0_attn_W_qkv, L0_attn_b_qkv, L0_attn_W_out, L0_attn_b_out,
           L0_ffn_W1, L0_ffn_Wg, L0_ffn_W2, L0_ffn_Ws1, L0_ffn_Wsg, L0_ffn_Ws2, L0_ffn_gate_w, L0_ffn_gate_b,
           L0_ffn_biases):
    import numpy as np
    import concourse.bacc as bacc
    from concourse.bass_utils import run_bass_kernel_spmd

    a = np.asarray
    arrays = {
        "ids": a(x).reshape(TILES, P).T,
        "emb": a(L0_tok_emb),
        "tok_w": np.concatenate([a(L0_tok_W), a(L0_tok_b)[None]], 0),
        "qkv_w": a(L0_attn_W_qkv).reshape(HEADS, 3, DK, D).transpose(3, 1, 0, 2).reshape(D, 3 * D),
        "qkv_b": a(L0_attn_b_qkv).reshape(HEADS, 3, DK).transpose(1, 0, 2).reshape(3 * D),
        "out_w": a(L0_attn_W_out).T,
        "out_b": a(L0_attn_b_out),
        "w1": a(L0_ffn_W1), "wg": a(L0_ffn_Wg), "w2": a(L0_ffn_W2),
        "ws1": a(L0_ffn_Ws1), "wsg": a(L0_ffn_Wsg), "ws2": a(L0_ffn_Ws2),
        "gate_w": a(L0_ffn_gate_w), "gate_b": a(L0_ffn_gate_b), "biases": a(L0_ffn_biases),
        "cs": rotations(),
    }
    arrays = {f"in_{k}": np.ascontiguousarray(v) for k, v in arrays.items()}
    nc = bacc.Bacc("TRN2", target_bir_lowering=False, num_devices=1)
    t = {k[3:]: nc.dram_tensor(k, v.shape, mybir.dt.from_np(v.dtype), kind="ExternalInput").ap()
         for k, v in arrays.items()}
    t["out"] = nc.dram_tensor("out", [TOKENS + P, D], F32, kind="ExternalOutput").ap()
    build(nc, t)
    r = run_bass_kernel_spmd(nc, [arrays], core_ids=[0])
    return r.results[0]["out"][:TOKENS].reshape(BATCH, SEQ, D)
```
